# Optimizing a Trainium2 kernel written in Bass

```python
import numpy as np
import jax
import jax.numpy as jnp

def _softmax(x, axis=-1):
    return jax.nn.softmax(x, axis=axis)

def _gelu(x):
    return jax.nn.gelu(x, approximate=True)

def _silu(x):
    return jax.nn.silu(x)

def _sigmoid(x):
    return jax.nn.sigmoid(x)

def _layernorm(x, axis=-1, eps=1e-05):
    m = jnp.mean(x, axis=axis, keepdims=True)
    v = jnp.var(x, axis=axis, keepdims=True)
    return (x - m) / jnp.sqrt(v + eps)

def _scatter_add(tgt, idx, src, axis=0):
    return tgt.at[idx].add(src)

def _segment_sum(src, seg, n):
    return jax.ops.segment_sum(src, seg, n)
kernel_name = 'mk_adj_preln_d4_adj_r2_9108d5'

def setup_inputs(seed: int=0):
    np.random.seed(seed)
    _w = jnp.asarray

    def _rec_inputs():
        import jax
        import jax.numpy as jnp
        _gk = jax.random.key(seed)
        x = -0.0005207 + 1.001 * jax.random.normal(jax.random.fold_in(_gk, 1), (4096, 128), jnp.float32)
        _a = jax.random.bernoulli(jax.random.fold_in(_gk, 2), 0.00195312, (4096, 4096))
        _a = jnp.logical_or(_a, jnp.eye(4096, dtype=bool))
        _af = _a.astype(jnp.float32)
        adj = _af
        return (x, adj)
    x, adj = _rec_inputs()

    def _L0_gnn_setup():
        import jax, jax.numpy as jnp
        import numpy as np
        N = 4096
        F = 128
        NEG_INF = -9000000000000000.0
        ALPHA = 0.2
        THRESH = 1e-06
        key = jax.random.key(seed)
        k1, k2, k3, k4 = jax.random.split(key, 4)
        x = jax.random.normal(k1, (N, F), jnp.float32)
        h0 = jax.random.normal(k2, (N, F), jnp.float32)
        limit = float(np.sqrt(6.0 / (2 * F + 1)) * 1.414)
        a = jax.random.uniform(k3, (2 * F, 1), jnp.float32, -limit, limit)
        temp = jnp.zeros((5,), jnp.float32)
        adj = jax.random.bernoulli(k4, 0.005, (N, N)).astype(jnp.float32)
        adj = jnp.maximum(adj, jnp.eye(N, dtype=jnp.float32))
        return {'x': x, 'h0': h0, 'a': a, 'temp': temp, 'adj': adj, 'l': 1}
    _L0_gnn_all = _L0_gnn_setup()
    _L0_gnn_in = {k: v for k, v in _L0_gnn_all.items() if k in ('h0', 'a', 'temp')}
    del _L0_gnn_all

    def _L1_gnn_setup():
        import jax, jax.numpy as jnp
        import numpy as np
        N = 3072
        HID = 128
        T = 350
        DENSITY = 0.05
        key = jax.random.key(seed)
        k1, k2, k3, k4, k5, k6 = jax.random.split(key, 6)
        h = jax.random.normal(k1, (N, HID), dtype=jnp.float32)
        a = jax.random.uniform(k2, (N, N), dtype=jnp.float32)
        mask = jax.random.uniform(k3, (N, N)) < DENSITY
        adj = jnp.where(mask, a, 0.0)
        simlar = jax.random.normal(k4, (N, N), dtype=jnp.float32)
        s = 1.0 / np.sqrt(HID)
        W_proj = jax.random.uniform(k5, (HID, HID), minval=-s, maxval=s, dtype=jnp.float32)
        b_proj = jnp.zeros((HID,), dtype=jnp.float32)
        W_gcn = jax.random.uniform(k6, (HID, HID), minval=-s, maxval=s, dtype=jnp.float32)
        b_gcn = jnp.zeros((HID,), dtype=jnp.float32)
        return {'h': h, 'adj': adj, 'simlar': simlar, 'W_proj': W_proj, 'b_proj': b_proj, 'W_gcn': W_gcn, 'b_gcn': b_gcn}
    _L1_gnn_all = _L1_gnn_setup()
    _L1_gnn_in = {k: v for k, v in _L1_gnn_all.items() if k in ('W_proj', 'b_proj', 'W_gcn', 'b_gcn')}
    del _L1_gnn_all

    def _L2_gnn_setup():
        import jax, jax.numpy as jnp
        import numpy as np
        N = 4096
        D = 128
        L = 3

        def _cxin_conv(x, a, eps, W, b):
            ax = a @ x
            h = ax + (1.0 + eps[0]) * ax
            for i in range(L):
                h = jax.nn.relu(h @ W[i].T + b[i])
            return h
        key = jax.random.key(seed)
        ks = jax.random.split(key, 8)
        s = 1.0 / np.sqrt(D)
        return {'x1': jax.random.normal(ks[0], (N, D), jnp.float32), 'x2': jax.random.normal(ks[1], (N, D), jnp.float32), 'G1': jax.random.uniform(ks[2], (N, N), jnp.float32), 'G2': jax.random.uniform(ks[3], (N, N), jnp.float32), 'eps1': jnp.zeros((1,), jnp.float32), 'eps2': jnp.zeros((1,), jnp.float32), 'W1': jax.random.normal(ks[4], (L, D, D), jnp.float32) * s, 'b1': jnp.zeros((L, D), jnp.float32), 'W2': jax.random.normal(ks[5], (L, D, D), jnp.float32) * s, 'b2': jnp.zeros((L, D), jnp.float32), 'Wm': jax.random.normal(ks[6], (D, 2 * D), jnp.float32) * (1.0 / np.sqrt(2 * D)), 'bm': jnp.zeros((D,), jnp.float32)}
    _L2_gnn_all = _L2_gnn_setup()
    _L2_gnn_in = {k: v for k, v in _L2_gnn_all.items() if k in ('x2', 'eps1', 'eps2', 'W1', 'b1', 'W2', 'b2', 'Wm', 'bm')}
    del _L2_gnn_all

    def _L3_gnn_setup():
        import jax, jax.numpy as jnp
        import numpy as np
        GAMMA = 0.5
        NEG_SLOPE = 0.2
        MASK_FILL = -9000000000000000.0
        N, M, D = (4096, 4096, 128)
        SPARSITY = 0.01
        key = jax.random.key(seed)
        k1, k2, k3, k4, k5 = jax.random.split(key, 5)
        input1 = jax.random.normal(k1, (N, D), dtype=jnp.float32)
        input2 = jax.random.normal(k2, (M, D), dtype=jnp.float32)
        adj = (jax.random.uniform(k3, (N, M)) < SPARSITY).astype(jnp.float32)
        std = 1.414 * np.sqrt(2.0 / (D + 1))
        a1 = jax.random.normal(k4, (D, 1), dtype=jnp.float32) * std
        a2 = jax.random.normal(k5, (D, 1), dtype=jnp.float32) * std
        return {'input1': input1, 'input2': input2, 'adj': adj, 'a1': a1, 'a2': a2}
    _L3_gnn_all = _L3_gnn_setup()
    _L3_gnn_in = {k: v for k, v in _L3_gnn_all.items() if k in ('input2', 'a1', 'a2')}
    del _L3_gnn_all
    return {'x': x, 'adj': adj, 'L0_gnn_h0': _L0_gnn_in['h0'], 'L0_gnn_a': _L0_gnn_in['a'], 'L0_gnn_temp': _L0_gnn_in['temp'], 'L1_gnn_W_proj': _L1_gnn_in['W_proj'], 'L1_gnn_b_proj': _L1_gnn_in['b_proj'], 'L1_gnn_W_gcn': _L1_gnn_in['W_gcn'], 'L1_gnn_b_gcn': _L1_gnn_in['b_gcn'], 'L2_gnn_x2': _L2_gnn_in['x2'], 'L2_gnn_eps1': _L2_gnn_in['eps1'], 'L2_gnn_eps2': _L2_gnn_in['eps2'], 'L2_gnn_W1': _L2_gnn_in['W1'], 'L2_gnn_b1': _L2_gnn_in['b1'], 'L2_gnn_W2': _L2_gnn_in['W2'], 'L2_gnn_b2': _L2_gnn_in['b2'], 'L2_gnn_Wm': _L2_gnn_in['Wm'], 'L2_gnn_bm': _L2_gnn_in['bm'], 'L3_gnn_input2': _L3_gnn_in['input2'], 'L3_gnn_a1': _L3_gnn_in['a1'], 'L3_gnn_a2': _L3_gnn_in['a2']}

def reference(x, adj, L0_gnn_h0, L0_gnn_a, L0_gnn_temp, L1_gnn_W_proj, L1_gnn_b_proj, L1_gnn_W_gcn, L1_gnn_b_gcn, L2_gnn_x2, L2_gnn_eps1, L2_gnn_eps2, L2_gnn_W1, L2_gnn_b1, L2_gnn_W2, L2_gnn_b2, L2_gnn_Wm, L2_gnn_bm, L3_gnn_input2, L3_gnn_a1, L3_gnn_a2):
    import jax
    import jax.numpy as jnp

    def _L0_gnn_ref(x, h0, a, temp, adj, l):
        import jax, jax.numpy as jnp
        import numpy as np
        N = 4096
        F = 128
        NEG_INF = -9000000000000000.0
        ALPHA = 0.2
        THRESH = 1e-06
        Fdim = x.shape[1]
        feat_1 = x @ a[:Fdim]
        feat_2 = x @ a[Fdim:]
        e = jax.nn.leaky_relu(feat_1 + feat_2.T, ALPHA)
        att = jnp.where(adj > 0, e, NEG_INF)
        U = jax.nn.softmax(att, axis=1)
        P = 0.5 * U
        prop_u = U @ x
        rowsum = jnp.sum(U * P, axis=1)
        coe = jax.nn.sigmoid(temp)
        xi = x * rowsum[:, None]
        feat_odd = prop_u - xi
        feat_even = x + prop_u - xi
        feat = coe[2] * feat_odd + (1.0 - coe[2]) * feat_even
        sgn = jnp.sign(feat)
        mod = jnp.abs(feat)
        mod = jnp.where(mod > THRESH, mod - THRESH, 0.0)
        feat = mod * sgn
        pu = U @ feat
        feat_odd2 = feat - coe[3] * pu
        feat_even2 = pu + feat_odd2 * rowsum[:, None]
        feat_odd2 = coe[0] * feat_odd2 + (1.0 - coe[0]) * h0
        out = coe[1] * feat_even2 + (1.0 - coe[1]) * feat_odd2
        return out

    def _L1_gnn_ref(h, adj, simlar, W_proj, b_proj, W_gcn, b_gcn):
        import jax, jax.numpy as jnp
        import numpy as np
        N = 3072
        HID = 128
        T = 350
        DENSITY = 0.05
        sim = jnp.tanh(adj * simlar)
        filt = sim * (adj > 0).astype(sim.dtype)
        vals, idx = jax.lax.top_k(filt, T)
        nnz = jnp.sum(filt != 0, axis=1)
        keep = jnp.arange(T)[None, :] < nnz[:, None]
        rows = jnp.arange(filt.shape[0])[:, None]
        new_adj = jnp.zeros_like(filt).at[rows, idx].set(jnp.where(keep, vals, 0.0))
        h2 = jnp.tanh(h @ W_proj + b_proj)
        feat = jax.nn.relu(new_adj @ (h2 @ W_gcn) + b_gcn)
        return feat

    def _L2_gnn_ref(x1, x2, G1, G2, eps1, eps2, W1, b1, W2, b2, Wm, bm):
        import jax, jax.numpy as jnp
        import numpy as np
        N = 4096
        D = 128
        L = 3

        def _cxin_conv(x, a, eps, W, b):
            ax = a @ x
            h = ax + (1.0 + eps[0]) * ax
            for i in range(L):
                h = jax.nn.relu(h @ W[i].T + b[i])
            return h
        out1 = _cxin_conv(x1, G1, eps1, W1, b1)
        out2 = _cxin_conv(x2, G2, eps2, W2, b2)
        merged = jnp.concatenate((out1, out2), axis=1)
        return merged @ Wm.T + bm

    def _L3_gnn_ref(input1, input2, adj, a1, a2):
        import jax, jax.numpy as jnp
        import numpy as np
        GAMMA = 0.5
        NEG_SLOPE = 0.2
        MASK_FILL = -9000000000000000.0
        N, M, D = (4096, 4096, 128)
        SPARSITY = 0.01
        e1 = input1 @ a1
        e2 = (input2 @ a2).T
        e = jax.nn.leaky_relu(e1 + e2, negative_slope=NEG_SLOPE)
        attention = jnp.where(adj > 0, e, MASK_FILL)
        attention = jax.nn.softmax(attention, axis=1)
        attention = attention * jnp.sum(adj, axis=1, keepdims=True)
        attention = attention * GAMMA + adj * (1.0 - GAMMA)
        return attention @ input2
    h = jnp.maximum(_layernorm(x, axis=-1), 0.0)
    x = x + _L0_gnn_ref(h, L0_gnn_h0, L0_gnn_a, L0_gnn_temp, adj, 1)
    h = jnp.maximum(_layernorm(x, axis=-1), 0.0)
    x = x + _L1_gnn_ref(h, adj, adj, L1_gnn_W_proj, L1_gnn_b_proj, L1_gnn_W_gcn, L1_gnn_b_gcn)
    h = jnp.maximum(_layernorm(x, axis=-1), 0.0)
    x = x + _L2_gnn_ref(h, L2_gnn_x2, adj, adj, L2_gnn_eps1, L2_gnn_eps2, L2_gnn_W1, L2_gnn_b1, L2_gnn_W2, L2_gnn_b2, L2_gnn_Wm, L2_gnn_bm)
    h = jnp.maximum(_layernorm(x, axis=-1), 0.0)
    x = x + _L3_gnn_ref(h, L3_gnn_input2, adj, L3_gnn_a1, L3_gnn_a2)
    return x

_drawn_inputs = setup_inputs


def setup_inputs(seed=0):
    import zlib

    import numpy as np

    out = dict(_drawn_inputs(seed))
    spreads = {'L0_gnn_temp': (0.0, 2.0),
     'L1_gnn_b_proj': (0.0, 0.1),
     'L1_gnn_b_gcn': (0.0, 0.308),
     'L2_gnn_b1': (0.0, 0.716),
     'L2_gnn_b2': (0.0, 0.683),
     'L2_gnn_bm': (0.0, 0.435)}
    factors = {'L0_gnn_a': 3.02}
    for name, (base, spread) in spreads.items():
        noise = np.random.default_rng([zlib.crc32(name.encode()), seed]).standard_normal(out[name].shape)
        drawn = base * np.exp(spread * noise) if base else spread * noise
        out[name] = jnp.asarray(drawn.astype(out[name].dtype))
    for name, factor in factors.items():
        out[name] = (out[name] * factor).astype(out[name].dtype)
    return out
```

```python
import numpy as np
import concourse.bass as bass
from concourse import mybir
from concourse.alu_op_type import AluOpType as ALU

ACT = mybir.ActivationFunctionType
AX = mybir.AxisListType
F32, F16, BF16 = mybir.dt.float32, mybir.dt.float16, mybir.dt.bfloat16
I32, U8, FP8 = mybir.dt.int32, mybir.dt.uint8, mybir.dt.float8e4

N = 4096
D = 128
T = N // D
SW = 256
S = N // SW
SB = T * SW
RH = 264
RW = 2 * RH
CH = 4
CB = SB // CH
FP8_ONE = 0x38
EXP_BITS = 0x7F800000
LO = 4096.0
VS = 2.0 ** 15
HS = 2.0 ** 11
FS = 2.0 ** 10
TH = 1e-6
LEAK = 0.2
EPS = 1e-5
TOPK = 350
DENOM_MIN = 2.0 ** -22


SEMAPHORES = """
x_in vec_in y_in x2_in w_in rows_in0 rows_in1 rows_in2 rows_in3 rows_used h_made f1t_made job_done x16_made
h_stored f1_stored r3_stored r2x_stored r1y_stored f1_in0 f1_in1 masks_ready at_ready
consts_made stats_made var_made rstd_made maxima_made maxima_all exps_wanted exps_made coe_exp scaled_made hi_made rhs0_ready
prod_a ev_a ev_free_a xin_a feat_ready hi_a rb_ready feat_stored rb_stored R_b0 R_b1 R_b2 R_b3
prod_b ev_b ev_free_b xin_b xin_free_b x1_ready x1_stored r1_ready r1_stored var_b rstd_b norm_b hb_b ht_ps ht_sb pj_ps h2_sb g_ps hi_b
R_10 R_11 R_12 R_13 rows3_in w8_in w8_ps w8t_ready copy_1 prod_1 ev_1 ev_free_1 xin_1 xb_ready xb_stored ay_ready ay_stored
r2_ready r2_stored var_1 rstd_1 norm_1 hi_1
R_20 R_21 R_22 R_23 copy_2 prod_2 ev_2 ev_free_2 xin_2 xin_free_2 ax_ready net_ps0 net_sb0 net_ps1 net_sb1 net_ps2 net_sb2 net_ps3 net_sb3 net_ps4
xc_ready xc_stored var_2 rstd_2 norm_2 hb_2 u3_wanted u3_made f1_done f1_ps f1b_stored
R_30 R_31 R_32 R_33 prod_3 ev_3 ev_free_3 xin_3 xin_free_3 out_ready out_stored
v_pro v_mask v_a v_b v_1 v_2 v_3 a_pro a_b a_1 g_pro
"""


class Steps:

    def __init__(self, eng, sem):
        self.eng, self.sem, self.start, self.n, self.per = eng, sem, 0, 0, None

    def begin(self, strip):
        self.start = 0 if isinstance(strip, int) and strip == 0 else strip * self.per
        self.n = 0

    def end(self):
        if self.per is None:
            self.per = self.n
        assert self.per == self.n

    def did(self, ins):
        ins.then_inc(self.sem, 1)
        self.n += 1

    def sync(self):
        self.eng.wait_ge(self.sem, self.start + self.n)

    def do(self, ins):
        self.did(ins)
        self.sync()


def build(nc, x, adj, h0, a0, temp, w_proj, b_proj, w_gcn, b_gcn, x2, eps1, eps2,
          w1, b1, w2, b2, wm, bm, y, a1, a2, out):
    from contextlib import ExitStack
    ctx = ExitStack()
    with ctx:
        def sb(name, shape, dt=F32):
            return ctx.enter_context(nc.sbuf_tensor(name, shape, dt))

        def sem(name):
            return ctx.enter_context(nc.semaphore(name))

        def dram(name, shape, dt=F32):
            return nc.dram_tensor(name, shape, dt)

        AT = sb("AT", [128, S * SB], U8)
        GH = sb("GH", [128, 2, 2, SB], U8)
        R = sb("R", [128, T * RW], F16)
        STG = sb("STG", [128, 4, 512])
        F1R = sb("F1R", [128, 2, SW])
        XIN = sb("XIN", [128, 3, 2, D])
        EV = sb("EV", [128, 2 * RW])
        T4 = sb("T4", [128, 4, D])
        WA = sb("WA", [128, 2, D])
        WB = sb("WB", [128, 2, D])
        ST16 = sb("ST16", [128, 2, RW], F16)
        ST32 = sb("ST32", [128, 2, D])
        WP = sb("WP", [128, D])
        WG = sb("WG", [128, D])
        IDF = sb("IDF", [128, D])
        IDB = sb("IDB", [128, D], BF16)
        TBL = sb("TBL", [128, S, 2, 8])
        CUR = sb("CUR", [128, 2, 8])
        RT = sb("RT", [128, S, 2, 4])
        RTC = sb("RTC", [128, 2, 4])
        DEN = sb("DEN", [128, 2, T])
        DEG = sb("DEG", [128, T])
        F1 = sb("F1", [128, T])
        F2N = sb("F2N", [128, 2, T])
        COL = sb("COL", [128, 48])
        SM = sb("SM", [128, 64])
        MV = sb("MV", [128, 2, 8])
        CO = sb("CO", [128, 6])

        def col(i):
            return COL[:, i:i + 1]
        (MX0, MX3, AMY, AMX, AMG, SY, SX, SG, ISY, ISX, ISG, C0, C1, C2, C3, K2, BP, TG, KE1, KE2,
         NM0, NM3, BIAS0) = range(23)
        B6 = 24
        CSY, OMC2, E5, C1C0, AX1, AX2, ONE, MH, NC3, CG = 30, 31, 33, 40, 41, 42, 43, 44, 45, 46
        NW = 12

        GHf = GH[:].bitcast(FP8)
        GH16 = GH[:].bitcast(mybir.dt.uint16)
        GHI = GH[:].bitcast(I32)
        slots = AT[:].bitcast(F32).rearrange("p (k n) -> p k n", n=N)
        PX2, PY, PT, PU, PX, PH = (slots[:, k, :].rearrange("p (t d) -> p t d", d=D) for k in range(2, 8))
        P16 = {k: slots[:, k, :].bitcast(F16).rearrange("p (t c) -> p t c", c=256) for k in (2, 3, 6, 7)}
        A3 = slots[:, 1, 0:3 * D].rearrange("p (k d) -> p k d", d=D)
        LT = slots[:, 1, 512:512 + 24 * T].rearrange("p (k t) -> p k t", t=T)
        E16 = slots[:, 1, 2048:2048 + 6 * T].bitcast(F16).rearrange("p (q k t) -> p q k t", q=4, k=3)
        X16 = slots[:, 1, 3072:3072 + 8 * T].bitcast(F16).rearrange("p (t g e) -> p t g e", g=2, e=8)
        R3 = R[:].rearrange("p (t c) -> p t c", c=RW)
        R5 = R[:, 0:T * 512].rearrange("p (t c) -> p t c", c=512)
        W8 = STG[:, 0:2, :].rearrange("p a (b d) -> p (a b) d", d=D)
        W8T = STG[:, 2:4, :].rearrange("p a (b d) -> p (a b) d", d=D)
        HT = STG[:, 0, 0:SW]
        H2T = STG[:, 1, 0:SW]
        NETS = GH[:, 0, 1, :].bitcast(F32).rearrange("p (l n) -> p l n", n=512)
        ROWS = GH[:, 1, 1, 0:4 * 3 * D].bitcast(F32).rearrange("p (k d) -> p k d", d=D)
        BG, BM, A1R = ROWS[:, 0, :], ROWS[:, 1, :], ROWS[:, 2, :]
        FT = T4[0:T, 0, :]
        F1T = T4[:, 0, 0:T]
        XT = EV[:, 0:6 * T].rearrange("p (k t) -> p k t", t=T)
        EVq = EV[:].rearrange("p (q c) -> p q c", c=RH)
        EV5 = EV[:, 0:1024].rearrange("p (q c) -> p q c", c=256)
        ST16q = ST16[:].rearrange("p i (g c) -> p (i g) c", c=RH)
        TBLt = TBL[:].rearrange("p s i w -> p (s i) w")
        RTt = RT[:].rearrange("p s i w -> p (s i) w")

        ps = [ctx.enter_context(nc.psum_tensor(f"ps{b}", [128, 512], F32)) for b in range(8)]

        f1_d = [dram(f"f1_{k}", [T, D]) for k in range(2)]
        h_d, feat_d, x1_d, xb_d, xc_d, ay_d = (dram(n, [128, T, D]) for n in ("h_s", "feat_s", "x1_s", "xb_s", "xc_s", "ay_s"))
        rb_d = dram("rb_s", [128, T, RW], F16)
        r1_d = dram("r1_s", [128, T, 512], F16)
        r2_d = dram("r2_s", [128, T, 512], F16)
        r3_d = dram("r3_s", [128, T, RW], F16)
        tile_rows = lambda t: t.rearrange("(t p) d -> p t d", p=128)

        sems = {n: sem(n) for n in SEMAPHORES.split()}
        sm = sems.__getitem__

        block = ctx.enter_context(nc.Block())
        BCAST = lambda ap1, n=D: ap1.unsqueeze(2).broadcast_to([128, ap1.shape[1], n])

        def ring(eng, body):
            for s in (0, 1):
                body(s, s, 0)
            with eng.Fori(1, S // 2 - 1) as k:
                body(k * 2, 0, k)
                body(k * 2 + 1, 1, k)
            for s in (S - 2, S - 1):
                body(s, s % 2, S // 2 - 1)

        first = lambda s: isinstance(s, int) and s == 0
        last = lambda s: isinstance(s, int) and s == S - 1

        @block.sync
        def _(sp):
            ld = lambda dst, src, s: sp.dma_start(dst, src).then_inc(sm(s), 16)
            ld(PX, tile_rows(x), "x_in")
            a0c = a0.rearrange("(k d) o -> k (d o)", k=2)
            ld(A3[:, 0, :], a0c[0, :].partition_broadcast(128), "vec_in")
            ld(A3[:, 1, :], a0c[1, :].partition_broadcast(128), "vec_in")
            ld(A3[:, 2, :], a2.rearrange("d o -> (d o)").partition_broadcast(128), "vec_in")
            ld(PY, tile_rows(y), "y_in")
            ld(PX2, tile_rows(x2), "x2_in")
            ld(WP[:], w_proj, "w_in")
            ld(WG[:], w_gcn, "w_in")
            ld(COL[:, C0:C0 + 5], temp.partition_broadcast(128), "w_in")
            ld(COL[:, KE1:KE1 + 1], eps1.partition_broadcast(128), "w_in")
            ld(COL[:, KE2:KE2 + 1], eps2.partition_broadcast(128), "w_in")
            ld(col(BP), b_proj.rearrange("(d o) -> d o", o=1), "w_in")
            for j, b in enumerate((b1, b2)):
                for l in range(3):
                    ld(COL[:, B6 + 3 * j + l:B6 + 3 * j + l + 1], b[l, :].rearrange("(d o) -> d o", o=1), "w_in")

            def load_strip_rows(s, between, start=0, stop=16):
                n = 0
                for cp in range(4):
                    for it in range(2):
                        for c in (2 * cp, 2 * cp + 1):
                            q = cp * 4 + it * 2 + c % 2
                            if not start <= q < stop:
                                continue
                            if not (isinstance(s, int) and s * 16 + q < 4):
                                sp.wait_ge(sm("rows_used"), s * 16 + (q - 3))
                            ld(STG[:, q % 4, :], adj[bass.ds(s * SW + it * 128, 128), c * 512:(c + 1) * 512],
                               f"rows_in{q % 4}")
                            if n in between:
                                between[n]()
                            n += 1

            load_strip_rows(0, {}, 0, 4)
            sp.wait_ge(sm("h_made"), 1)
            ld(h_d[:, :, :], PH, "h_stored")
            sp.wait_ge(sm("f1t_made"), 1)
            ld(f1_d[0][:, :], FT, "f1_stored")
            sp.wait_ge(sm("job_done"), 4)
            ld(r3_d[:, :, 0:256], P16[6], "r3_stored")
            ld(r3_d[:, :, RH:RH + 256], P16[7], "r3_stored")
            sp.wait_ge(sm("x16_made"), 1)
            ld(r3_d[:, :, 256:RH], X16[:, :, 0, :], "r3_stored")
            ld(r3_d[:, :, RH + 256:RW], X16[:, :, 1, :], "r3_stored")
            sp.wait_ge(sm("job_done"), 5)
            ld(r2_d[:, :, 256:512], P16[2], "r2x_stored")
            sp.wait_ge(sm("job_done"), 6)
            ld(r1_d[:, :, 256:512], P16[3], "r1y_stored")
            load_strip_rows(0, {}, 4, 16)
            sp.wait_ge(sm("h_stored"), 16)
            sp.wait_ge(sm("f1_stored"), 16)
            f1row = lambda k: f1_d[k].rearrange("t p -> (t p)")

            def load_f1(k, s, par, g):
                if g is not None:
                    sp.wait_ge(sm("masks_ready"), g)
                ld(F1R[:, par, :], f1row(k)[bass.ds(s * SW, SW)].partition_broadcast(128), f"f1_in{par}")

            load_f1(0, 0, 0, None)
            load_f1(0, 1, 1, None)

            def l0a(s, par, k):
                def early():
                    load_f1(0, (s + 2) if not (isinstance(s, int) and s >= S - 2) else s + 2 - S, par, 4 * (s + 1))

                def late():
                    if not first(s):
                        store_a(s - 1)
                        sp.wait_ge(sm("feat_ready"), s)
                    ld(XIN[:, 0, :, :], h_d[:, bass.ds(s * 2, 2), :], "xin_a")

                if last(s):
                    early(), late()
                else:
                    load_strip_rows(s + 1, {7: early, 11: late})

            def store_a(s):
                sp.wait_ge(sm("feat_ready"), s + 1)
                ld(feat_d[:, bass.ds(s * 2, 2), :], ST32[:], "feat_stored")
                sp.wait_ge(sm("rb_ready"), s + 1)
                ld(rb_d[:, bass.ds(s * 2, 2), :], ST16[:], "rb_stored")

            ring(sp, l0a)
            store_a(S - 1)

            def load_R(src, width, stored, count, used, usedn, name):
                sp.wait_ge(sm(stored), count)
                sp.wait_ge(sm(used), usedn)
                dst = R[:, 0:T * width].rearrange("p (t c) -> p t c", c=width)
                for c in range(4):
                    ld(dst[:, 8 * c:8 * c + 8, :], src[:, 8 * c:8 * c + 8, :], name + str(c))

            load_R(rb_d, RW, "rb_stored", 16 * S, "prod_a", 2 * S, "R_b")
            sp.wait_ge(sm("feat_stored"), 16 * S)

            xt = tile_rows(x)
            h0t = tile_rows(h0)

            def l0b(s, par, k):
                if not first(s):
                    sp.wait_ge(sm("xin_free_b"), s)
                ld(XIN[:, 0, :, :], xt[:, bass.ds(s * 2, 2), :], "xin_b")
                ld(XIN[:, 1, :, :], feat_d[:, bass.ds(s * 2, 2), :], "xin_b")
                ld(XIN[:, 2, :, :], h0t[:, bass.ds(s * 2, 2), :], "xin_b")
                if not (isinstance(s, int) and s >= S - 2):
                    load_f1(0, s + 2, par, 4 * S + 4 * (s + 1))
                if not first(s):
                    store_b(s - 1)

            def store_b(s):
                sp.wait_ge(sm("x1_ready"), s + 1)
                ld(x1_d[:, bass.ds(s * 2, 2), :], ST32[:], "x1_stored")
                sp.wait_ge(sm("r1_ready"), s + 1)
                ld(r1_d[:, bass.ds(s * 2, 2), 0:256], ST16[:, :, 0:256], "r1_stored")

            ring(sp, l0b)
            store_b(S - 1)
            sp.wait_ge(sm("r1y_stored"), 16)
            load_R(r1_d, 512, "r1_stored", 16 * S, "prod_b", 2 * S, "R_1")
            sp.wait_ge(sm("x1_stored"), 16 * S)

            for k, v in enumerate((b_gcn, bm, a1.rearrange("d o -> (d o)"))):
                ld(ROWS[:, k, :], v.partition_broadcast(128), "rows3_in")
            for j, w in enumerate((w1, w2)):
                for l in range(3):
                    ld(W8[:, 3 * j + l, :], w[l, :, :], "w8_in")
            for j in range(2):
                ld(W8[:, 6 + j, :], wm[:, j * D:(j + 1) * D], "w8_in")

            def l1(s, par, k):
                if not first(s):
                    sp.wait_ge(sm("xb_ready"), s)
                ld(XIN[:, 0, :, :], x1_d[:, bass.ds(s * 2, 2), :], "xin_1")
                if not first(s):
                    store_1(s - 1)

            def store_1(s):
                sp.wait_ge(sm("xb_ready"), s + 1)
                ld(xb_d[:, bass.ds(s * 2, 2), :], ST32[:], "xb_stored")
                sp.wait_ge(sm("ay_ready"), s + 1)
                ld(ay_d[:, bass.ds(s * 2, 2), :], WB[:], "ay_stored")
                sp.wait_ge(sm("r2_ready"), s + 1)
                ld(r2_d[:, bass.ds(s * 2, 2), 0:256], ST16[:, :, 0:256], "r2_stored")

            ring(sp, l1)
            store_1(S - 1)
            sp.wait_ge(sm("r2x_stored"), 16)
            load_R(r2_d, 512, "r2_stored", 16 * S, "prod_1", 2 * S, "R_2")
            sp.wait_ge(sm("xb_stored"), 16 * S)
            sp.wait_ge(sm("ay_stored"), 16 * S)

            def l2(s, par, k):
                if not first(s):
                    sp.wait_ge(sm("xin_free_2"), s)
                ld(XIN[:, 0, :, :], xb_d[:, bass.ds(s * 2, 2), :], "xin_2")
                if not first(s):
                    store_2(s - 1)

            def store_2(s):
                sp.wait_ge(sm("xc_ready"), s + 1)
                ld(xc_d[:, bass.ds(s * 2, 2), :], ST32[:], "xc_stored")

            ring(sp, l2)
            store_2(S - 1)
            sp.wait_ge(sm("r3_stored"), 16)
            load_R(r3_d, RW, "r3_stored", 64, "prod_2", 2 * S, "R_3")
            sp.wait_ge(sm("xc_stored"), 16 * S)
            sp.wait_ge(sm("f1t_made"), 2)
            ld(f1_d[1][:, :], FT, "f1b_stored")
            sp.wait_ge(sm("f1b_stored"), 16)

            load_f1(1, 0, 0, None)
            load_f1(1, 1, 1, None)

            def l3(s, par, k):
                if not first(s):
                    sp.wait_ge(sm("xin_free_3"), s)
                ld(XIN[:, 0, :, :], xc_d[:, bass.ds(s * 2, 2), :], "xin_3")
                ld(XIN[:, 1, :, :], ay_d[:, bass.ds(s * 2, 2), :], "xin_3")
                if not (isinstance(s, int) and s >= S - 2):
                    load_f1(1, s + 2, par, 8 * S + 4 * (s + 1))
                if not first(s):
                    store_3(s - 1)

            ot = tile_rows(out)

            def store_3(s):
                sp.wait_ge(sm("out_ready"), s + 1)
                ld(ot[:, bass.ds(s * 2, 2), :], ST32[:], "out_stored")

            ring(sp, l3)
            store_3(S - 1)
            sp.wait_ge(sm("out_stored"), 16 * S)


        @block.gpsimd
        def _(pool):
            g = Steps(pool, sm("g_pro"))
            g.did(pool.memset(IDF[:], 0.0))
            g.did(pool.memset(IDB[:], 0.0))
            g.sync()
            for m in (IDF, IDB):
                g.did(pool.affine_select(out=m[:], in_=m[:], compare_op=ALU.not_equal, fill=1.0, base=0,
                                         pattern=[[-1, D]], channel_multiplier=1))
            for k in range(3):
                for q in range(2):
                    g.did(pool.memset(CO[:, 3 * q + k:3 * q + k + 1], 1.0 / VS / LO ** k))
            g.did(pool.memset(LT[:, 0, :], -0.5))
            g.did(pool.memset(COL[:, ONE:ONE + 1], 1.0))
            g.did(pool.memset(ST16[:], 0.0))
            g.did(pool.memset(COL[:, MH:MH + 1], -0.5))
            for w in (0, RH):
                g.did(pool.memset(R3[:, :, w + 262:w + 263], 1.0))
                g.did(pool.memset(R3[:, :, w + 263:w + 264], 0.0))
            g.did(pool.memset(X16[:, :, :, 6:7], 1.0))
            g.did(pool.memset(X16[:, :, :, 7:8], 0.0))
            g.sync()
            pool.nop().then_inc(sm("consts_made"), 1)
            pool.wait_ge(sm("var_made"), 1)
            pool.tensor_tensor(LT[:, 2, :], LT[:, 1, :], LT[:, 0, :], ALU.pow).then_inc(sm("rstd_made"), 1)
            pool.wait_ge(sm("maxima_made"), 1)
            pool.partition_all_reduce(COL[:, 0:5], SM[:, 0:5], 128, bass.bass_isa.ReduceOp.max).then_inc(sm("maxima_all"), 1)

            def rstd(phase):
                def body(s, par, k):
                    pool.wait_ge(sm("var_" + phase), s + 1)
                    pool.tensor_tensor(MV[:, :, 3], MV[:, :, 2], col(MH).broadcast_to([128, 2]),
                                       ALU.pow).then_inc(sm("rstd_" + phase), 1)
                with pool.Fori(0, S) as s:
                    body(s, 0, 0)

            rstd("b")
            rstd("1")
            rstd("2")

        @block.vector
        def _(dve):
            v = Steps(dve, sm("v_pro"))
            ts, tt, stt, red = dve.tensor_scalar, dve.tensor_tensor, dve.scalar_tensor_tensor, dve.tensor_reduce
            lt = lambda k: LT[:, k, :]
            dve.wait_ge(sm("consts_made"), 1)
            dve.wait_ge(sm("x_in"), 16)
            v.do(red(lt(3), PX, AX.X, ALU.add))
            v.do(ts(lt(3), lt(3), 1.0 / D, None, ALU.mult))
            v.do(tt(PT, PX, BCAST(lt(3)), ALU.subtract))
            v.do(tt(PU, PT, PT, ALU.mult))
            v.do(red(lt(1), PU, AX.X, ALU.add))
            ts(lt(1), lt(1), 1.0 / D, EPS, ALU.mult, ALU.add).then_inc(sm("var_made"), 1)
            dve.wait_ge(sm("rstd_made"), 1)
            stt(PH, PT, 0.0, BCAST(lt(2)), ALU.max, ALU.mult).then_inc(sm("h_made"), 1)
            dve.wait_ge(sm("h_made"), 1)
            vec = lambda k: A3[:, k, :].unsqueeze(1).broadcast_to([128, T, D])
            dve.wait_ge(sm("vec_in"), 48)
            v.do(tt(PU, PH, vec(0), ALU.mult))
            red(F1[:], PU, AX.X, ALU.add).then_inc(sm("f1_done"), 1)
            dve.wait_ge(sm("f1_done"), 1)
            v.do(tt(PU, PH, vec(1), ALU.mult))
            v.do(red(lt(4), PU, AX.X, ALU.add))
            dve.wait_ge(sm("y_in"), 16)
            v.do(tt(PU, PY, vec(2), ALU.mult))
            v.do(red(lt(5), PU, AX.X, ALU.add))
            dve.wait_ge(sm("x2_in"), 16)
            dve.wait_ge(sm("w_in"), 16 * NW)
            v.did(red(SM[:, 0:1], lt(4), AX.X, ALU.max))
            v.did(red(SM[:, 1:2], lt(5), AX.X, ALU.max))
            v.did(red(SM[:, 2:3], PY, AX.XY, ALU.max, apply_absolute_value=True))
            v.did(red(SM[:, 3:4], PX2, AX.XY, ALU.max, apply_absolute_value=True))
            v.do(red(SM[:, 4:5], WG[:], AX.X, ALU.max, apply_absolute_value=True))
            v.do(ts(SM[:, 4:5], SM[:, 4:5], float(D), None, ALU.mult))
            dve.engine_nop().then_inc(sm("maxima_made"), 1)
            dve.wait_ge(sm("f1_ps"), 1)
            dve.tensor_copy(FT, ps[7][0:T, 0:D]).then_inc(sm("f1t_made"), 1)
            dve.wait_ge(sm("maxima_all"), 1)
            v.do(ts(SM[:, 8:11], COL[:, AMY:AMG + 1], 1e-30, None, ALU.max))
            v.do(ts(SM[:, 8:11].bitcast(I32), SM[:, 8:11].bitcast(I32), EXP_BITS, None, ALU.bitwise_and))
            v.did(ts(COL[:, ISY:ISY + 3], SM[:, 8:11], 1.0 / 8192, None, ALU.mult))
            v.do(dve.reciprocal(SM[:, 12:15], SM[:, 8:11]))
            v.did(ts(COL[:, SY:SY + 3], SM[:, 12:15], 8192.0, None, ALU.mult))
            v.did(ts(COL[:, NM0:NM0 + 2], COL[:, MX0:MX0 + 2], -1.0, None, ALU.mult))
            v.sync()
            v.do(ts(lt(6), F1[:], col(MX0), None, ALU.add))
            v.do(stt(lt(7), lt(6), LEAK, lt(6), ALU.mult, ALU.max))
            v.did(tt(lt(8), lt(6), lt(7), ALU.subtract))
            v.did(stt(lt(9), lt(6), LEAK, lt(7), ALU.mult, ALU.subtract))
            v.did(ts(lt(10), lt(4), col(MX0), None, ALU.subtract))
            v.did(ts(lt(11), lt(4), col(MX0), LEAK, ALU.subtract, ALU.mult))
            v.did(ts(lt(12), lt(5), col(MX3), None, ALU.subtract))
            v.did(ts(lt(13), lt(5), col(MX3), LEAK, ALU.subtract, ALU.mult))
            v.did(ts(F2N[:, 0, :], lt(4), -1.0, None, ALU.mult))
            v.did(ts(F2N[:, 1, :], lt(5), -1.0, None, ALU.mult))
            v.sync()
            dve.engine_nop().then_inc(sm("exps_wanted"), 1)
            dve.wait_ge(sm("exps_made"), 1)

            def factors(u, up):
                v.did(dve.tensor_copy(TBLt[:, :, 0], u))
                v.did(tt(TBLt[:, :, 1], u, u, ALU.mult))
                v.did(dve.tensor_copy(TBLt[:, :, 2], up))
                v.did(tt(TBLt[:, :, 3], up, up, ALU.mult))

            factors(lt(14), lt(15))
            for k, c in ((4, FS), (6, FS * LO)):
                v.did(ts(TBLt[:, :, k], lt(16), c, None, ALU.mult))
                v.did(ts(TBLt[:, :, k + 1], lt(17), c, None, ALU.mult))

            def extras(va, vb, dst):
                VV, RR = LT[:, 20:24, :], slots[:, 1, 3584:3584 + 4 * T].rearrange("p (k t) -> p k t", t=T)
                v.sync()
                v.did(ts(lt(20), va, VS, None, ALU.mult))
                v.did(ts(lt(22), vb, VS, None, ALU.mult))
                v.did(stt(lt(21), va, VS, va, ALU.mult, ALU.mult))
                v.do(stt(lt(23), vb, VS, vb, ALU.mult, ALU.mult))
                for part in range(3):
                    v.do(dve.tensor_copy(E16[:, :, part, :], VV))
                    if part < 2:
                        v.do(tt(RR, VV, E16[:, :, part, :], ALU.subtract))
                        v.do(ts(VV, RR, LO, None, ALU.mult))
                for q in range(4):
                    v.did(dve.tensor_copy(dst(q), E16[:, q, :, :].rearrange("p k t -> p t k")))
                v.sync()

            extras(lt(16), lt(17), lambda q: R3[:, :, RH * (q // 2) + 256 + 3 * (q % 2):RH * (q // 2) + 259 + 3 * (q % 2)])
            v.did(ts(lt(16), lt(16), HS, None, ALU.mult))
            v.did(ts(lt(17), lt(17), HS, None, ALU.mult))
            extras(lt(18), lt(19), lambda q: X16[:, :, q // 2, 3 * (q % 2):3 * (q % 2) + 3])
            dve.engine_nop().then_inc(sm("x16_made"), 1)
            v.did(ts(lt(18), lt(18), col(SY), None, ALU.mult))
            v.did(ts(lt(19), lt(19), col(SY), None, ALU.mult))
            c = lambda k: col(C0 + k)
            v.do(ts(COL[:, E5:E5 + 5], COL[:, E5:E5 + 5], 1.0, None, ALU.add))
            v.do(dve.reciprocal(COL[:, C0:C0 + 5], COL[:, E5:E5 + 5]))
            v.did(ts(SM[:, 16:20], COL[:, C0:C0 + 4], -1.0, 1.0, ALU.mult, ALU.add))
            v.sync()
            v.did(dve.tensor_copy(col(OMC2), SM[:, 18:19]))
            v.did(tt(col(K2), SM[:, 17:18], SM[:, 16:17], ALU.mult))
            v.did(tt(col(C1C0), SM[:, 17:18], c(0), ALU.mult))
            v.did(ts(col(NC3), c(3), -1.0, None, ALU.mult))
            v.did(tt(col(CG), col(TG), col(ISG), ALU.mult))
            v.did(ts(col(CSY), col(ISY), 0.5, None, ALU.mult))
            v.did(ts(col(AX1), col(KE1), 2.0, 1.0 / HS, ALU.add, ALU.mult))
            v.did(stt(col(AX2), col(KE2), 2.0, col(ISX), ALU.add, ALU.mult))
            v.sync()
            jobs = [(PH, lt(16), R3[:, :, 0:128], R3[:, :, 128:256]),
                    (PH, lt(17), R3[:, :, RH:RH + 128], R3[:, :, RH + 128:RH + 256]),
                    (PY, lt(18), P16[6][:, :, 0:128], P16[6][:, :, 128:256]),
                    (PY, lt(19), P16[7][:, :, 0:128], P16[7][:, :, 128:256]),
                    (PX2, col(SX), P16[2][:, :, 0:128], P16[2][:, :, 128:256]),
                    (PY, col(SY), P16[3][:, :, 0:128], P16[3][:, :, 128:256])]
            for j, (src, scale, hi, lo) in enumerate(jobs):
                if j < 4:
                    tt(PT, src, BCAST(scale), ALU.mult).then_inc(sm("scaled_made"), 1)
                else:
                    ts(PT, src, scale, None, ALU.mult).then_inc(sm("scaled_made"), 1)
                dve.wait_ge(sm("scaled_made"), j + 1)
                v.did(ts(PU, PT, LO, None, ALU.mult))
                dve.wait_ge(sm("hi_made"), j + 1)
                v.sync()
                stt(lo, hi, -LO, PU, ALU.mult, ALU.add).then_inc(sm("job_done"), 1)
                dve.wait_ge(sm("job_done"), j + 1)

            m = Steps(dve, sm("v_mask"))

            def masks(layer, s, par, k, chunks):
                q = s + layer * S
                mk = F2N[:, 0 if layer < 2 else 1, :]
                for ch in chunks:
                    if ch == 0:
                        dve.wait_ge(sm(f"f1_in{par}"), (k + layer * (S // 2) + 1) * 16)
                        if layer == 0 and not (isinstance(s, int) and s < 2):
                            dve.wait_ge(sm("prod_a"), 2 * (s - 1))
                        if layer == 1 and isinstance(s, int) and s < 2:
                            dve.wait_ge(sm("prod_a"), 2 * (S + s - 1))
                        elif layer == 1:
                            dve.wait_ge(sm("prod_b"), 2 * (s - 1))
                        if layer == 2 and not (isinstance(s, int) and s < 2):
                            dve.wait_ge(sm("prod_3"), 2 * (s - 1))
                    if layer == 0:
                        dve.wait_ge(sm("at_ready"), s * 8 + (2 * ch + 2))
                    for jb in range(8 * ch, 8 * ch + 8):
                        last_ = ts(GH[:, par, 0, jb * SW:(jb + 1) * SW], F1R[:, par, :], mk[:, jb:jb + 1],
                                   float(FP8_ONE), ALU.is_gt, ALU.mult)
                    last_.then_inc(sm("v_mask"), 1)
                    dve.wait_ge(sm("v_mask"), q * 8 + (2 * ch + 1))
                    at = AT[:, bass.ds(s * SB + ch * CB, CB)].bitcast(I32)
                    g0, g1 = GHI[:, par, 0, ch * (CB // 4):(ch + 1) * (CB // 4)], GHI[:, par, 1, ch * (CB // 4):(ch + 1) * (CB // 4)]
                    tt(g0, g0, at, ALU.bitwise_and).then_inc(sm("v_mask"), 1)
                    dve.wait_ge(sm("v_mask"), q * 8 + (2 * ch + 2))
                    tt(g1, g0, at, ALU.bitwise_xor).then_inc(sm("masks_ready"), 1)

            def softmax_sums(w, s, layer):
                w.do(dve.tensor_copy(CUR[:], TBL[:, bass.ds(s, 1), :, :].rearrange("p o i w -> p (o i) w")))
                w.do(tt(SM[:, 0:24].rearrange("p (q k) -> p q k", k=6), EVq[:, :, 256:262],
                        CO[:].unsqueeze(1).broadcast_to([128, 4, 6]), ALU.mult))
                w.do(red(SM[:, 24:32], SM[:, 0:24].rearrange("p (q k) -> p q k", k=3), AX.X, ALU.add))
                w.do(tt(SM[:, 32:40].rearrange("p (i w) -> p i w", i=2), SM[:, 24:32].rearrange("p (i w) -> p i w", i=2),
                        CUR[:, :, 0:4], ALU.mult))
                four = SM[:, 32:40].rearrange("p (i g w) -> p i g w", i=2, g=2)
                dq = SM[:, 40:44].rearrange("p (i w) -> p i w", i=2)
                w.do(tt(dq, four[:, :, 0, :], four[:, :, 1, :], ALU.add))
                w.did(dve.tensor_copy(DEN[:, layer, bass.ds(s * 2, 2)], dq[:, :, 0]))
                w.do(dve.reciprocal(SM[:, 44:46], dq[:, :, 0]))
                return dq, SM[:, 44:46]

            def combine(w, s, ev, name):
                stt(T4[:], ev[:, :, 128:256], 1.0 / LO, ev[:, :, 0:128], ALU.mult, ALU.add).then_inc(sm(name), 1)
                w.sync()
                dve.wait_ge(sm(name), s + 1)

            wa = Steps(dve, sm("v_a"))

            def filter_1(s):
                wa.begin(s)
                dve.wait_ge(sm("ev_a"), s * 2 + 2)
                dq, rd = softmax_sums(wa, s, 0)
                wa.do(tt(SM[:, 46:48], dq[:, :, 1], rd, ALU.mult))
                wa.do(stt(RTC[:, :, 2], SM[:, 46:48], 0.5, rd, ALU.mult, ALU.mult))
                wa.did(stt(RTC[:, :, 0:2], CUR[:, :, 0:4:2], 1.0 / HS, BCAST(rd, 2), ALU.mult, ALU.mult))
                wa.do(ts(RTC[:, :, 3], RTC[:, :, 2], -1.0, col(OMC2), ALU.mult, ALU.add))
                wa.did(dve.tensor_copy(RT[:, bass.ds(s, 1), :, :].rearrange("p o i w -> p (o i) w"), RTC[:]))
                combine(wa, s, EVq, "ev_free_a")
                dve.wait_ge(sm("xin_a"), s * 16 + 16)
                for it in range(2):
                    wa.did(ts(WA[:, it, :], T4[:, 2 * it + 1, :], RTC[:, it, 1:2], None, ALU.mult))
                wa.sync()
                for it in range(2):
                    wa.did(stt(WA[:, it, :], T4[:, 2 * it, :], RTC[:, it, 0:1], WA[:, it, :], ALU.mult, ALU.add))
                wa.sync()
                for it in range(2):
                    wa.did(stt(WA[:, it, :], XIN[:, 0, it, :], RTC[:, it, 3:4], WA[:, it, :], ALU.mult, ALU.add))
                wa.sync()
                wa.do(ts(WB[:], WA[:], TH, -TH, ALU.min, ALU.max))
                if not first(s):
                    dve.wait_ge(sm("feat_stored"), s * 16)
                tt(ST32[:], WA[:], WB[:], ALU.subtract).then_inc(sm("feat_ready"), 1)

            def filter_2(s):
                dve.wait_ge(sm("hi_a"), s + 1)
                stt(ST16q[:, :, 128:256], ST16q[:, :, 0:128], -LO, T4[:], ALU.mult, ALU.add).then_inc(sm("rb_ready"), 1)
                wa.end()

            masks(0, 0, 0, 0, range(CH))

            def l0a(s, par, k):
                if first(s):
                    masks(0, 1, 1, 0, range(CH))
                    return
                filter_1(s - 1)
                nxt = (1, 0, 0, 0) if last(s) else (0, s + 1, 1 - par, k if par == 0 else k + 1)
                masks(*nxt, range(0, 1))
                filter_2(s - 1)
                masks(*nxt, range(1, CH))

            ring(dve, l0a)
            filter_1(S - 1)
            filter_2(S - 1)

            t0 = RTt[:, :, 2]
            v.did(ts(t0, t0, c(1), col(C1C0), ALU.mult, ALU.add))
            dve.wait_ge(sm("rb_ready"), S)
            v.sync()
            v.do(ts(F1T, t0, col(NC3), c(1), ALU.mult, ALU.add))
            for i in range(2):
                v.did(stt(RTt[:, :, i], RTt[:, :, i], HS / FS, F1T, ALU.mult, ALU.mult))
            v.sync()
            wb = Steps(dve, sm("v_b"))
            dve.wait_ge(sm("feat_stored"), 16 * S)

            def normalise(w, src, phase):
                for it in range(2):
                    w.did(dve.bn_stats(SM[:, 48 + 6 * it:54 + 6 * it], src[:, it, :]))
                w.sync()
                dve.memset(MV[:, :, 5:6], 0.0)
                for it in range(2):
                    w.did(dve.bn_aggr(MV[:, it, 0:2], SM[:, 48 + 6 * it:54 + 6 * it]))
                w.sync()
                ts(MV[:, :, 2], MV[:, :, 1], EPS, None, ALU.add).then_inc(sm("var_" + phase), 1)

            def normalise_2(s, phase):
                dve.wait_ge(sm("rstd_" + phase), s + 1)
                stt(MV[:, :, 4], MV[:, :, 0], -1.0, MV[:, :, 3], ALU.mult, ALU.mult).then_inc(sm("norm_" + phase), 1)

            def feed_1(s):
                wb.begin(s)
                wb.do(dve.tensor_copy(RTC[:], RT[:, bass.ds(s, 1), :, :].rearrange("p o i w -> p (o i) w")))
                dve.wait_ge(sm("ev_b"), s * 2 + 2)
                if not first(s):
                    dve.wait_ge(sm("r1_ready"), s)
                combine(wb, s, EVq, "ev_free_b")
                dve.wait_ge(sm("xin_b"), s * 48 + 48)
                wb.do(stt(WA[:], XIN[:, 2, :, :], col(K2), XIN[:, 0, :, :], ALU.mult, ALU.add))
                for it in range(2):
                    ins = stt(WA[:, it, :], XIN[:, 1, it, :], RTC[:, it, 2:3], WA[:, it, :], ALU.mult, ALU.add)
                ins.then_inc(sm("xin_free_b"), 1)
                dve.wait_ge(sm("xin_free_b"), s + 1)
                for it in range(2):
                    wb.did(stt(WA[:, it, :], T4[:, 2 * it, :], RTC[:, it, 0:1], WA[:, it, :], ALU.mult, ALU.add))
                wb.sync()
                if not first(s):
                    dve.wait_ge(sm("x1_stored"), s * 16)
                for it in range(2):
                    ins = stt(ST32[:, it, :], T4[:, 2 * it + 1, :], RTC[:, it, 1:2], WA[:, it, :], ALU.mult, ALU.add)
                ins.then_inc(sm("x1_ready"), 1)
                dve.wait_ge(sm("x1_ready"), s + 1)
                normalise(wb, ST32, "b")

            def feed_2(s):
                dve.wait_ge(sm("hi_b"), s + 1)
                stt(ST16[:, :, 128:256], ST16[:, :, 0:128], -LO, T4[:, 0:2, :], ALU.mult, ALU.add)\
                    .then_inc(sm("r1_ready"), 1)
                wb.end()

            def l0b(s, par, k):
                nxt = None if last(s) else (1, s + 1, 1 - par, k if par == 0 else k + 1)
                if first(s):
                    masks(*nxt, range(CH))
                    return
                feed_1(s - 1)
                if nxt:
                    masks(*nxt, range(0, 1))
                normalise_2(s - 1, "b")
                if nxt:
                    masks(*nxt, range(1, CH))
                feed_2(s - 1)

            ring(dve, l0b)
            feed_1(S - 1)
            normalise_2(S - 1, "b")
            feed_2(S - 1)

            def copy_strip(phase, s, par):
                if not (isinstance(s, int) and s < 2):
                    dve.wait_ge(sm("prod_" + phase), 2 * (s - 1))
                at = AT[:, bass.ds(s * SB, SB)].bitcast(mybir.dt.uint16)
                dve.tensor_copy(GH16[:, par, 0, :], at).then_inc(sm("copy_" + phase), 1)

            dve.wait_ge(sm("prod_b"), 2 * S)
            copy_strip("1", 0, 0)
            for b in range(2):
                dve.wait_ge(sm("w8_ps"), b + 1)
                dve.tensor_copy(W8T[:, 4 * b:4 * b + 4, :], ps[6 + b][:].rearrange("p (b d) -> p b d", d=D))\
                    .then_inc(sm("w8t_ready"), 1)
            w1s = Steps(dve, sm("v_1"))
            dve.wait_ge(sm("x1_stored"), 16 * S)
            dve.wait_ge(sm("rows3_in"), 48)
            two = lambda r: r.unsqueeze(1).broadcast_to([128, 2, D])

            def prune(s):
                w1s.begin(s)
                dve.wait_ge(sm("ev_1"), s * 2 + 2)
                if not first(s):
                    dve.wait_ge(sm("r2_ready"), s)
                combine(w1s, s, EV5, "ev_free_1")
                w1s.do(stt(WA[:], T4[:, 0:4:2, :], col(CG), two(BG), ALU.mult, ALU.add))
                dve.wait_ge(sm("xin_1"), s * 16 + 16)
                if not first(s):
                    dve.wait_ge(sm("xb_stored"), s * 16)
                stt(ST32[:], WA[:], 0.0, XIN[:, 0, :, :], ALU.max, ALU.add).then_inc(sm("xb_ready"), 1)
                dve.wait_ge(sm("xb_ready"), s + 1)
                if not first(s):
                    dve.wait_ge(sm("ay_stored"), s * 16)
                ts(WB[:], T4[:, 1:4:2, :], col(CSY), None, ALU.mult).then_inc(sm("ay_ready"), 1)
                normalise(w1s, ST32, "1")
                normalise_2(s, "1")
                dve.wait_ge(sm("hi_1"), s + 1)
                stt(ST16[:, :, 128:256], ST16[:, :, 0:128], -LO, T4[:, 2:4, :], ALU.mult, ALU.add)\
                    .then_inc(sm("r2_ready"), 1)
                w1s.end()

            def l1(s, par, k):
                if not last(s):
                    copy_strip("1", s + 1, 1 - par)
                if not first(s):
                    prune(s - 1)

            ring(dve, l1)
            prune(S - 1)

            dve.wait_ge(sm("prod_1"), 2 * S)
            copy_strip("2", 0, 0)
            w2s = Steps(dve, sm("v_2"))
            dve.wait_ge(sm("xb_stored"), 16 * S)

            def merge(s):
                w2s.begin(s)
                dve.wait_ge(sm("ev_2"), s * 2 + 2)
                combine(w2s, s, EV5, "ev_free_2")
                dve.wait_ge(sm("net_ps0"), s + 1)
                dve.tensor_copy(NETS[:, 0, :], ps[4][:]).then_inc(sm("net_sb0"), 1)
                dve.wait_ge(sm("xin_2"), s * 16 + 16)
                tt(WA[:], XIN[:, 0, :, :], two(BM), ALU.add).then_inc(sm("xin_free_2"), 1)
                dve.wait_ge(sm("xin_free_2"), s + 1)
                if not first(s):
                    dve.wait_ge(sm("xc_stored"), s * 16)
                dve.wait_ge(sm("net_ps4"), s + 1)
                tt(ST32[:], WA[:], ps[7][:, 0:SW].rearrange("p (i d) -> p i d", d=D), ALU.add).then_inc(sm("xc_ready"), 1)
                dve.wait_ge(sm("xc_ready"), s + 1)
                normalise(w2s, ST32, "2")
                normalise_2(s, "2")
                dve.wait_ge(sm("hb_2"), s + 1)
                w2s.do(tt(WA[:], WB[:], two(A1R), ALU.mult))
                w2s.do(red(F1[:, bass.ds(s * 2, 2)], WA[:], AX.X, ALU.add))
                w2s.end()

            def l2(s, par, k):
                if not last(s):
                    copy_strip("2", s + 1, 1 - par)
                if not first(s):
                    merge(s - 1)

            ring(dve, l2)
            merge(S - 1)

            dve.engine_nop().then_inc(sm("f1_done"), 1)
            xs = lambda k: XT[:, k, :]
            v.do(ts(xs(0), F1[:], col(MX3), None, ALU.add))
            v.do(stt(xs(1), xs(0), LEAK, xs(0), ALU.mult, ALU.max))
            v.did(tt(xs(2), xs(0), xs(1), ALU.subtract))
            v.did(stt(xs(3), xs(0), LEAK, xs(1), ALU.mult, ALU.subtract))
            v.sync()
            dve.wait_ge(sm("f1_ps"), 2)
            dve.tensor_copy(FT, ps[7][0:T, 0:D]).then_inc(sm("f1t_made"), 1)
            dve.engine_nop().then_inc(sm("u3_wanted"), 1)
            dve.wait_ge(sm("u3_made"), 1)
            factors(xs(4), xs(5))
            v.sync()
            dve.wait_ge(sm("prod_2"), 2 * S)
            masks(2, 0, 0, 0, range(CH))
            w3 = Steps(dve, sm("v_3"))
            dve.wait_ge(sm("xc_stored"), 16 * S)

            def attend(s):
                w3.begin(s)
                dve.wait_ge(sm("ev_3"), s * 2 + 2)
                dq, rd = softmax_sums(w3, s, 1)
                w3.do(tt(SM[:, 48:50], EVq[:, 0:4:2, 262], EVq[:, 1:4:2, 262], ALU.add))
                w3.did(dve.tensor_copy(DEG[:, bass.ds(s * 2, 2)], SM[:, 48:50]))
                w3.do(stt(SM[:, 50:52], SM[:, 48:50], col(CSY), rd, ALU.mult, ALU.mult))
                w3.do(tt(RTC[:, :, 0:2], CUR[:, :, 0:4:2], BCAST(SM[:, 50:52], 2), ALU.mult))
                combine(w3, s, EVq, "ev_free_3")
                dve.wait_ge(sm("xin_3"), s * 32 + 32)
                tt(WA[:], XIN[:, 0, :, :], XIN[:, 1, :, :], ALU.add).then_inc(sm("xin_free_3"), 1)
                dve.wait_ge(sm("xin_free_3"), s + 1)
                for it in range(2):
                    w3.did(stt(WA[:, it, :], T4[:, 2 * it, :], RTC[:, it, 0:1], WA[:, it, :], ALU.mult, ALU.add))
                w3.sync()
                if not first(s):
                    dve.wait_ge(sm("out_stored"), s * 16)
                for it in range(2):
                    ins = stt(ST32[:, it, :], T4[:, 2 * it + 1, :], RTC[:, it, 1:2], WA[:, it, :], ALU.mult, ALU.add)
                ins.then_inc(sm("out_ready"), 1)
                w3.end()

            def l3(s, par, k):
                nxt = None if last(s) else (2, s + 1, 1 - par, k if par == 0 else k + 1)
                if not first(s):
                    attend(s - 1)
                if nxt:
                    masks(*nxt, range(CH))

            ring(dve, l3)
            attend(S - 1)

        @block.scalar
        def _(act):
            A = act.activation
            ap = Steps(act, sm("a_pro"))
            act.wait_ge(sm("w_in"), 16 * NW)
            act.wait_ge(sm("consts_made"), 1)
            ap.did(A(COL[:, E5:E5 + 5], COL[:, C0:C0 + 5], ACT.Exp, scale=-1.0))
            ap.do(A(col(TG), col(ONE), ACT.Tanh))
            act.wait_ge(sm("exps_wanted"), 1)
            A(LT[:, 14:20, :], LT[:, 8:14, :], ACT.Exp).then_inc(sm("exps_made"), 1)
            for j, hi in enumerate((R3[:, :, 0:128], R3[:, :, RH:RH + 128], P16[6][:, :, 0:128], P16[7][:, :, 0:128],
                                    P16[2][:, :, 0:128], P16[3][:, :, 0:128])):
                act.wait_ge(sm("scaled_made"), j + 1)
                if j == 3:
                    act.wait_ge(sm("h_stored"), 16)
                A(hi, PT, ACT.Copy).then_inc(sm("hi_made"), 1)

            def keep_transposed(s, r):
                if isinstance(s, int) and s == 2 and r == 0:
                    for name, n in (("h_stored", 16), ("r3_stored", 64), ("r2x_stored", 16), ("r1y_stored", 16)):
                        act.wait_ge(sm(name), n)
                act.wait_ge(sm("rows_used"), s * 16 + (2 * r + 2))
                cp, it = r // 2, r % 2
                dst = AT[:, bass.ds(s * SB, SB)].rearrange("p (j i) -> p j i", i=SW)[:, 8 * cp:8 * cp + 8, it * D:(it + 1) * D]
                A(dst, ps[r % 2][:].bitcast(BF16).rearrange("p (j i) -> p j i", i=D), ACT.Copy, scale=float(FP8_ONE))\
                    .then_inc(sm("at_ready"), 1)

            def evacuate(phase, s, it, banks, width):
                act.wait_ge(sm("prod_" + phase), s * 2 + (it + 1))
                if it == 0 and not first(s):
                    act.wait_ge(sm("ev_free_" + phase), s)
                elif it == 0 and phase != "a":
                    act.wait_ge(sm("ev_free_" + {"b": "a", "1": "b", "2": "1", "3": "2"}[phase]), S)
                for n, b in enumerate(banks):
                    ins = A(EV[:, (it * len(banks) + n) * width:(it * len(banks) + n + 1) * width], ps[b][:, 0:width], ACT.Copy)
                ins.then_inc(sm("ev_" + phase), 1)

            for r in range(8):
                keep_transposed(0, r)

            def split_feat(s):
                act.wait_ge(sm("feat_ready"), s + 1)
                if not first(s):
                    act.wait_ge(sm("rb_stored"), s * 16)
                for it in range(2):
                    for g in range(2):
                        A(ST16[:, it, g * RH:g * RH + D], ST32[:, it, :], ACT.Copy, scale=CUR[:, it, 4 + g:5 + g])
                        ins = A(T4[:, 2 * it + g, :], ST32[:, it, :], ACT.Copy, scale=CUR[:, it, 6 + g:7 + g])
                ins.then_inc(sm("hi_a"), 1)

            def l0a(s, par, k):
                if not first(s):
                    evacuate("a", s - 1, 1, (4, 5), RH)
                if not last(s):
                    for r in range(4):
                        keep_transposed(s + 1, r)
                if not first(s):
                    split_feat(s - 1)
                evacuate("a", s, 0, (2, 3), RH)
                if not last(s):
                    for r in range(4, 8):
                        keep_transposed(s + 1, r)

            ring(act, l0a)
            evacuate("a", S - 1, 1, (4, 5), RH)
            split_feat(S - 1)

            ab = Steps(act, sm("a_b"))

            def project(s):
                ab.begin(s)
                act.wait_ge(sm("norm_b"), s + 1)
                for it in range(2):
                    ins = A(WB[:, it, :], ST32[:, it, :], ACT.Relu, bias=MV[:, it, 4:5], scale=MV[:, it, 3:4])
                ins.then_inc(sm("hb_b"), 1)
                act.wait_ge(sm("ht_ps"), s + 1)
                A(HT, ps[0][:, 0:SW], ACT.Copy).then_inc(sm("ht_sb"), 1)
                act.wait_ge(sm("pj_ps"), s + 1)
                A(H2T, ps[1][:, 0:SW], ACT.Tanh, bias=col(BP)).then_inc(sm("h2_sb"), 1)
                act.wait_ge(sm("g_ps"), s + 1)
                ab.do(A(WB[:], ps[6][:, 0:SW].rearrange("p (i d) -> p i d", d=D), ACT.Copy, scale=col(SG)))
                if not first(s):
                    act.wait_ge(sm("r1_stored"), s * 16)
                A(ST16[:, :, 0:D], WB[:], ACT.Copy)
                A(T4[:, 0:2, :], WB[:], ACT.Copy, scale=LO).then_inc(sm("hi_b"), 1)
                ab.end()

            act.wait_ge(sm("rb_stored"), 16 * S)

            def l0b(s, par, k):
                if not first(s):
                    evacuate("b", s - 1, 1, (4, 5), RH)
                    project(s - 1)
                evacuate("b", s, 0, (2, 3), RH)

            ring(act, l0b)
            evacuate("b", S - 1, 1, (4, 5), RH)
            project(S - 1)
            act.wait_ge(sm("r1_stored"), 16 * S)

            a1s = Steps(act, sm("a_1"))

            def split_1(s):
                a1s.begin(s)
                act.wait_ge(sm("norm_1"), s + 1)
                for it in range(2):
                    a1s.did(A(T4[:, it, :], ST32[:, it, :], ACT.Relu, bias=MV[:, it, 4:5], scale=MV[:, it, 3:4]))
                a1s.sync()
                if not first(s):
                    act.wait_ge(sm("r2_stored"), s * 16)
                A(ST16[:, :, 0:D], T4[:, 0:2, :], ACT.Copy, scale=HS)
                A(T4[:, 2:4, :], T4[:, 0:2, :], ACT.Copy, scale=HS * LO).then_inc(sm("hi_1"), 1)
                a1s.end()

            def l1(s, par, k):
                if not first(s):
                    evacuate("1", s - 1, 1, (2 * (1 - par) + 1,), 512)
                    split_1(s - 1)
                evacuate("1", s, 0, (2 * par,), 512)

            ring(act, l1)
            evacuate("1", S - 1, 1, (3,), 512)
            split_1(S - 1)

            act.wait_ge(sm("ay_stored"), 16 * S)

            def nets(s):
                for l in range(3):
                    act.wait_ge(sm(f"net_ps{l + 1}"), s + 1)
                    for j in range(2):
                        ins = A(NETS[:, l + 1, j * SW:(j + 1) * SW], ps[5 + l % 2][:, j * SW:(j + 1) * SW], ACT.Relu,
                          bias=col(B6 + 3 * j + l), scale=(col(AX1 + j) if l == 0 else 1.0))
                    ins.then_inc(sm(f"net_sb{l + 1}"), 1)
                act.wait_ge(sm("norm_2"), s + 1)
                for it in range(2):
                    ins = A(WB[:, it, :], ST32[:, it, :], ACT.Relu, bias=MV[:, it, 4:5], scale=MV[:, it, 3:4])
                ins.then_inc(sm("hb_2"), 1)

            def l2(s, par, k):
                if not first(s):
                    evacuate("2", s - 1, 1, (2 * (1 - par) + 1,), 512)
                    nets(s - 1)
                evacuate("2", s, 0, (2 * par,), 512)

            ring(act, l2)
            evacuate("2", S - 1, 1, (3,), 512)
            nets(S - 1)

            act.wait_ge(sm("u3_wanted"), 1)
            A(XT[:, 4:6, :], XT[:, 2:4, :], ACT.Exp).then_inc(sm("u3_made"), 1)

            def l3(s, par, k):
                if not first(s):
                    evacuate("3", s - 1, 1, (4, 5), RH)
                evacuate("3", s, 0, (2, 3), RH)

            ring(act, l3)
            evacuate("3", S - 1, 1, (4, 5), RH)

        @block.tensor
        def _(pe):
            def transpose_pair(s, r):
                cp, it = r // 2, r % 2
                if not (isinstance(s, int) and s == 0 and r < 2):
                    pe.wait_ge(sm("at_ready"), s * 8 + (r - 1))
                for cc in range(2):
                    q = cp * 4 + it * 2 + cc
                    pe.wait_ge(sm(f"rows_in{q % 4}"), s * 64 + 16 * (q // 4 + 1))
                    rows = STG[:, q % 4, :].bitcast(BF16).rearrange("p (c two) -> p c two", two=2)
                    for b in range(4):
                        o = (cc * 4 + b) * D
                        ins = pe.transpose(ps[r % 2][:].bitcast(BF16)[:, o:o + D], rows[:, b * D:(b + 1) * D, 1], IDB[:])
                    ins.then_inc(sm("rows_used"), 1)

            def gate(s, bank, fresh):
                if not isinstance(s, int):
                    pe.matmul(ps[bank][:, 511:512], IDB[:], IDB[:, 0:1], start=fresh, stop=True, skip_group_check=True)

            def two_halves(phase, q0, s, par, r_ready, hooks):
                for u in range(16):
                    if u in hooks:
                        hooks[u]()
                    it, c8 = u // 8, u % 8
                    if c8 == 0 and not first(s):
                        pe.wait_ge(sm("ev_" + phase), s * 2 + (it - 1))
                    if it == 0 and c8 % 2 == 0:
                        pe.wait_ge(sm("masks_ready"), (s + q0) * 4 + (c8 // 2 + 1))
                        if first(s):
                            r_ready(c8 // 2)
                    if c8 == 0 or (it == 0 and c8 % 2 == 0):
                        gate(s, 2 + 2 * it, c8 == 0)
                    for jb in range(4 * c8, 4 * c8 + 4):
                        for g in range(2):
                            b = 2 + 2 * it + g
                            o = jb * SW + it * D
                            ins = pe.matmul(ps[b][:, 0:RH], GHf[:, par, g, o:o + D], R3[:, jb, g * RH:(g + 1) * RH],
                                            start=jb == 0, stop=jb == T - 1, skip_group_check=True)
                    if c8 == 7:
                        ins.then_inc(sm("prod_" + phase), 1)

            pe.wait_ge(sm("consts_made"), 1)
            for r in range(2):
                transpose_pair(0, r)
            pe.wait_ge(sm("f1_done"), 1)
            pe.transpose(ps[7][0:T, 0:D], F1[:], IDF[:]).then_inc(sm("f1_ps"), 1)
            for r in range(2, 8):
                transpose_pair(0, r)

            def l0a(s, par, k):
                hooks = {} if last(s) else {2 * r: (lambda r=r: transpose_pair(s + 1, r)) for r in range(8)}
                two_halves("a", 0, s, par, lambda c: pe.wait_ge(sm("job_done"), 2), hooks)

            ring(pe, l0a)

            def norm_transposed(s):
                pe.wait_ge(sm("hb_b"), s + 1)
                for it in range(2):
                    ins = pe.transpose(ps[0][:, it * D:(it + 1) * D], WB[:, it, :], IDF[:])
                ins.then_inc(sm("ht_ps"), 1)

            def proj(s):
                pe.wait_ge(sm("ht_sb"), s + 1)
                pe.matmul(ps[1][:, 0:SW], WP[:], HT, start=True, stop=True).then_inc(sm("pj_ps"), 1)

            def gcn(s):
                pe.wait_ge(sm("h2_sb"), s + 1)
                for it in range(2):
                    ins = pe.matmul(ps[6][:, it * D:(it + 1) * D], H2T[:, it * D:(it + 1) * D], WG[:], start=True, stop=True)
                ins.then_inc(sm("g_ps"), 1)

            def l0b(s, par, k):
                hooks = {} if first(s) else {8: lambda: norm_transposed(s - 1), 10: lambda: proj(s - 1), 13: lambda: gcn(s - 1)}
                two_halves("b", S, s, par, lambda c: pe.wait_ge(sm(f"R_b{c}"), 16), hooks)

            ring(pe, l0b)
            norm_transposed(S - 1)
            proj(S - 1)
            gcn(S - 1)

            def one_half(phase, s, par, hooks):
                pe.wait_ge(sm("copy_" + phase), s + 1)
                for u in range(16):
                    if u in hooks:
                        hooks[u]()
                    it, c8 = u // 8, u % 8
                    if c8 == 0 and not (isinstance(s, int) and s < 2):
                        pe.wait_ge(sm("ev_" + phase), s * 2 + (it - 3))
                    if first(s) and it == 0 and c8 % 2 == 0:
                        pe.wait_ge(sm(f"R_{phase}{c8 // 2}"), 16)
                    if c8 == 0:
                        gate(s, 2 * par + it, True)
                    for jb in range(4 * c8, 4 * c8 + 4):
                        o = jb * SW + it * D
                        ins = pe.matmul(ps[2 * par + it][:], GHf[:, par, 0, o:o + D], R5[:, jb, :],
                                        start=jb == 0, stop=jb == T - 1)
                    if c8 == 7:
                        ins.then_inc(sm("prod_" + phase), 1)

            pe.wait_ge(sm("w8_in"), 16 * 8)
            pe.wait_ge(sm("hi_b"), S)
            for b in range(2):
                for j in range(4):
                    ins = pe.transpose(ps[6 + b][:, j * D:(j + 1) * D], W8[:, 4 * b + j, :], IDF[:])
                ins.then_inc(sm("w8_ps"), 1)
            ring(pe, lambda s, par, k: one_half("1", s, par, {}))

            pe.wait_ge(sm("w8t_ready"), 2)

            def net_in(s):
                pe.wait_ge(sm("ev_free_2"), s + 1)
                for j in range(2):
                    for it in range(2):
                        o = (2 * j + it) * D
                        ins = pe.transpose(ps[4][:, o:o + D], T4[:, 2 * it + j, :], IDF[:])
                ins.then_inc(sm("net_ps0"), 1)

            def net_layer(s, l):
                pe.wait_ge(sm(f"net_sb{l}"), s + 1)
                for j in range(2):
                    ins = pe.matmul(ps[5 + l % 2][:, j * SW:(j + 1) * SW], W8T[:, 3 * j + l, :],
                                    NETS[:, l, j * SW:(j + 1) * SW], start=True, stop=True)
                ins.then_inc(sm(f"net_ps{l + 1}"), 1)

            def net_out(s):
                pe.wait_ge(sm("net_sb3"), s + 1)
                if not first(s):
                    pe.wait_ge(sm("xc_ready"), s)
                for it in range(2):
                    for j in range(2):
                        o = j * SW + it * D
                        ins = pe.matmul(ps[7][:, it * D:(it + 1) * D], NETS[:, 3, o:o + D], W8T[:, 6 + j, :],
                                        start=j == 0, stop=j == 1)
                ins.then_inc(sm("net_ps4"), 1)

            def l2(s, par, k):
                hooks = {} if first(s) else {3: lambda: net_in(s - 1), 5: lambda: net_layer(s - 1, 0),
                                             8: lambda: net_layer(s - 1, 1), 10: lambda: net_layer(s - 1, 2),
                                             13: lambda: net_out(s - 1)}
                one_half("2", s, par, hooks)

            ring(pe, l2)
            net_in(S - 1)
            for l in range(3):
                net_layer(S - 1, l)
            net_out(S - 1)

            pe.wait_ge(sm("f1_done"), 2)
            pe.transpose(ps[7][0:T, 0:D], F1[:], IDF[:]).then_inc(sm("f1_ps"), 1)
            ring(pe, lambda s, par, k: two_halves("3", 2 * S, s, par, lambda c: pe.wait_ge(sm(f"R_3{c}"), 16), {}))


_INS = ["x", "adj", "L0_gnn_h0", "L0_gnn_a", "L0_gnn_temp", "L1_gnn_W_proj", "L1_gnn_b_proj", "L1_gnn_W_gcn",
        "L1_gnn_b_gcn", "L2_gnn_x2", "L2_gnn_eps1", "L2_gnn_eps2", "L2_gnn_W1", "L2_gnn_b1", "L2_gnn_W2", "L2_gnn_b2",
        "L2_gnn_Wm", "L2_gnn_bm", "L3_gnn_input2", "L3_gnn_a1", "L3_gnn_a2"]


def kernel(**inputs):
    import numpy as _np
    import concourse.bacc as _bacc
    from concourse import mybir as _mybir
    from concourse.bass_utils import run_bass_kernel_spmd as _run

    nc = _bacc.Bacc("TRN2", target_bir_lowering=False, num_devices=1, dynamic_dma_scratch_size=1024)
    arrays, args = {}, []
    for name in _INS:
        a = _np.ascontiguousarray(inputs[name])
        arrays[f"in_{name}_dram"] = a
        args.append(nc.dram_tensor(f"in_{name}_dram", a.shape, _mybir.dt.from_np(a.dtype), kind="ExternalInput").ap())
    out = nc.dram_tensor("out_0_dram", (N, D), _mybir.dt.float32, kind="ExternalOutput").ap()
    build(nc, *args, out)
    r = _run(nc, [arrays], core_ids=[0])
    return r.results[0]["out_0_dram"]
```

```python
import numpy as np
import concourse.bass as bass
from concourse import mybir
from concourse.alu_op_type import AluOpType as ALU

ACT = mybir.ActivationFunctionType
AX = mybir.AxisListType
F32, F16, BF16 = mybir.dt.float32, mybir.dt.float16, mybir.dt.bfloat16
I32, U8, FP8 = mybir.dt.int32, mybir.dt.uint8, mybir.dt.float8e4

N = 4096
D = 128
T = N // D
SW = 256
S = N // SW
SB = T * SW
RH = 264
RW = 2 * RH
CH = 4
CB = SB // CH
FP8_ONE = 0x38
EXP_BITS = 0x7F800000
LO = 4096.0
VS = 2.0 ** 15
HS = 2.0 ** 11
FS = 2.0 ** 10
TH = 1e-6
LEAK = 0.2
EPS = 1e-5
DENOM_FLOOR = 2.0 ** -40
TOPK = 350
MASK_FILL = 9e15
DENOM_MIN = 2.0 ** -22


SEMAPHORES = """
x_in vec_in y_in x2_in w_in rows_in0 rows_in1 rows_in2 rows_in3 rows_used h_made f1t_made job_done x16_made
h_stored f1_stored r3_stored r2x_stored r1y_stored f1_in0 f1_in1 masks_ready at_ready
consts_made stats_made var_made rstd_made maxima_made maxima_all exps_wanted exps_made scaled_made hi_made
prod_a ev_a ev_free_a xin_a feat_ready hi_a rb_ready feat_stored rb_stored R_b0 R_b1 R_b2 R_b3
prod_b ev_b ev_free_b xin_b xin_free_b x1_ready x1_stored r1_ready r1_stored var_b rstd_b norm_b hb_b ht_ps ht_sb pj_ps h2_sb g_ps hi_b
R_10 R_11 R_12 R_13 rows3_in w8_in w8_ps w8t_ready copy_1 prod_1 ev_1 ev_free_1 xin_1 xb_ready xb_stored ay_ready ay_stored
r2_ready r2_stored var_1 rstd_1 norm_1 hi_1
R_20 R_21 R_22 R_23 copy_2 prod_2 ev_2 ev_free_2 xin_2 xin_free_2 net_ps0 net_sb0 net_ps1 net_sb1 net_ps2 net_sb2 net_ps3 net_sb3 net_ps4
xc_ready xc_stored var_2 rstd_2 norm_2 hb_2 u3_wanted u3_made f1_done f1_ps f1b_stored
R_30 R_31 R_32 R_33 prod_3 ev_3 ev_free_3 xin_3 xin_free_3 out_ready out_stored
v_pro v_mask v_a v_b v_1 v_2 v_3 a_pro a_b a_1 g_pro
bad_rows bad_any flag_ready g_rows g_weights g_turned g_copied g_added g_ax g_x v_g v_tiles
"""


class Steps:

    def __init__(self, eng, sem, per=None, base=0):
        self.eng, self.sem, self.start, self.n, self.per, self.base = eng, sem, 0, 0, per, base

    def begin(self, strip):
        self.start = 0 if isinstance(strip, int) and strip == 0 else strip * self.per
        self.n = 0

    def end(self):
        if self.per is None:
            self.per = self.n
        assert self.per == self.n, (self.per, self.n)

    def did(self, ins):
        ins.then_inc(self.sem, 1)
        self.n += 1

    def sync(self):
        self.eng.wait_ge(self.sem, self.start + (self.base + self.n))

    def do(self, ins):
        self.did(ins)
        self.sync()


def build(nc, x, adj, h0, a0, temp, w_proj, b_proj, w_gcn, b_gcn, x2, eps1, eps2,
          w1, b1, w2, b2, wm, bm, y, a1, a2, out):
    from contextlib import ExitStack
    ctx = ExitStack()
    with ctx:
        def sb(name, shape, dt=F32):
            return ctx.enter_context(nc.sbuf_tensor(name, shape, dt))

        def sem(name):
            return ctx.enter_context(nc.semaphore(name))

        def dram(name, shape, dt=F32):
            return nc.dram_tensor(name, shape, dt)

        AT = sb("AT", [128, S * SB], U8)
        GH = sb("GH", [128, 2, 2, SB], U8)
        R = sb("R", [128, T * RW], F16)
        STG = sb("STG", [128, 4, 512])
        F1R = sb("F1R", [128, 2, SW])
        XIN = sb("XIN", [128, 3, 2, D])
        EV = sb("EV", [128, 2 * RW])
        T4 = sb("T4", [128, 4, D])
        WA = sb("WA", [128, 2, D])
        WB = sb("WB", [128, 2, D])
        ST16 = sb("ST16", [128, 2, RW], F16)
        ST32 = sb("ST32", [128, 2, D])
        WP = sb("WP", [128, D])
        WG = sb("WG", [128, D])
        IDF = sb("IDF", [128, D])
        IDB = sb("IDB", [128, D], BF16)
        TBL = sb("TBL", [128, S, 2, 8])
        CUR = sb("CUR", [128, 2, 8])
        RT = sb("RT", [128, S, 2, 4])
        RTC = sb("RTC", [128, 2, 4])
        DEN = sb("DEN", [128, 2, T])
        DEG = sb("DEG", [128, T])
        F1 = sb("F1", [128, T])
        F2N = sb("F2N", [128, 2, T])
        COL = sb("COL", [128, 48])
        SM = sb("SM", [128, 64])
        MV = sb("MV", [128, 2, 8])
        CO = sb("CO", [128, 6])
        FLG = sb("FLG", [128, 3])

        def col(i):
            return COL[:, i:i + 1]
        (MX0, MX3, AMY, AMX, AMG, SY, SX, SG, ISY, ISX, ISG, C0, C1, C2, C3, K2, BP, TG, KE1, KE2,
         NM0, NM3, BIAS0) = range(23)
        B6 = 24
        CSY, OMC2, E5, C1C0, AX1, AX2, ONE, MH, NC3, CG = 30, 31, 33, 40, 41, 42, 43, 44, 45, 46
        NW = 12

        GHf = GH[:].bitcast(FP8)
        GH16 = GH[:].bitcast(mybir.dt.uint16)
        GHI = GH[:].bitcast(I32)
        slots = AT[:].bitcast(F32).rearrange("p (k n) -> p k n", n=N)
        PX2, PY, PT, PU, PX, PH = (slots[:, k, :].rearrange("p (t d) -> p t d", d=D) for k in range(2, 8))
        P16 = {k: slots[:, k, :].bitcast(F16).rearrange("p (t c) -> p t c", c=256) for k in (2, 3, 6, 7)}
        A3 = slots[:, 1, 0:3 * D].rearrange("p (k d) -> p k d", d=D)
        LT = slots[:, 1, 512:512 + 24 * T].rearrange("p (k t) -> p k t", t=T)
        E16 = slots[:, 1, 2048:2048 + 6 * T].bitcast(F16).rearrange("p (q k t) -> p q k t", q=4, k=3)
        X16 = slots[:, 1, 3072:3072 + 8 * T].bitcast(F16).rearrange("p (t g e) -> p t g e", g=2, e=8)
        R3 = R[:].rearrange("p (t c) -> p t c", c=RW)
        R5 = R[:, 0:T * 512].rearrange("p (t c) -> p t c", c=512)
        W8 = STG[:, 0:2, :].rearrange("p a (b d) -> p (a b) d", d=D)
        W8T = STG[:, 2:4, :].rearrange("p a (b d) -> p (a b) d", d=D)
        HT = STG[:, 0, 0:SW]
        H2T = STG[:, 1, 0:SW]
        NETS = GH[:, 0, 1, :].bitcast(F32).rearrange("p (l n) -> p l n", n=512)
        ROWS = GH[:, 1, 1, 0:4 * 3 * D].bitcast(F32).rearrange("p (k d) -> p k d", d=D)
        BG, BM, A1R = ROWS[:, 0, :], ROWS[:, 1, :], ROWS[:, 2, :]
        FT = T4[0:T, 0, :]
        F1T = T4[:, 0, 0:T]
        XT = EV[:, 0:6 * T].rearrange("p (k t) -> p k t", t=T)
        EVq = EV[:].rearrange("p (q c) -> p q c", c=RH)
        EV5 = EV[:, 0:1024].rearrange("p (q c) -> p q c", c=256)
        ST16q = ST16[:].rearrange("p i (g c) -> p (i g) c", c=RH)
        TBLt = TBL[:].rearrange("p s i w -> p (s i) w")
        RTt = RT[:].rearrange("p s i w -> p (s i) w")

        ps = [ctx.enter_context(nc.psum_tensor(f"ps{b}", [128, 512], F32)) for b in range(8)]

        f1_d = [dram(f"f1_{k}", [T, D]) for k in range(2)]
        h_d, feat_d, x1_d, xb_d, xc_d, ay_d = (dram(n, [128, T, D]) for n in ("h_s", "feat_s", "x1_s", "xb_s", "xc_s", "ay_s"))
        rb_d = dram("rb_s", [128, T, RW], F16)
        r1_d = dram("r1_s", [128, T, 512], F16)
        r2_d = dram("r2_s", [128, T, 512], F16)
        r3_d = dram("r3_s", [128, T, RW], F16)
        tile_rows = lambda t: t.rearrange("(t p) d -> p t d", p=128)

        wide = [slots[:, k, :] for k in range(8)] + [GH[:].rearrange("p a b n -> p (a b n)").bitcast(F32)[:, N * k:N * k + N] for k in range(2)] \
            + [R[:].bitcast(F32)[:, N * k:N * k + N] for k in range(2)]
        QX, QH, QB, QA, QW, QS, QY, QX2, QF, QM, Q0, QC = wide
        nodes = lambda q: q.rearrange("p (t d) -> p t d", d=D)
        NX, NH, NB, NW_, NS, NY, NX2, N0 = (nodes(q) for q in (QX, QH, QB, QW, QS, QY, QX2, Q0))
        GT = R[:].bitcast(F32)[:, 2 * N:2 * N + 6 * T].rearrange("p (k t) -> p k t", t=T)
        GMEAN, GVAR, GRSTD, GF1, GF2, GRS = range(6)
        TURN = EV[:, 0:1024].rearrange("p (b n) -> p b n", n=512)
        GROWS = STG[:, 0:2, :].rearrange("p a (b d) -> p (a b) d", d=D)
        GNET = [XIN[:, 0, :, :], XIN[:, 1, :, :], XIN[:, 2, :, :], ST32[:]]
        GA1, BAD = 38, 47
        FLAG = FLG[0:1, 0:1].bitcast(I32)
        one = lambda q, t: q[:, bass.ds(t, 1), :].rearrange("p o d -> p (o d)")

        sems = {n: sem(n) for n in SEMAPHORES.split()}
        sm = sems.__getitem__

        block = ctx.enter_context(nc.Block())
        BCAST = lambda ap1, n=D: ap1.unsqueeze(2).broadcast_to([128, ap1.shape[1], n])

        def ring(eng, body):
            for s in (0, 1):
                body(s, s, 0)
            with eng.Fori(1, S // 2 - 1) as k:
                body(k * 2, 0, k)
                body(k * 2 + 1, 1, k)
            for s in (S - 2, S - 1):
                body(s, s % 2, S // 2 - 1)

        first = lambda s: isinstance(s, int) and s == 0
        last = lambda s: isinstance(s, int) and s == S - 1

        @block.sync
        def _(sp):
            ld = lambda dst, src, s: sp.dma_start(dst, src).then_inc(sm(s), 16)
            ld(PX, tile_rows(x), "x_in")
            a0c = a0.rearrange("(k d) o -> k (d o)", k=2)
            ld(A3[:, 0, :], a0c[0, :].partition_broadcast(128), "vec_in")
            ld(A3[:, 1, :], a0c[1, :].partition_broadcast(128), "vec_in")
            ld(A3[:, 2, :], a2.rearrange("d o -> (d o)").partition_broadcast(128), "vec_in")
            ld(PY, tile_rows(y), "y_in")
            ld(PX2, tile_rows(x2), "x2_in")
            ld(WP[:], w_proj, "w_in")
            ld(WG[:], w_gcn, "w_in")
            ld(COL[:, C0:C0 + 5], temp.partition_broadcast(128), "w_in")
            ld(COL[:, KE1:KE1 + 1], eps1.partition_broadcast(128), "w_in")
            ld(COL[:, KE2:KE2 + 1], eps2.partition_broadcast(128), "w_in")
            ld(col(BP), b_proj.rearrange("(d o) -> d o", o=1), "w_in")
            for j, b in enumerate((b1, b2)):
                for l in range(3):
                    ld(COL[:, B6 + 3 * j + l:B6 + 3 * j + l + 1], b[l, :].rearrange("(d o) -> d o", o=1), "w_in")

            def load_strip_rows(s, between, start=0, stop=16):
                n = 0
                for cp in range(4):
                    for it in range(2):
                        for c in (2 * cp, 2 * cp + 1):
                            q = cp * 4 + it * 2 + c % 2
                            if not start <= q < stop:
                                continue
                            if not (isinstance(s, int) and s * 16 + q < 4):
                                sp.wait_ge(sm("rows_used"), s * 16 + (q - 3))
                            ld(STG[:, q % 4, :], adj[bass.ds(s * SW + it * 128, 128), c * 512:(c + 1) * 512],
                               f"rows_in{q % 4}")
                            if n in between:
                                between[n]()
                            n += 1

            load_strip_rows(0, {}, 0, 4)
            sp.wait_ge(sm("h_made"), 1)
            ld(h_d[:, :, :], PH, "h_stored")
            sp.wait_ge(sm("f1t_made"), 1)
            ld(f1_d[0][:, :], FT, "f1_stored")
            sp.wait_ge(sm("job_done"), 4)
            ld(r3_d[:, :, 0:256], P16[6], "r3_stored")
            ld(r3_d[:, :, RH:RH + 256], P16[7], "r3_stored")
            sp.wait_ge(sm("x16_made"), 1)
            ld(r3_d[:, :, 256:RH], X16[:, :, 0, :], "r3_stored")
            ld(r3_d[:, :, RH + 256:RW], X16[:, :, 1, :], "r3_stored")
            sp.wait_ge(sm("job_done"), 5)
            ld(r2_d[:, :, 256:512], P16[2], "r2x_stored")
            sp.wait_ge(sm("job_done"), 6)
            ld(r1_d[:, :, 256:512], P16[3], "r1y_stored")
            load_strip_rows(0, {}, 4, 16)
            sp.wait_ge(sm("h_stored"), 16)
            sp.wait_ge(sm("f1_stored"), 16)
            f1row = lambda k: f1_d[k].rearrange("t p -> (t p)")

            def load_f1(k, s, par, g):
                if g is not None:
                    sp.wait_ge(sm("masks_ready"), g)
                ld(F1R[:, par, :], f1row(k)[bass.ds(s * SW, SW)].partition_broadcast(128), f"f1_in{par}")

            load_f1(0, 0, 0, None)
            load_f1(0, 1, 1, None)

            def l0a(s, par, k):
                def early():
                    load_f1(0, (s + 2) if not (isinstance(s, int) and s >= S - 2) else s + 2 - S, par, 4 * (s + 1))

                def late():
                    if not first(s):
                        store_a(s - 1)
                        sp.wait_ge(sm("feat_ready"), s)
                    ld(XIN[:, 0, :, :], h_d[:, bass.ds(s * 2, 2), :], "xin_a")

                if last(s):
                    early(), late()
                else:
                    load_strip_rows(s + 1, {7: early, 11: late})

            def store_a(s):
                sp.wait_ge(sm("feat_ready"), s + 1)
                ld(feat_d[:, bass.ds(s * 2, 2), :], ST32[:], "feat_stored")
                sp.wait_ge(sm("rb_ready"), s + 1)
                ld(rb_d[:, bass.ds(s * 2, 2), :], ST16[:], "rb_stored")

            ring(sp, l0a)
            store_a(S - 1)

            def load_R(src, width, stored, count, used, usedn, name):
                sp.wait_ge(sm(stored), count)
                sp.wait_ge(sm(used), usedn)
                dst = R[:, 0:T * width].rearrange("p (t c) -> p t c", c=width)
                for c in range(4):
                    ld(dst[:, 8 * c:8 * c + 8, :], src[:, 8 * c:8 * c + 8, :], name + str(c))

            load_R(rb_d, RW, "rb_stored", 16 * S, "prod_a", 2 * S, "R_b")
            sp.wait_ge(sm("feat_stored"), 16 * S)

            xt = tile_rows(x)
            h0t = tile_rows(h0)

            def l0b(s, par, k):
                if not first(s):
                    sp.wait_ge(sm("xin_free_b"), s)
                ld(XIN[:, 0, :, :], xt[:, bass.ds(s * 2, 2), :], "xin_b")
                ld(XIN[:, 1, :, :], feat_d[:, bass.ds(s * 2, 2), :], "xin_b")
                ld(XIN[:, 2, :, :], h0t[:, bass.ds(s * 2, 2), :], "xin_b")
                if not (isinstance(s, int) and s >= S - 2):
                    load_f1(0, s + 2, par, 4 * S + 4 * (s + 1))
                if not first(s):
                    store_b(s - 1)

            def store_b(s):
                sp.wait_ge(sm("x1_ready"), s + 1)
                ld(x1_d[:, bass.ds(s * 2, 2), :], ST32[:], "x1_stored")
                sp.wait_ge(sm("r1_ready"), s + 1)
                ld(r1_d[:, bass.ds(s * 2, 2), 0:256], ST16[:, :, 0:256], "r1_stored")

            ring(sp, l0b)
            store_b(S - 1)
            sp.wait_ge(sm("r1y_stored"), 16)
            load_R(r1_d, 512, "r1_stored", 16 * S, "prod_b", 2 * S, "R_1")
            sp.wait_ge(sm("x1_stored"), 16 * S)

            for k, v in enumerate((b_gcn, bm, a1.rearrange("d o -> (d o)"))):
                ld(ROWS[:, k, :], v.partition_broadcast(128), "rows3_in")
            for j, w in enumerate((w1, w2)):
                for l in range(3):
                    ld(W8[:, 3 * j + l, :], w[l, :, :], "w8_in")
            for j in range(2):
                ld(W8[:, 6 + j, :], wm[:, j * D:(j + 1) * D], "w8_in")

            def l1(s, par, k):
                if not first(s):
                    sp.wait_ge(sm("xb_ready"), s)
                ld(XIN[:, 0, :, :], x1_d[:, bass.ds(s * 2, 2), :], "xin_1")
                if not first(s):
                    store_1(s - 1)

            def store_1(s):
                sp.wait_ge(sm("xb_ready"), s + 1)
                ld(xb_d[:, bass.ds(s * 2, 2), :], ST32[:], "xb_stored")
                sp.wait_ge(sm("ay_ready"), s + 1)
                ld(ay_d[:, bass.ds(s * 2, 2), :], WB[:], "ay_stored")
                sp.wait_ge(sm("r2_ready"), s + 1)
                ld(r2_d[:, bass.ds(s * 2, 2), 0:256], ST16[:, :, 0:256], "r2_stored")

            ring(sp, l1)
            store_1(S - 1)
            sp.wait_ge(sm("r2x_stored"), 16)
            load_R(r2_d, 512, "r2_stored", 16 * S, "prod_1", 2 * S, "R_2")
            sp.wait_ge(sm("xb_stored"), 16 * S)
            sp.wait_ge(sm("ay_stored"), 16 * S)

            def l2(s, par, k):
                if not first(s):
                    sp.wait_ge(sm("xin_free_2"), s)
                ld(XIN[:, 0, :, :], xb_d[:, bass.ds(s * 2, 2), :], "xin_2")
                if not first(s):
                    store_2(s - 1)

            def store_2(s):
                sp.wait_ge(sm("xc_ready"), s + 1)
                ld(xc_d[:, bass.ds(s * 2, 2), :], ST32[:], "xc_stored")

            ring(sp, l2)
            store_2(S - 1)
            sp.wait_ge(sm("r3_stored"), 16)
            load_R(r3_d, RW, "r3_stored", 64, "prod_2", 2 * S, "R_3")
            sp.wait_ge(sm("xc_stored"), 16 * S)
            sp.wait_ge(sm("f1t_made"), 2)
            ld(f1_d[1][:, :], FT, "f1b_stored")
            sp.wait_ge(sm("f1b_stored"), 16)

            load_f1(1, 0, 0, None)
            load_f1(1, 1, 1, None)

            def l3(s, par, k):
                if not first(s):
                    sp.wait_ge(sm("xin_free_3"), s)
                ld(XIN[:, 0, :, :], xc_d[:, bass.ds(s * 2, 2), :], "xin_3")
                ld(XIN[:, 1, :, :], ay_d[:, bass.ds(s * 2, 2), :], "xin_3")
                if not (isinstance(s, int) and s >= S - 2):
                    load_f1(1, s + 2, par, 8 * S + 4 * (s + 1))
                if not first(s):
                    store_3(s - 1)

            ot = tile_rows(out)

            def store_3(s):
                sp.wait_ge(sm("out_ready"), s + 1)
                ld(ot[:, bass.ds(s * 2, 2), :], ST32[:], "out_stored")

            ring(sp, l3)
            store_3(S - 1)
            sp.wait_ge(sm("out_stored"), 16 * S)

            def general():
                for dst, src in ((NX, x), (NY, y), (NX2, x2), (N0, h0)):
                    ld(dst, tile_rows(src), "x_in")
                for k, src in enumerate((a0c[0, :], a0c[1, :], a1.rearrange("d o -> (d o)"), a2.rearrange("d o -> (d o)"),
                                         b_gcn, bm)):
                    ld(GROWS[:, k, :], src.partition_broadcast(128), "vec_in")

                def f2_row(k):
                    sp.wait_ge(sm("f1t_made"), k + 1 + 2)
                    ld(f1_d[k][:, :], FT, "f1b_stored")
                    sp.wait_ge(sm("f1b_stored"), 16 * (k + 1) + 16)
                    ld(QF, f1row(k).partition_broadcast(128), "f1_in0")

                def rows(a):
                    with sp.Fori(0, T) as t:
                        sp.wait_ge(sm("g_weights"), t + (a * T + 1))
                        ld(QA, adj[bass.ds(t * D, D), :], "g_rows")

                f2_row(0)
                for a in range(4):
                    rows(a)
                f2_row(1)
                rows(4)
                sp.wait_ge(sm("g_x"), 1)
                ld(tile_rows(out), NX, "out_stored")
                sp.wait_ge(sm("out_stored"), 16 + 16 * S)

            sp.wait_ge(sm("flag_ready"), 1)
            flag = sp.value_load(FLAG)
            with sp.If(flag > 0):
                general()

        @block.gpsimd
        def _(pool):
            g = Steps(pool, sm("g_pro"))
            g.did(pool.memset(IDF[:], 0.0))
            g.did(pool.memset(IDB[:], 0.0))
            g.sync()
            for m in (IDF, IDB):
                g.did(pool.affine_select(out=m[:], in_=m[:], compare_op=ALU.not_equal, fill=1.0, base=0,
                                         pattern=[[-1, D]], channel_multiplier=1))
            for k in range(3):
                for q in range(2):
                    g.did(pool.memset(CO[:, 3 * q + k:3 * q + k + 1], 1.0 / VS / LO ** k))
            g.did(pool.memset(LT[:, 0, :], -0.5))
            g.did(pool.memset(COL[:, ONE:ONE + 1], 1.0))
            g.did(pool.memset(ST16[:], 0.0))
            g.did(pool.memset(COL[:, MH:MH + 1], -0.5))
            for w in (0, RH):
                g.did(pool.memset(R3[:, :, w + 262:w + 263], 1.0))
                g.did(pool.memset(R3[:, :, w + 263:w + 264], 0.0))
            g.did(pool.memset(X16[:, :, :, 6:7], 1.0))
            g.did(pool.memset(X16[:, :, :, 7:8], 0.0))
            g.sync()
            pool.nop().then_inc(sm("consts_made"), 1)
            pool.wait_ge(sm("var_made"), 1)
            pool.tensor_tensor(LT[:, 2, :], LT[:, 1, :], LT[:, 0, :], ALU.pow).then_inc(sm("rstd_made"), 1)
            pool.wait_ge(sm("maxima_made"), 1)
            pool.partition_all_reduce(COL[:, 0:5], SM[:, 0:5], 128, bass.bass_isa.ReduceOp.max).then_inc(sm("maxima_all"), 1)

            def rstd(phase):
                def body(s, par, k):
                    pool.wait_ge(sm("var_" + phase), s + 1)
                    pool.tensor_tensor(MV[:, :, 3], MV[:, :, 2], col(MH).broadcast_to([128, 2]),
                                       ALU.pow).then_inc(sm("rstd_" + phase), 1)
                with pool.Fori(0, S) as s:
                    body(s, 0, 0)

            rstd("b")
            rstd("1")
            rstd("2")

            pool.wait_ge(sm("bad_rows"), 1)
            pool.partition_all_reduce(col(BAD), SM[:, 2:3], 128, bass.bass_isa.ReduceOp.max).then_inc(sm("bad_any"), 1)

            pool.wait_ge(sm("flag_ready"), 1)
            flag = pool.value_load(FLAG)
            with pool.If(flag > 0):
                for n in range(4):
                    pool.wait_ge(sm("var_b"), n + 1 + S)
                    pool.tensor_tensor(GT[:, GRSTD, :], GT[:, GVAR, :], col(MH).broadcast_to([128, T]),
                                       ALU.pow).then_inc(sm("rstd_b"), 1)

        @block.vector
        def _(dve):
            v = Steps(dve, sm("v_pro"))
            ts, tt, stt, red = dve.tensor_scalar, dve.tensor_tensor, dve.scalar_tensor_tensor, dve.tensor_reduce
            lt = lambda k: LT[:, k, :]
            dve.wait_ge(sm("consts_made"), 1)
            dve.wait_ge(sm("x_in"), 16)
            v.do(red(lt(3), PX, AX.X, ALU.add))
            v.do(ts(lt(3), lt(3), 1.0 / D, None, ALU.mult))
            v.do(tt(PT, PX, BCAST(lt(3)), ALU.subtract))
            v.do(tt(PU, PT, PT, ALU.mult))
            v.do(red(lt(1), PU, AX.X, ALU.add))
            ts(lt(1), lt(1), 1.0 / D, EPS, ALU.mult, ALU.add).then_inc(sm("var_made"), 1)
            dve.wait_ge(sm("rstd_made"), 1)
            stt(PH, PT, 0.0, BCAST(lt(2)), ALU.max, ALU.mult).then_inc(sm("h_made"), 1)
            dve.wait_ge(sm("h_made"), 1)
            vec = lambda k: A3[:, k, :].unsqueeze(1).broadcast_to([128, T, D])
            dve.wait_ge(sm("vec_in"), 48)
            v.do(tt(PU, PH, vec(0), ALU.mult))
            red(F1[:], PU, AX.X, ALU.add).then_inc(sm("f1_done"), 1)
            dve.wait_ge(sm("f1_done"), 1)
            v.do(tt(PU, PH, vec(1), ALU.mult))
            v.do(red(lt(4), PU, AX.X, ALU.add))
            dve.wait_ge(sm("y_in"), 16)
            v.do(tt(PU, PY, vec(2), ALU.mult))
            v.do(red(lt(5), PU, AX.X, ALU.add))
            dve.wait_ge(sm("x2_in"), 16)
            dve.wait_ge(sm("w_in"), 16 * NW)
            v.did(red(SM[:, 0:1], lt(4), AX.X, ALU.max))
            v.did(red(SM[:, 1:2], lt(5), AX.X, ALU.max))
            v.did(red(SM[:, 2:3], PY, AX.XY, ALU.max, apply_absolute_value=True))
            v.did(red(SM[:, 3:4], PX2, AX.XY, ALU.max, apply_absolute_value=True))
            v.do(red(SM[:, 4:5], WG[:], AX.X, ALU.max, apply_absolute_value=True))
            v.do(ts(SM[:, 4:5], SM[:, 4:5], float(D), None, ALU.mult))
            dve.engine_nop().then_inc(sm("maxima_made"), 1)
            dve.wait_ge(sm("f1_ps"), 1)
            dve.tensor_copy(FT, ps[7][0:T, 0:D]).then_inc(sm("f1t_made"), 1)
            dve.wait_ge(sm("maxima_all"), 1)
            v.do(ts(SM[:, 8:11], COL[:, AMY:AMG + 1], 1e-30, None, ALU.max))
            v.do(ts(SM[:, 8:11].bitcast(I32), SM[:, 8:11].bitcast(I32), EXP_BITS, None, ALU.bitwise_and))
            v.did(ts(COL[:, ISY:ISY + 3], SM[:, 8:11], 1.0 / 8192, None, ALU.mult))
            v.do(dve.reciprocal(SM[:, 12:15], SM[:, 8:11]))
            v.did(ts(COL[:, SY:SY + 3], SM[:, 12:15], 8192.0, None, ALU.mult))
            v.did(ts(COL[:, NM0:NM0 + 2], COL[:, MX0:MX0 + 2], -1.0, None, ALU.mult))
            v.sync()
            v.do(ts(lt(6), F1[:], col(MX0), None, ALU.add))
            v.do(stt(lt(7), lt(6), LEAK, lt(6), ALU.mult, ALU.max))
            v.did(tt(lt(8), lt(6), lt(7), ALU.subtract))
            v.did(stt(lt(9), lt(6), LEAK, lt(7), ALU.mult, ALU.subtract))
            v.did(ts(lt(10), lt(4), col(MX0), None, ALU.subtract))
            v.did(ts(lt(11), lt(4), col(MX0), LEAK, ALU.subtract, ALU.mult))
            v.did(ts(lt(12), lt(5), col(MX3), None, ALU.subtract))
            v.did(ts(lt(13), lt(5), col(MX3), LEAK, ALU.subtract, ALU.mult))
            v.did(ts(F2N[:, 0, :], lt(4), -1.0, None, ALU.mult))
            v.did(ts(F2N[:, 1, :], lt(5), -1.0, None, ALU.mult))
            v.sync()
            dve.engine_nop().then_inc(sm("exps_wanted"), 1)
            dve.wait_ge(sm("exps_made"), 1)

            def factors(u, up):
                v.did(dve.tensor_copy(TBLt[:, :, 0], u))
                v.did(tt(TBLt[:, :, 1], u, u, ALU.mult))
                v.did(dve.tensor_copy(TBLt[:, :, 2], up))
                v.did(tt(TBLt[:, :, 3], up, up, ALU.mult))

            factors(lt(14), lt(15))
            for k, c in ((4, FS), (6, FS * LO)):
                v.did(ts(TBLt[:, :, k], lt(16), c, None, ALU.mult))
                v.did(ts(TBLt[:, :, k + 1], lt(17), c, None, ALU.mult))

            def extras(va, vb, dst):
                VV, RR = LT[:, 20:24, :], slots[:, 1, 3584:3584 + 4 * T].rearrange("p (k t) -> p k t", t=T)
                v.sync()
                v.did(ts(lt(20), va, VS, None, ALU.mult))
                v.did(ts(lt(22), vb, VS, None, ALU.mult))
                v.did(stt(lt(21), va, VS, va, ALU.mult, ALU.mult))
                v.do(stt(lt(23), vb, VS, vb, ALU.mult, ALU.mult))
                for part in range(3):
                    v.do(dve.tensor_copy(E16[:, :, part, :], VV))
                    if part < 2:
                        v.do(tt(RR, VV, E16[:, :, part, :], ALU.subtract))
                        v.do(ts(VV, RR, LO, None, ALU.mult))
                for q in range(4):
                    v.did(dve.tensor_copy(dst(q), E16[:, q, :, :].rearrange("p k t -> p t k")))
                v.sync()

            extras(lt(16), lt(17), lambda q: R3[:, :, RH * (q // 2) + 256 + 3 * (q % 2):RH * (q // 2) + 259 + 3 * (q % 2)])
            v.did(ts(lt(16), lt(16), HS, None, ALU.mult))
            v.did(ts(lt(17), lt(17), HS, None, ALU.mult))
            extras(lt(18), lt(19), lambda q: X16[:, :, q // 2, 3 * (q % 2):3 * (q % 2) + 3])
            dve.engine_nop().then_inc(sm("x16_made"), 1)
            v.did(ts(lt(18), lt(18), col(SY), None, ALU.mult))
            v.did(ts(lt(19), lt(19), col(SY), None, ALU.mult))
            c = lambda k: col(C0 + k)
            v.do(ts(COL[:, E5:E5 + 5], COL[:, E5:E5 + 5], 1.0, None, ALU.add))
            v.do(dve.reciprocal(COL[:, C0:C0 + 5], COL[:, E5:E5 + 5]))
            v.did(ts(SM[:, 16:20], COL[:, C0:C0 + 4], -1.0, 1.0, ALU.mult, ALU.add))
            v.sync()
            v.did(dve.tensor_copy(col(OMC2), SM[:, 18:19]))
            v.did(tt(col(K2), SM[:, 17:18], SM[:, 16:17], ALU.mult))
            v.did(tt(col(C1C0), SM[:, 17:18], c(0), ALU.mult))
            v.did(ts(col(NC3), c(3), -1.0, None, ALU.mult))
            v.did(tt(col(CG), col(TG), col(ISG), ALU.mult))
            v.did(ts(col(CSY), col(ISY), 0.5, None, ALU.mult))
            v.did(ts(col(AX1), col(KE1), 2.0, 1.0 / HS, ALU.add, ALU.mult))
            v.did(stt(col(AX2), col(KE2), 2.0, col(ISX), ALU.add, ALU.mult))
            v.sync()
            jobs = [(PH, lt(16), R3[:, :, 0:128], R3[:, :, 128:256]),
                    (PH, lt(17), R3[:, :, RH:RH + 128], R3[:, :, RH + 128:RH + 256]),
                    (PY, lt(18), P16[6][:, :, 0:128], P16[6][:, :, 128:256]),
                    (PY, lt(19), P16[7][:, :, 0:128], P16[7][:, :, 128:256]),
                    (PX2, col(SX), P16[2][:, :, 0:128], P16[2][:, :, 128:256]),
                    (PY, col(SY), P16[3][:, :, 0:128], P16[3][:, :, 128:256])]
            for j, (src, scale, hi, lo) in enumerate(jobs):
                if j < 4:
                    tt(PT, src, BCAST(scale), ALU.mult).then_inc(sm("scaled_made"), 1)
                else:
                    ts(PT, src, scale, None, ALU.mult).then_inc(sm("scaled_made"), 1)
                dve.wait_ge(sm("scaled_made"), j + 1)
                v.did(ts(PU, PT, LO, None, ALU.mult))
                dve.wait_ge(sm("hi_made"), j + 1)
                v.sync()
                stt(lo, hi, -LO, PU, ALU.mult, ALU.add).then_inc(sm("job_done"), 1)
                dve.wait_ge(sm("job_done"), j + 1)

            m = Steps(dve, sm("v_mask"))

            def masks(layer, s, par, k, chunks):
                q = s + layer * S
                mk = F2N[:, 0 if layer < 2 else 1, :]
                for ch in chunks:
                    if ch == 0:
                        dve.wait_ge(sm(f"f1_in{par}"), (k + layer * (S // 2) + 1) * 16)
                        if layer == 0 and not (isinstance(s, int) and s < 2):
                            dve.wait_ge(sm("prod_a"), 2 * (s - 1))
                        if layer == 1 and isinstance(s, int) and s < 2:
                            dve.wait_ge(sm("prod_a"), 2 * (S + s - 1))
                        elif layer == 1:
                            dve.wait_ge(sm("prod_b"), 2 * (s - 1))
                        if layer == 2 and not (isinstance(s, int) and s < 2):
                            dve.wait_ge(sm("prod_3"), 2 * (s - 1))
                    if layer == 0:
                        dve.wait_ge(sm("at_ready"), s * 8 + (2 * ch + 2))
                    for jb in range(8 * ch, 8 * ch + 8):
                        ins = ts(GH[:, par, 0, jb * SW:(jb + 1) * SW], F1R[:, par, :], mk[:, jb:jb + 1],
                                 float(FP8_ONE), ALU.is_gt, ALU.mult)
                    ins.then_inc(sm("v_mask"), 1)
                    if ch > 0:
                        mask_edges(q, s, par, ch - 1, (1, 2, 4)[ch - 1], (3, 5, 7)[ch - 1])
                if CH - 1 in chunks:
                    mask_edges(q, s, par, CH - 1, 6, 8)

            def mask_edges(q, s, par, ch, compared, anded):
                at = AT[:, bass.ds(s * SB + ch * CB, CB)].bitcast(I32)
                g0, g1 = (GHI[:, par, g, ch * (CB // 4):(ch + 1) * (CB // 4)] for g in range(2))
                dve.wait_ge(sm("v_mask"), q * 8 + compared)
                tt(g0, g0, at, ALU.bitwise_and).then_inc(sm("v_mask"), 1)
                dve.wait_ge(sm("v_mask"), q * 8 + anded)
                tt(g1, g0, at, ALU.bitwise_xor).then_inc(sm("masks_ready"), 1)

            def softmax_sums(w, s, layer):
                w.do(dve.tensor_copy(CUR[:], TBL[:, bass.ds(s, 1), :, :].rearrange("p o i w -> p (o i) w")))
                w.do(tt(SM[:, 0:24].rearrange("p (q k) -> p q k", k=6), EVq[:, :, 256:262],
                        CO[:].unsqueeze(1).broadcast_to([128, 4, 6]), ALU.mult))
                w.do(red(SM[:, 24:32], SM[:, 0:24].rearrange("p (q k) -> p q k", k=3), AX.X, ALU.add))
                w.do(tt(SM[:, 32:40].rearrange("p (i w) -> p i w", i=2), SM[:, 24:32].rearrange("p (i w) -> p i w", i=2),
                        CUR[:, :, 0:4], ALU.mult))
                four = SM[:, 32:40].rearrange("p (i g w) -> p i g w", i=2, g=2)
                dq = SM[:, 40:44].rearrange("p (i w) -> p i w", i=2)
                w.do(tt(dq, four[:, :, 0, :], four[:, :, 1, :], ALU.add))
                w.did(dve.tensor_copy(DEN[:, layer, bass.ds(s * 2, 2)], dq[:, :, 0]))
                w.do(ts(SM[:, 44:46], dq[:, :, 0], DENOM_FLOOR, None, ALU.max))
                w.do(dve.reciprocal(SM[:, 44:46], SM[:, 44:46]))
                return dq, SM[:, 44:46]

            def combine(w, s, ev, name):
                stt(T4[:], ev[:, :, 128:256], 1.0 / LO, ev[:, :, 0:128], ALU.mult, ALU.add).then_inc(sm(name), 1)
                w.sync()
                dve.wait_ge(sm(name), s + 1)

            wa = Steps(dve, sm("v_a"))

            def filter_1(s):
                wa.begin(s)
                dve.wait_ge(sm("ev_a"), s * 2 + 2)
                dq, rd = softmax_sums(wa, s, 0)
                wa.do(tt(SM[:, 46:48], dq[:, :, 1], rd, ALU.mult))
                wa.do(stt(RTC[:, :, 2], SM[:, 46:48], 0.5, rd, ALU.mult, ALU.mult))
                wa.did(stt(RTC[:, :, 0:2], CUR[:, :, 0:4:2], 1.0 / HS, BCAST(rd, 2), ALU.mult, ALU.mult))
                wa.do(ts(RTC[:, :, 3], RTC[:, :, 2], -1.0, col(OMC2), ALU.mult, ALU.add))
                wa.did(dve.tensor_copy(RT[:, bass.ds(s, 1), :, :].rearrange("p o i w -> p (o i) w"), RTC[:]))
                combine(wa, s, EVq, "ev_free_a")
                dve.wait_ge(sm("xin_a"), s * 16 + 16)
                for it in range(2):
                    wa.did(ts(WA[:, it, :], T4[:, 2 * it + 1, :], RTC[:, it, 1:2], None, ALU.mult))
                wa.sync()
                for it in range(2):
                    wa.did(stt(WA[:, it, :], T4[:, 2 * it, :], RTC[:, it, 0:1], WA[:, it, :], ALU.mult, ALU.add))
                wa.sync()
                for it in range(2):
                    wa.did(stt(WA[:, it, :], XIN[:, 0, it, :], RTC[:, it, 3:4], WA[:, it, :], ALU.mult, ALU.add))
                wa.sync()
                wa.do(ts(WB[:], WA[:], TH, -TH, ALU.min, ALU.max))
                if not first(s):
                    dve.wait_ge(sm("feat_stored"), s * 16)
                tt(ST32[:], WA[:], WB[:], ALU.subtract).then_inc(sm("feat_ready"), 1)

            def filter_2(s):
                dve.wait_ge(sm("hi_a"), s + 1)
                stt(ST16q[:, :, 128:256], ST16q[:, :, 0:128], -LO, T4[:], ALU.mult, ALU.add).then_inc(sm("rb_ready"), 1)
                wa.end()

            masks(0, 0, 0, 0, range(CH))

            def l0a(s, par, k):
                if first(s):
                    masks(0, 1, 1, 0, range(CH))
                    return
                filter_1(s - 1)
                nxt = (1, 0, 0, 0) if last(s) else (0, s + 1, 1 - par, k if par == 0 else k + 1)
                masks(*nxt, range(0, 1))
                filter_2(s - 1)
                masks(*nxt, range(1, CH))

            ring(dve, l0a)
            filter_1(S - 1)
            filter_2(S - 1)

            t0 = RTt[:, :, 2]
            v.did(ts(t0, t0, c(1), col(C1C0), ALU.mult, ALU.add))
            dve.wait_ge(sm("rb_ready"), S)
            v.sync()
            v.do(ts(F1T, t0, col(NC3), c(1), ALU.mult, ALU.add))
            for i in range(2):
                v.did(stt(RTt[:, :, i], RTt[:, :, i], HS / FS, F1T, ALU.mult, ALU.mult))
            v.sync()
            wb = Steps(dve, sm("v_b"))
            dve.wait_ge(sm("feat_stored"), 16 * S)

            def normalise(w, src, phase):
                for it in range(2):
                    w.did(dve.bn_stats(SM[:, 48 + 6 * it:54 + 6 * it], src[:, it, :]))
                w.sync()
                dve.memset(MV[:, :, 5:6], 0.0)
                for it in range(2):
                    w.did(dve.bn_aggr(MV[:, it, 0:2], SM[:, 48 + 6 * it:54 + 6 * it]))
                w.sync()
                ts(MV[:, :, 2], MV[:, :, 1], EPS, None, ALU.add).then_inc(sm("var_" + phase), 1)

            def normalise_2(s, phase):
                dve.wait_ge(sm("rstd_" + phase), s + 1)
                stt(MV[:, :, 4], MV[:, :, 0], -1.0, MV[:, :, 3], ALU.mult, ALU.mult).then_inc(sm("norm_" + phase), 1)

            def feed_1(s):
                wb.begin(s)
                wb.do(dve.tensor_copy(RTC[:], RT[:, bass.ds(s, 1), :, :].rearrange("p o i w -> p (o i) w")))
                dve.wait_ge(sm("ev_b"), s * 2 + 2)
                if not first(s):
                    dve.wait_ge(sm("r1_ready"), s)
                combine(wb, s, EVq, "ev_free_b")
                dve.wait_ge(sm("xin_b"), s * 48 + 48)
                wb.do(stt(WA[:], XIN[:, 2, :, :], col(K2), XIN[:, 0, :, :], ALU.mult, ALU.add))
                for it in range(2):
                    ins = stt(WA[:, it, :], XIN[:, 1, it, :], RTC[:, it, 2:3], WA[:, it, :], ALU.mult, ALU.add)
                ins.then_inc(sm("xin_free_b"), 1)
                dve.wait_ge(sm("xin_free_b"), s + 1)
                for it in range(2):
                    wb.did(stt(WA[:, it, :], T4[:, 2 * it, :], RTC[:, it, 0:1], WA[:, it, :], ALU.mult, ALU.add))
                wb.sync()
                if not first(s):
                    dve.wait_ge(sm("x1_stored"), s * 16)
                for it in range(2):
                    ins = stt(ST32[:, it, :], T4[:, 2 * it + 1, :], RTC[:, it, 1:2], WA[:, it, :], ALU.mult, ALU.add)
                ins.then_inc(sm("x1_ready"), 1)
                dve.wait_ge(sm("x1_ready"), s + 1)
                normalise(wb, ST32, "b")

            def feed_2(s):
                dve.wait_ge(sm("hi_b"), s + 1)
                stt(ST16[:, :, 128:256], ST16[:, :, 0:128], -LO, T4[:, 0:2, :], ALU.mult, ALU.add)\
                    .then_inc(sm("r1_ready"), 1)
                wb.end()

            def l0b(s, par, k):
                nxt = None if last(s) else (1, s + 1, 1 - par, k if par == 0 else k + 1)
                if first(s):
                    masks(*nxt, range(CH))
                    return
                feed_1(s - 1)
                if nxt:
                    masks(*nxt, range(0, 1))
                normalise_2(s - 1, "b")
                if nxt:
                    masks(*nxt, range(1, CH))
                feed_2(s - 1)

            ring(dve, l0b)
            feed_1(S - 1)
            normalise_2(S - 1, "b")
            feed_2(S - 1)

            def copy_strip(phase, s, par):
                if not (isinstance(s, int) and s < 2):
                    dve.wait_ge(sm("prod_" + phase), 2 * (s - 1))
                at = AT[:, bass.ds(s * SB, SB)].bitcast(mybir.dt.uint16)
                dve.tensor_copy(GH16[:, par, 0, :], at).then_inc(sm("copy_" + phase), 1)

            dve.wait_ge(sm("prod_b"), 2 * S)
            copy_strip("1", 0, 0)
            for b in range(2):
                dve.wait_ge(sm("w8_ps"), b + 1)
                dve.tensor_copy(W8T[:, 4 * b:4 * b + 4, :], ps[6 + b][:].rearrange("p (b d) -> p b d", d=D))\
                    .then_inc(sm("w8t_ready"), 1)
            w1s = Steps(dve, sm("v_1"))
            dve.wait_ge(sm("x1_stored"), 16 * S)
            dve.wait_ge(sm("rows3_in"), 48)
            two = lambda r: r.unsqueeze(1).broadcast_to([128, 2, D])

            def prune(s):
                w1s.begin(s)
                dve.wait_ge(sm("ev_1"), s * 2 + 2)
                if not first(s):
                    dve.wait_ge(sm("r2_ready"), s)
                combine(w1s, s, EV5, "ev_free_1")
                w1s.do(stt(WA[:], T4[:, 0:4:2, :], col(CG), two(BG), ALU.mult, ALU.add))
                dve.wait_ge(sm("xin_1"), s * 16 + 16)
                if not first(s):
                    dve.wait_ge(sm("xb_stored"), s * 16)
                stt(ST32[:], WA[:], 0.0, XIN[:, 0, :, :], ALU.max, ALU.add).then_inc(sm("xb_ready"), 1)
                dve.wait_ge(sm("xb_ready"), s + 1)
                if not first(s):
                    dve.wait_ge(sm("ay_stored"), s * 16)
                ts(WB[:], T4[:, 1:4:2, :], col(CSY), None, ALU.mult).then_inc(sm("ay_ready"), 1)
                normalise(w1s, ST32, "1")
                normalise_2(s, "1")
                dve.wait_ge(sm("hi_1"), s + 1)
                stt(ST16[:, :, 128:256], ST16[:, :, 0:128], -LO, T4[:, 2:4, :], ALU.mult, ALU.add)\
                    .then_inc(sm("r2_ready"), 1)
                w1s.end()

            def l1(s, par, k):
                if not last(s):
                    copy_strip("1", s + 1, 1 - par)
                if not first(s):
                    prune(s - 1)

            ring(dve, l1)
            prune(S - 1)

            dve.wait_ge(sm("prod_1"), 2 * S)
            copy_strip("2", 0, 0)
            w2s = Steps(dve, sm("v_2"))
            dve.wait_ge(sm("xb_stored"), 16 * S)

            def merge(s):
                w2s.begin(s)
                dve.wait_ge(sm("ev_2"), s * 2 + 2)
                combine(w2s, s, EV5, "ev_free_2")
                dve.wait_ge(sm("net_ps0"), s + 1)
                dve.tensor_copy(NETS[:, 0, :], ps[4][:]).then_inc(sm("net_sb0"), 1)
                dve.wait_ge(sm("xin_2"), s * 16 + 16)
                tt(WA[:], XIN[:, 0, :, :], two(BM), ALU.add).then_inc(sm("xin_free_2"), 1)
                dve.wait_ge(sm("xin_free_2"), s + 1)
                if not first(s):
                    dve.wait_ge(sm("xc_stored"), s * 16)
                dve.wait_ge(sm("net_ps4"), s + 1)
                tt(ST32[:], WA[:], ps[7][:, 0:SW].rearrange("p (i d) -> p i d", d=D), ALU.add).then_inc(sm("xc_ready"), 1)
                dve.wait_ge(sm("xc_ready"), s + 1)
                normalise(w2s, ST32, "2")
                normalise_2(s, "2")
                dve.wait_ge(sm("hb_2"), s + 1)
                w2s.do(tt(WA[:], WB[:], two(A1R), ALU.mult))
                w2s.do(red(F1[:, bass.ds(s * 2, 2)], WA[:], AX.X, ALU.add))
                w2s.end()

            def l2(s, par, k):
                if not last(s):
                    copy_strip("2", s + 1, 1 - par)
                if not first(s):
                    merge(s - 1)

            ring(dve, l2)
            merge(S - 1)

            dve.engine_nop().then_inc(sm("f1_done"), 1)
            xs = lambda k: XT[:, k, :]
            v.do(ts(xs(0), F1[:], col(MX3), None, ALU.add))
            v.do(stt(xs(1), xs(0), LEAK, xs(0), ALU.mult, ALU.max))
            v.did(tt(xs(2), xs(0), xs(1), ALU.subtract))
            v.did(stt(xs(3), xs(0), LEAK, xs(1), ALU.mult, ALU.subtract))
            v.sync()
            dve.wait_ge(sm("f1_ps"), 2)
            dve.tensor_copy(FT, ps[7][0:T, 0:D]).then_inc(sm("f1t_made"), 1)
            dve.engine_nop().then_inc(sm("u3_wanted"), 1)
            dve.wait_ge(sm("u3_made"), 1)
            factors(xs(4), xs(5))
            v.sync()
            dve.wait_ge(sm("prod_2"), 2 * S)
            masks(2, 0, 0, 0, range(CH))
            w3 = Steps(dve, sm("v_3"))
            dve.wait_ge(sm("xc_stored"), 16 * S)

            def attend(s):
                w3.begin(s)
                dve.wait_ge(sm("ev_3"), s * 2 + 2)
                dq, rd = softmax_sums(w3, s, 1)
                w3.do(tt(SM[:, 48:50], EVq[:, 0:4:2, 262], EVq[:, 1:4:2, 262], ALU.add))
                w3.did(dve.tensor_copy(DEG[:, bass.ds(s * 2, 2)], SM[:, 48:50]))
                w3.do(stt(SM[:, 50:52], SM[:, 48:50], col(CSY), rd, ALU.mult, ALU.mult))
                w3.do(tt(RTC[:, :, 0:2], CUR[:, :, 0:4:2], BCAST(SM[:, 50:52], 2), ALU.mult))
                combine(w3, s, EVq, "ev_free_3")
                dve.wait_ge(sm("xin_3"), s * 32 + 32)
                tt(WA[:], XIN[:, 0, :, :], XIN[:, 1, :, :], ALU.add).then_inc(sm("xin_free_3"), 1)
                dve.wait_ge(sm("xin_free_3"), s + 1)
                for it in range(2):
                    w3.did(stt(WA[:, it, :], T4[:, 2 * it, :], RTC[:, it, 0:1], WA[:, it, :], ALU.mult, ALU.add))
                w3.sync()
                if not first(s):
                    dve.wait_ge(sm("out_stored"), s * 16)
                for it in range(2):
                    ins = stt(ST32[:, it, :], T4[:, 2 * it + 1, :], RTC[:, it, 1:2], WA[:, it, :], ALU.mult, ALU.add)
                ins.then_inc(sm("out_ready"), 1)
                w3.end()

            def l3(s, par, k):
                nxt = None if last(s) else (2, s + 1, 1 - par, k if par == 0 else k + 1)
                if not first(s):
                    attend(s - 1)
                if nxt:
                    masks(*nxt, range(CH))

            ring(dve, l3)
            attend(S - 1)

            f = Steps(dve, sm("v_g"))
            w3.sync()
            for layer in range(2):
                f.do(ts(SM[:, 0:T], DEN[:, layer, :], DENOM_MIN, None, ALU.is_ge))
                f.do(red(FLG[:, 1 + layer:2 + layer], SM[:, 0:T], AX.X, ALU.min))
            f.do(ts(SM[:, 0:T], DEG[:], float(TOPK), None, ALU.is_le))
            f.do(red(SM[:, T:T + 1], SM[:, 0:T], AX.X, ALU.min))
            f.do(tt(SM[:, T:T + 1], SM[:, T:T + 1], FLG[:, 1:2], ALU.min))
            f.do(tt(SM[:, T:T + 1], SM[:, T:T + 1], FLG[:, 2:3], ALU.min))
            ts(SM[:, 2:3], SM[:, T:T + 1], -1.0, 1.0, ALU.mult, ALU.add).then_inc(sm("bad_rows"), 1)
            dve.wait_ge(sm("bad_any"), 1)
            dve.tensor_copy(FLG[:, 0:1].bitcast(I32), col(BAD)).then_inc(sm("flag_ready"), 1)

            def general():
                q = f
                steps = (21, 21, 1, 31, 5, 17)
                loop = lambda n: Steps(dve, sm("v_tiles"), steps[n], T * sum(steps[:n]))
                gt = lambda k: GT[:, k, :]
                same = lambda dst, src: ts(dst, src, 1.0, None, ALU.mult)

                def layer_norm(n):
                    q.do(red(gt(GMEAN), NX, AX.X, ALU.add))
                    q.do(ts(gt(GMEAN), gt(GMEAN), 1.0 / D, None, ALU.mult))
                    q.do(tt(NS, NX, BCAST(gt(GMEAN)), ALU.subtract))
                    q.do(tt(NW_, NS, NS, ALU.mult))
                    q.do(red(gt(GVAR), NW_, AX.X, ALU.add))
                    ts(gt(GVAR), gt(GVAR), 1.0 / D, EPS, ALU.mult, ALU.add).then_inc(sm("var_b"), 1)
                    dve.wait_ge(sm("rstd_b"), n + 1 + S)
                    q.do(stt(NH, NS, 0.0, BCAST(gt(GRSTD)), ALU.max, ALU.mult))

                def scores(n, src1, k1, src2, k2):
                    row = lambda k: GROWS[:, k, :].unsqueeze(1).broadcast_to([128, T, D])
                    q.do(tt(NS, src1, row(k1), ALU.mult))
                    q.do(red(gt(GF1), NS, AX.X, ALU.add))
                    q.do(tt(NS, src2, row(k2), ALU.mult))
                    red(gt(GF2), NS, AX.X, ALU.add).then_inc(sm("f1_done"), 1)
                    dve.wait_ge(sm("f1_ps"), n + 1 + 2)
                    dve.tensor_copy(FT, ps[7][0:T, 0:D]).then_inc(sm("f1t_made"), 1)
                    dve.wait_ge(sm("f1_in0"), 16 * (n + 1) + 24 * S)

                def softmax_tile(w, t, a, e):
                    w.do(same(SM[:, 0:1], GT[:, GF1, bass.ds(t, 1)]))
                    dve.wait_ge(sm("g_rows"), (t + a * T + 1) * 16)
                    w.do(ts(QW, QF, SM[:, 0:1], None, ALU.add))
                    w.do(stt(QW, QW, LEAK, QW, ALU.mult, ALU.max))
                    w.do(ts(QM, QA, 0.0, None, ALU.is_gt))
                    w.do(tt(QW, QW, QM, ALU.mult))
                    w.do(ts(QM, QM, 1.0, MASK_FILL, ALU.subtract, ALU.mult))
                    w.do(tt(QW, QW, QM, ALU.add))
                    w.do(red(SM[:, 1:2], QW, AX.X, ALU.max))
                    ts(QW, QW, SM[:, 1:2], -200.0, ALU.subtract, ALU.max).then_inc(sm("exps_wanted"), 1)
                    dve.wait_ge(sm("exps_made"), t + (e * T + 1) + 1)
                    w.do(red(SM[:, 2:3], QS, AX.X, ALU.add))
                    w.do(dve.reciprocal(SM[:, 3:4], SM[:, 2:3]))
                    w.do(ts(QW, QS, SM[:, 3:4], None, ALU.mult))

                def aggregate(w, t, a):
                    w.sync()
                    dve.memset(FLG[:, 2:3], 0.0).then_inc(sm("g_weights"), 1)
                    for b in range(8):
                        dve.wait_ge(sm("g_turned"), (t + a * T) * 8 + (b + 1))
                        dve.wait_ge(sm("g_added"), (t + a * T) * 8 + (1 + max(b - 1, 0)))
                        dve.tensor_copy(TURN[:, b % 2, :], ps[b % 2][:]).then_inc(sm("g_copied"), 1)
                    dve.wait_ge(sm("g_added"), (t + a * T) * 8 + 9)

                for free in ("g_weights", "g_copied", "g_added"):
                    dve.engine_nop().then_inc(sm(free), 1)
                dve.wait_ge(sm("x_in"), 64 + 16)
                dve.wait_ge(sm("vec_in"), 96 + 48)
                layer_norm(0)
                scores(0, NH, 0, NH, 1)
                w0 = loop(0)
                with dve.Fori(0, T) as t:
                    w0.begin(t)
                    softmax_tile(w0, t, 0, 0)
                    w0.do(tt(QS, QW, QW, ALU.mult))
                    w0.do(red(SM[:, 4:5], QS, AX.X, ALU.add))
                    w0.do(ts(SM[:, 5:6], SM[:, 4:5], 0.5, None, ALU.mult))
                    w0.do(same(GT[:, GRS, bass.ds(t, 1)], SM[:, 5:6]))
                    w0.do(ts(SM[:, 6:7], SM[:, 5:6], -1.0, col(OMC2), ALU.mult, ALU.add))
                    w0.do(same(WA[:, 0, :], one(NH, t)))
                    aggregate(w0, t, 0)
                    w0.do(stt(WA[:, 1, :], WA[:, 0, :], SM[:, 6:7], ps[2][:, 0:D], ALU.mult, ALU.add))
                    w0.do(ts(WB[:, 0, :], WA[:, 1, :], TH, -TH, ALU.min, ALU.max))
                    w0.do(tt(WA[:, 0, :], WA[:, 1, :], WB[:, 0, :], ALU.subtract))
                    w0.do(same(one(NB, t), WA[:, 0, :]))
                    w0.end()
                w1_ = loop(1)
                with dve.Fori(0, T) as t:
                    w1_.begin(t)
                    softmax_tile(w1_, t, 1, 1)
                    w1_.do(same(SM[:, 4:5], GT[:, GRS, bass.ds(t, 1)]))
                    w1_.do(ts(SM[:, 5:6], SM[:, 4:5], c(1), col(C1C0), ALU.mult, ALU.add))
                    w1_.do(same(WA[:, 0, :], one(NB, t)))
                    w1_.do(same(WB[:, 0, :], one(N0, t)))
                    w1_.do(same(WB[:, 1, :], one(NX, t)))
                    w1_.do(stt(WB[:, 0, :], WB[:, 0, :], col(K2), WB[:, 1, :], ALU.mult, ALU.add))
                    aggregate(w1_, t, 1)
                    w1_.do(stt(WA[:, 0, :], ps[2][:, 0:D], col(NC3), WA[:, 0, :], ALU.mult, ALU.add))
                    w1_.do(stt(WB[:, 0, :], WA[:, 0, :], SM[:, 5:6], WB[:, 0, :], ALU.mult, ALU.add))
                    w1_.do(stt(WB[:, 0, :], ps[2][:, 0:D], c(1), WB[:, 0, :], ALU.mult, ALU.add))
                    w1_.do(same(one(NX, t), WB[:, 0, :]))
                    w1_.end()
                layer_norm(1)
                w2_ = loop(2)
                with dve.Fori(0, T) as t:
                    w2_.begin(t)
                    same(WB[:, 0, :], one(NH, t)).then_inc(sm("hb_b"), 1)
                    dve.wait_ge(sm("ht_ps"), t + 1 + S)
                    dve.tensor_copy(WA[:, 0, :], ps[4][:, 0:D]).then_inc(sm("ht_sb"), 1)
                    dve.wait_ge(sm("g_ps"), t + 1 + S)
                    w2_.do(same(one(NB, t), ps[6][:, 0:D]))
                    w2_.end()
                w3_ = loop(3)
                with dve.Fori(0, T) as t:
                    w3_.begin(t)
                    w3_.do(same(WB[:, 0, :], one(NX, t)))
                    dve.wait_ge(sm("g_rows"), (t + 2 * T + 1) * 16)
                    w3_.do(ts(QM, QA, 0.0, None, ALU.is_gt))
                    src = QM
                    for k in range(12):
                        dst, sh = (QS, QC)[k % 2], 2 ** k
                        w3_.did(dve.tensor_copy(dst[:, 0:sh], src[:, 0:sh]))
                        w3_.do(tt(dst[:, sh:N], src[:, sh:N], src[:, 0:N - sh], ALU.add))
                        src = dst
                    w3_.do(stt(QW, src, float(TOPK), QM, ALU.is_le, ALU.mult))
                    w3_.do(ts(QW, QW, col(TG), None, ALU.mult))
                    aggregate(w3_, t, 2)
                    w3_.do(tt(WA[:, 0, :], ps[2][:, 0:D], GROWS[:, 4, :], ALU.add))
                    w3_.do(stt(WB[:, 0, :], WA[:, 0, :], 0.0, WB[:, 0, :], ALU.max, ALU.add))
                    w3_.do(same(one(NX, t), WB[:, 0, :]))
                    w3_.end()
                layer_norm(2)
                q.do(ts(COL[:, GA1:GA1 + 2], COL[:, KE1:KE1 + 2], 2.0, None, ALU.add))
                w4_ = loop(4)
                with dve.Fori(0, T) as t:
                    w4_.begin(t)
                    w4_.do(same(WA[:, 0, :], one(NX, t)))
                    dve.wait_ge(sm("g_rows"), (t + 3 * T + 1) * 16)
                    w4_.do(dve.tensor_copy(QW, QA))
                    aggregate(w4_, t, 3)
                    for j in range(2):
                        ins = ts(WB[:, j, :], ps[2 + j][:, 0:D], col(GA1 + j), None, ALU.mult)
                    ins.then_inc(sm("g_ax"), 1)
                    dve.wait_ge(sm("net_ps0"), t + 1 + S)
                    dve.tensor_copy(GNET[0], ps[4][:, 0:SW].rearrange("p (i d) -> p i d", d=D)).then_inc(sm("net_sb0"), 1)
                    dve.wait_ge(sm("net_ps4"), t + 1 + S)
                    w4_.do(tt(WA[:, 1, :], ps[7][:, 0:D], GROWS[:, 5, :], ALU.add))
                    w4_.do(tt(WA[:, 0, :], WA[:, 0, :], WA[:, 1, :], ALU.add))
                    w4_.do(same(one(NX, t), WA[:, 0, :]))
                    w4_.end()
                layer_norm(3)
                scores(1, NH, 2, NY, 3)
                w5_ = loop(5)
                with dve.Fori(0, T) as t:
                    w5_.begin(t)
                    softmax_tile(w5_, t, 4, 2)
                    w5_.do(red(SM[:, 4:5], QA, AX.X, ALU.add))
                    w5_.do(ts(QW, QW, SM[:, 4:5], 0.5, ALU.mult, ALU.mult))
                    w5_.do(stt(QW, QA, 0.5, QW, ALU.mult, ALU.add))
                    w5_.do(same(WA[:, 0, :], one(NX, t)))
                    aggregate(w5_, t, 4)
                    w5_.do(tt(WA[:, 0, :], WA[:, 0, :], ps[2][:, 0:D], ALU.add))
                    w5_.do(same(one(NX, t), WA[:, 0, :]))
                    w5_.end()
                dve.engine_nop().then_inc(sm("g_x"), 1)

            dve.wait_ge(sm("flag_ready"), 1)
            flag = dve.value_load(FLAG)
            with dve.If(flag > 0):
                general()

        @block.scalar
        def _(act):
            A = act.activation
            ap = Steps(act, sm("a_pro"))
            act.wait_ge(sm("w_in"), 16 * NW)
            act.wait_ge(sm("consts_made"), 1)
            ap.did(A(COL[:, E5:E5 + 5], COL[:, C0:C0 + 5], ACT.Exp, scale=-1.0))
            ap.do(A(col(TG), col(ONE), ACT.Tanh))
            act.wait_ge(sm("exps_wanted"), 1)
            A(LT[:, 14:20, :], LT[:, 8:14, :], ACT.Exp).then_inc(sm("exps_made"), 1)
            for j, hi in enumerate((R3[:, :, 0:128], R3[:, :, RH:RH + 128], P16[6][:, :, 0:128], P16[7][:, :, 0:128],
                                    P16[2][:, :, 0:128], P16[3][:, :, 0:128])):
                act.wait_ge(sm("scaled_made"), j + 1)
                if j == 3:
                    act.wait_ge(sm("h_stored"), 16)
                A(hi, PT, ACT.Copy).then_inc(sm("hi_made"), 1)

            def keep_transposed(s, r):
                if isinstance(s, int) and s == 2 and r == 0:
                    for name, n in (("h_stored", 16), ("r3_stored", 64), ("r2x_stored", 16), ("r1y_stored", 16)):
                        act.wait_ge(sm(name), n)
                act.wait_ge(sm("rows_used"), s * 16 + (2 * r + 2))
                cp, it = r // 2, r % 2
                dst = AT[:, bass.ds(s * SB, SB)].rearrange("p (j i) -> p j i", i=SW)[:, 8 * cp:8 * cp + 8, it * D:(it + 1) * D]
                A(dst, ps[r % 2][:].bitcast(BF16).rearrange("p (j i) -> p j i", i=D), ACT.Copy, scale=float(FP8_ONE))\
                    .then_inc(sm("at_ready"), 1)

            def evacuate(phase, s, it, banks, width):
                act.wait_ge(sm("prod_" + phase), s * 2 + (it + 1))
                if it == 0 and not first(s):
                    act.wait_ge(sm("ev_free_" + phase), s)
                elif it == 0 and phase != "a":
                    act.wait_ge(sm("ev_free_" + {"b": "a", "1": "b", "2": "1", "3": "2"}[phase]), S)
                for n, b in enumerate(banks):
                    ins = A(EV[:, (it * len(banks) + n) * width:(it * len(banks) + n + 1) * width], ps[b][:, 0:width], ACT.Copy)
                ins.then_inc(sm("ev_" + phase), 1)

            for r in range(8):
                keep_transposed(0, r)

            def split_feat(s):
                act.wait_ge(sm("feat_ready"), s + 1)
                if not first(s):
                    act.wait_ge(sm("rb_stored"), s * 16)
                for it in range(2):
                    for g in range(2):
                        A(ST16[:, it, g * RH:g * RH + D], ST32[:, it, :], ACT.Copy, scale=CUR[:, it, 4 + g:5 + g])
                        ins = A(T4[:, 2 * it + g, :], ST32[:, it, :], ACT.Copy, scale=CUR[:, it, 6 + g:7 + g])
                ins.then_inc(sm("hi_a"), 1)

            def l0a(s, par, k):
                if not first(s):
                    evacuate("a", s - 1, 1, (4, 5), RH)
                if not last(s):
                    for r in range(4):
                        keep_transposed(s + 1, r)
                if not first(s):
                    split_feat(s - 1)
                evacuate("a", s, 0, (2, 3), RH)
                if not last(s):
                    for r in range(4, 8):
                        keep_transposed(s + 1, r)

            ring(act, l0a)
            evacuate("a", S - 1, 1, (4, 5), RH)
            split_feat(S - 1)

            ab = Steps(act, sm("a_b"))

            def project(s):
                ab.begin(s)
                act.wait_ge(sm("norm_b"), s + 1)
                for it in range(2):
                    ins = A(WB[:, it, :], ST32[:, it, :], ACT.Relu, bias=MV[:, it, 4:5], scale=MV[:, it, 3:4])
                ins.then_inc(sm("hb_b"), 1)
                act.wait_ge(sm("ht_ps"), s + 1)
                A(HT, ps[0][:, 0:SW], ACT.Copy).then_inc(sm("ht_sb"), 1)
                act.wait_ge(sm("pj_ps"), s + 1)
                A(H2T, ps[1][:, 0:SW], ACT.Tanh, bias=col(BP)).then_inc(sm("h2_sb"), 1)
                act.wait_ge(sm("g_ps"), s + 1)
                ab.do(A(WB[:], ps[6][:, 0:SW].rearrange("p (i d) -> p i d", d=D), ACT.Copy, scale=col(SG)))
                if not first(s):
                    act.wait_ge(sm("r1_stored"), s * 16)
                A(ST16[:, :, 0:D], WB[:], ACT.Copy)
                A(T4[:, 0:2, :], WB[:], ACT.Copy, scale=LO).then_inc(sm("hi_b"), 1)
                ab.end()

            act.wait_ge(sm("rb_stored"), 16 * S)

            def l0b(s, par, k):
                if not first(s):
                    evacuate("b", s - 1, 1, (4, 5), RH)
                    project(s - 1)
                evacuate("b", s, 0, (2, 3), RH)

            ring(act, l0b)
            evacuate("b", S - 1, 1, (4, 5), RH)
            project(S - 1)
            act.wait_ge(sm("r1_stored"), 16 * S)

            a1s = Steps(act, sm("a_1"))

            def split_1(s):
                a1s.begin(s)
                act.wait_ge(sm("norm_1"), s + 1)
                for it in range(2):
                    a1s.did(A(T4[:, it, :], ST32[:, it, :], ACT.Relu, bias=MV[:, it, 4:5], scale=MV[:, it, 3:4]))
                a1s.sync()
                if not first(s):
                    act.wait_ge(sm("r2_stored"), s * 16)
                A(ST16[:, :, 0:D], T4[:, 0:2, :], ACT.Copy, scale=HS)
                A(T4[:, 2:4, :], T4[:, 0:2, :], ACT.Copy, scale=HS * LO).then_inc(sm("hi_1"), 1)
                a1s.end()

            def l1(s, par, k):
                if not first(s):
                    evacuate("1", s - 1, 1, (2 * (1 - par) + 1,), 512)
                    split_1(s - 1)
                evacuate("1", s, 0, (2 * par,), 512)

            ring(act, l1)
            evacuate("1", S - 1, 1, (3,), 512)
            split_1(S - 1)

            act.wait_ge(sm("ay_stored"), 16 * S)

            def nets(s):
                for l in range(3):
                    act.wait_ge(sm(f"net_ps{l + 1}"), s + 1)
                    for j in range(2):
                        ins = A(NETS[:, l + 1, j * SW:(j + 1) * SW], ps[5 + l % 2][:, j * SW:(j + 1) * SW], ACT.Relu,
                          bias=col(B6 + 3 * j + l), scale=(col(AX1 + j) if l == 0 else 1.0))
                    ins.then_inc(sm(f"net_sb{l + 1}"), 1)
                act.wait_ge(sm("norm_2"), s + 1)
                for it in range(2):
                    ins = A(WB[:, it, :], ST32[:, it, :], ACT.Relu, bias=MV[:, it, 4:5], scale=MV[:, it, 3:4])
                ins.then_inc(sm("hb_2"), 1)

            def l2(s, par, k):
                if not first(s):
                    evacuate("2", s - 1, 1, (2 * (1 - par) + 1,), 512)
                    nets(s - 1)
                evacuate("2", s, 0, (2 * par,), 512)

            ring(act, l2)
            evacuate("2", S - 1, 1, (3,), 512)
            nets(S - 1)

            act.wait_ge(sm("u3_wanted"), 1)
            A(XT[:, 4:6, :], XT[:, 2:4, :], ACT.Exp).then_inc(sm("u3_made"), 1)

            def l3(s, par, k):
                if not first(s):
                    evacuate("3", s - 1, 1, (4, 5), RH)
                evacuate("3", s, 0, (2, 3), RH)

            ring(act, l3)
            evacuate("3", S - 1, 1, (4, 5), RH)

            def general():
                def exps(e):
                    with act.Fori(0, T) as t:
                        act.wait_ge(sm("exps_wanted"), t + (e * T + 1) + 1)
                        A(QS, QW, ACT.Exp).then_inc(sm("exps_made"), 1)

                exps(0)
                exps(1)
                with act.Fori(0, T) as t:
                    act.wait_ge(sm("pj_ps"), t + 1 + S)
                    A(T4[:, 1, :], ps[5][:, 0:D], ACT.Tanh, bias=col(BP)).then_inc(sm("h2_sb"), 1)
                with act.Fori(0, T) as t:
                    for l in range(3):
                        act.wait_ge(sm(f"net_ps{l + 1}"), t + 1 + S)
                        for j in range(2):
                            ins = A(GNET[l + 1][:, j, :], ps[5 + l % 2][:, j * D:(j + 1) * D], ACT.Relu, bias=col(B6 + 3 * j + l))
                        ins.then_inc(sm(f"net_sb{l + 1}"), 1)
                exps(2)

            act.wait_ge(sm("flag_ready"), 1)
            flag = act.value_load(FLAG)
            with act.If(flag > 0):
                general()

        @block.tensor
        def _(pe):
            def transpose_pair(s, r):
                cp, it = r // 2, r % 2
                if not (isinstance(s, int) and s == 0 and r < 2):
                    pe.wait_ge(sm("at_ready"), s * 8 + (r - 1))
                for cc in range(2):
                    q = cp * 4 + it * 2 + cc
                    pe.wait_ge(sm(f"rows_in{q % 4}"), s * 64 + 16 * (q // 4 + 1))
                    rows = STG[:, q % 4, :].bitcast(BF16).rearrange("p (c two) -> p c two", two=2)
                    for b in range(4):
                        o = (cc * 4 + b) * D
                        ins = pe.transpose(ps[r % 2][:].bitcast(BF16)[:, o:o + D], rows[:, b * D:(b + 1) * D, 1], IDB[:])
                    ins.then_inc(sm("rows_used"), 1)

            def gate(s, bank, fresh):
                if not isinstance(s, int):
                    pe.matmul(ps[bank][:, 511:512], IDB[:], IDB[:, 0:1], start=fresh, stop=True, skip_group_check=True)

            def two_halves(phase, q0, s, par, r_ready, hooks):
                for u in range(16):
                    if u in hooks:
                        hooks[u]()
                    it, c8 = u // 8, u % 8
                    if c8 == 0 and not first(s):
                        pe.wait_ge(sm("ev_" + phase), s * 2 + (it - 1))
                    if it == 0 and c8 % 2 == 0:
                        pe.wait_ge(sm("masks_ready"), (s + q0) * 4 + (c8 // 2 + 1))
                        if first(s):
                            r_ready(c8 // 2)
                    if c8 == 0 or (it == 0 and c8 % 2 == 0):
                        gate(s, 2 + 2 * it, c8 == 0)
                    for jb in range(4 * c8, 4 * c8 + 4):
                        for g in range(2):
                            b = 2 + 2 * it + g
                            o = jb * SW + it * D
                            ins = pe.matmul(ps[b][:, 0:RH], GHf[:, par, g, o:o + D], R3[:, jb, g * RH:(g + 1) * RH],
                                            start=jb == 0, stop=jb == T - 1, skip_group_check=True)
                    if c8 == 7:
                        ins.then_inc(sm("prod_" + phase), 1)

            pe.wait_ge(sm("consts_made"), 1)
            for r in range(2):
                transpose_pair(0, r)
            pe.wait_ge(sm("f1_done"), 1)
            pe.transpose(ps[7][0:T, 0:D], F1[:], IDF[:]).then_inc(sm("f1_ps"), 1)
            for r in range(2, 8):
                transpose_pair(0, r)

            def l0a(s, par, k):
                hooks = {} if last(s) else {2 * r: (lambda r=r: transpose_pair(s + 1, r)) for r in range(8)}
                two_halves("a", 0, s, par, lambda c: pe.wait_ge(sm("job_done"), 2), hooks)

            ring(pe, l0a)

            def norm_transposed(s):
                pe.wait_ge(sm("hb_b"), s + 1)
                for it in range(2):
                    ins = pe.transpose(ps[0][:, it * D:(it + 1) * D], WB[:, it, :], IDF[:])
                ins.then_inc(sm("ht_ps"), 1)

            def proj(s):
                pe.wait_ge(sm("ht_sb"), s + 1)
                pe.matmul(ps[1][:, 0:SW], WP[:], HT, start=True, stop=True).then_inc(sm("pj_ps"), 1)

            def gcn(s):
                pe.wait_ge(sm("h2_sb"), s + 1)
                for it in range(2):
                    ins = pe.matmul(ps[6][:, it * D:(it + 1) * D], H2T[:, it * D:(it + 1) * D], WG[:], start=True, stop=True)
                ins.then_inc(sm("g_ps"), 1)

            def l0b(s, par, k):
                hooks = {} if first(s) else {8: lambda: norm_transposed(s - 1), 10: lambda: proj(s - 1), 13: lambda: gcn(s - 1)}
                two_halves("b", S, s, par, lambda c: pe.wait_ge(sm(f"R_b{c}"), 16), hooks)

            ring(pe, l0b)
            norm_transposed(S - 1)
            proj(S - 1)
            gcn(S - 1)

            def one_half(phase, s, par, hooks):
                pe.wait_ge(sm("copy_" + phase), s + 1)
                for u in range(16):
                    if u in hooks:
                        hooks[u]()
                    it, c8 = u // 8, u % 8
                    if c8 == 0 and not (isinstance(s, int) and s < 2):
                        pe.wait_ge(sm("ev_" + phase), s * 2 + (it - 3))
                    if first(s) and it == 0 and c8 % 2 == 0:
                        pe.wait_ge(sm(f"R_{phase}{c8 // 2}"), 16)
                    if c8 == 0:
                        gate(s, 2 * par + it, True)
                    for jb in range(4 * c8, 4 * c8 + 4):
                        o = jb * SW + it * D
                        ins = pe.matmul(ps[2 * par + it][:], GHf[:, par, 0, o:o + D], R5[:, jb, :],
                                        start=jb == 0, stop=jb == T - 1)
                    if c8 == 7:
                        ins.then_inc(sm("prod_" + phase), 1)

            pe.wait_ge(sm("w8_in"), 16 * 8)
            pe.wait_ge(sm("hi_b"), S)
            for b in range(2):
                for j in range(4):
                    ins = pe.transpose(ps[6 + b][:, j * D:(j + 1) * D], W8[:, 4 * b + j, :], IDF[:])
                ins.then_inc(sm("w8_ps"), 1)
            ring(pe, lambda s, par, k: one_half("1", s, par, {}))

            pe.wait_ge(sm("w8t_ready"), 2)

            def net_in(s):
                pe.wait_ge(sm("ev_free_2"), s + 1)
                for j in range(2):
                    for it in range(2):
                        o = (2 * j + it) * D
                        ins = pe.transpose(ps[4][:, o:o + D], T4[:, 2 * it + j, :], IDF[:])
                ins.then_inc(sm("net_ps0"), 1)

            def net_layer(s, l):
                pe.wait_ge(sm(f"net_sb{l}"), s + 1)
                for j in range(2):
                    ins = pe.matmul(ps[5 + l % 2][:, j * SW:(j + 1) * SW], W8T[:, 3 * j + l, :],
                                    NETS[:, l, j * SW:(j + 1) * SW], start=True, stop=True)
                ins.then_inc(sm(f"net_ps{l + 1}"), 1)

            def net_out(s):
                pe.wait_ge(sm("net_sb3"), s + 1)
                if not first(s):
                    pe.wait_ge(sm("xc_ready"), s)
                for it in range(2):
                    for j in range(2):
                        o = j * SW + it * D
                        ins = pe.matmul(ps[7][:, it * D:(it + 1) * D], NETS[:, 3, o:o + D], W8T[:, 6 + j, :],
                                        start=j == 0, stop=j == 1)
                ins.then_inc(sm("net_ps4"), 1)

            def l2(s, par, k):
                hooks = {} if first(s) else {4: lambda: net_in(s - 1), 7: lambda: net_layer(s - 1, 0),
                                             9: lambda: net_layer(s - 1, 1), 11: lambda: net_layer(s - 1, 2),
                                             13: lambda: net_out(s - 1)}
                one_half("2", s, par, hooks)

            ring(pe, l2)
            net_in(S - 1)
            for l in range(3):
                net_layer(S - 1, l)
            net_out(S - 1)

            pe.wait_ge(sm("f1_done"), 2)
            pe.transpose(ps[7][0:T, 0:D], F1[:], IDF[:]).then_inc(sm("f1_ps"), 1)
            ring(pe, lambda s, par, k: two_halves("3", 2 * S, s, par, lambda c: pe.wait_ge(sm(f"R_3{c}"), 16), {}))

            def general():
                def f2_row(n):
                    pe.wait_ge(sm("f1_done"), n + 1 + 2)
                    pe.transpose(ps[7][0:T, 0:D], GT[:, GF2, :], IDF[:]).then_inc(sm("f1_ps"), 1)

                def product(t, a, right):
                    pe.wait_ge(sm("g_weights"), t + (a * T + 2))
                    for b in range(8):
                        pe.wait_ge(sm("g_copied"), (t + a * T) * 8 + (1 + max(b - 1, 0)))
                        for j in range(4):
                            o = (4 * b + j) * D
                            ins = pe.transpose(ps[b % 2][:, j * D:(j + 1) * D], QW[:, o:o + D], IDF[:])
                        ins.then_inc(sm("g_turned"), 1)
                        pe.wait_ge(sm("g_copied"), (t + a * T) * 8 + (b + 2))
                        for j in range(4):
                            for n, r in enumerate(right):
                                ins = pe.matmul(ps[2 + n][:, 0:D], TURN[:, b % 2, j * D:(j + 1) * D], r[:, 4 * b + j, :],
                                                start=b == 0 and j == 0, stop=b == 7 and j == 3)
                        ins.then_inc(sm("g_added"), 1)

                f2_row(0)
                with pe.Fori(0, T) as t:
                    product(t, 0, [NH])
                with pe.Fori(0, T) as t:
                    product(t, 1, [NB])
                with pe.Fori(0, T) as t:
                    pe.wait_ge(sm("hb_b"), t + 1 + S)
                    pe.transpose(ps[4][:, 0:D], WB[:, 0, :], IDF[:]).then_inc(sm("ht_ps"), 1)
                    pe.wait_ge(sm("ht_sb"), t + 1 + S)
                    pe.matmul(ps[5][:, 0:D], WP[:], WA[:, 0, :], start=True, stop=True).then_inc(sm("pj_ps"), 1)
                    pe.wait_ge(sm("h2_sb"), t + 1 + S)
                    pe.matmul(ps[6][:, 0:D], T4[:, 1, :], WG[:], start=True, stop=True).then_inc(sm("g_ps"), 1)
                with pe.Fori(0, T) as t:
                    product(t, 2, [NB])
                with pe.Fori(0, T) as t:
                    product(t, 3, [NH, NX2])
                    pe.wait_ge(sm("g_ax"), t + 1)
                    for j in range(2):
                        ins = pe.transpose(ps[4][:, j * D:(j + 1) * D], WB[:, j, :], IDF[:])
                    ins.then_inc(sm("net_ps0"), 1)
                    for l in range(3):
                        pe.wait_ge(sm(f"net_sb{l}"), t + 1 + S)
                        for j in range(2):
                            ins = pe.matmul(ps[5 + l % 2][:, j * D:(j + 1) * D], W8T[:, 3 * j + l, :], GNET[l][:, j, :],
                                            start=True, stop=True)
                        ins.then_inc(sm(f"net_ps{l + 1}"), 1)
                    pe.wait_ge(sm("net_sb3"), t + 1 + S)
                    for j in range(2):
                        ins = pe.matmul(ps[7][:, 0:D], GNET[3][:, j, :], W8T[:, 6 + j, :], start=j == 0, stop=j == 1)
                    ins.then_inc(sm("net_ps4"), 1)
                f2_row(1)
                with pe.Fori(0, T) as t:
                    product(t, 4, [NY])

            pe.wait_ge(sm("flag_ready"), 1)
            flag = pe.value_load(FLAG)
            with pe.If(flag > 0):
                general()


_INS = ["x", "adj", "L0_gnn_h0", "L0_gnn_a", "L0_gnn_temp", "L1_gnn_W_proj", "L1_gnn_b_proj", "L1_gnn_W_gcn",
        "L1_gnn_b_gcn", "L2_gnn_x2", "L2_gnn_eps1", "L2_gnn_eps2", "L2_gnn_W1", "L2_gnn_b1", "L2_gnn_W2", "L2_gnn_b2",
        "L2_gnn_Wm", "L2_gnn_bm", "L3_gnn_input2", "L3_gnn_a1", "L3_gnn_a2"]


def kernel(**inputs):
    import numpy as _np
    import concourse.bacc as _bacc
    from concourse import mybir as _mybir
    from concourse.bass_utils import run_bass_kernel_spmd as _run

    nc = _bacc.Bacc("TRN2", target_bir_lowering=False, num_devices=1, dynamic_dma_scratch_size=1024)
    arrays, args = {}, []
    for name in _INS:
        a = _np.ascontiguousarray(inputs[name])
        arrays[f"in_{name}_dram"] = a
        args.append(nc.dram_tensor(f"in_{name}_dram", a.shape, _mybir.dt.from_np(a.dtype), kind="ExternalInput").ap())
    out = nc.dram_tensor("out_0_dram", (N, D), _mybir.dt.float32, kind="ExternalOutput").ap()
    build(nc, *args, out)
    r = _run(nc, [arrays], core_ids=[0])
    return r.results[0]["out_0_dram"]
```

```python
import numpy as np
import concourse.bass as bass
from concourse import mybir
from concourse.alu_op_type import AluOpType as ALU

ACT = mybir.ActivationFunctionType
AX = mybir.AxisListType
F32, F16, BF16 = mybir.dt.float32, mybir.dt.float16, mybir.dt.bfloat16
I32, U8, FP8 = mybir.dt.int32, mybir.dt.uint8, mybir.dt.float8e4

N = 4096
D = 128
T = N // D
SW = 256
S = N // SW
SB = T * SW
RH = 264
RW = 2 * RH
CH = 4
CB = SB // CH
CODED = 2
P2, P3 = 3 * CODED, 3 * (CH - CODED)
M0, M2 = 8 * S, (8 + P2) * S
FP8_ONE = 0x38
every = lambda byte: byte * 0x01010101
TAKE_0 = ((0x40, 0.5), (0x20, 8.0))
TAKE_A = (0x18, 16.0)
TAKE_3 = ((0x20, 8.0), (0x10, 32.0))
EXP_BITS = 0x7F800000
LO = 4096.0
VS = 2.0 ** 15
HS = 2.0 ** 11
FS = 2.0 ** 10
TH = 1e-6
LEAK = 0.2
EPS = 1e-5
DENOM_FLOOR = 2.0 ** -40
TOPK = 350
MASK_FILL = 9e15
DENOM_MIN = 2.0 ** -22


SEMAPHORES = """
x_in vec_in y_in x2_in w_in rows_in0 rows_in1 rows_in2 rows_in3 rows_used h_made f1t_made job_done x16_made
h_x16_stored f1_stored r3_f1_stored r2x_stored r1y_stored f1_in0 f1_in1 masks_ready at_ready
consts_made stats_made var_made rstd_made maxima_made maxima_all exps_wanted exps_made scaled_made hi_made rest_made
prod_a ev_a ev_free_a xin_a feat_ready hi_a rb_ready feat_stored rb_stored R_free R_in0 R_in1 R_in2 R_in3
prod_b ev_b ev_free_b xin_b xin_free_b x1_ready x1_stored r1_ready r1_stored var_b rstd_b norm_b hb_b ht_ps ht_sb pj_ps h2_sb g_ps hi_b
 rows3_in w8_in w8_ps w8t_ready copy_1 prod_1 ev_1 ev_free_1 xin_1 xb_ready xb_stored ay_ready ay_stored
r2_ready r2_stored var_1 rstd_1 norm_1 hi_1
 copy_2 prod_2 ev_2 ev_free_2 xin_2 xin_free_2 net_ps0 net_sb0 net_ps1 net_sb1 net_ps2 net_sb2 net_ps3 net_sb3 net_ps4
xc_ready xc_stored var_2 rstd_2 norm_2 hb_2 u3_wanted u3_made f1_done f1_ps f1b_stored
 prod_3 ev_3 ev_free_3 xin_3 xin_free_3 out_ready out_stored
v_pro v_mask v_a v_b v_1 v_2 v_3 a_pro a_b a_1 g_pro
coded_0 cleaned diag_made f1_row_ps f1_row bad_rows bad_any flag_ready g_rows g_weights g_turned g_copied g_added g_ax g_x v_g v_tiles
"""


class Steps:

    def __init__(self, eng, sem, per=None, base=0):
        self.eng, self.sem, self.start, self.n, self.per, self.base = eng, sem, 0, 0, per, base

    def begin(self, strip):
        self.start = 0 if isinstance(strip, int) and strip == 0 else strip * self.per
        self.n = 0

    def end(self):
        if self.per is None:
            self.per = self.n
        assert self.per == self.n, (self.per, self.n)

    def did(self, ins):
        ins.then_inc(self.sem, 1)
        self.n += 1

    def sync(self):
        self.eng.wait_ge(self.sem, self.start + (self.base + self.n))

    def do(self, ins):
        self.did(ins)
        self.sync()


def build(nc, x, adj, h0, a0, temp, w_proj, b_proj, w_gcn, b_gcn, x2, eps1, eps2,
          w1, b1, w2, b2, wm, bm, y, a1, a2, out):
    from contextlib import ExitStack
    ctx = ExitStack()
    with ctx:
        def sb(name, shape, dt=F32):
            return ctx.enter_context(nc.sbuf_tensor(name, shape, dt))

        def sem(name):
            return ctx.enter_context(nc.semaphore(name))

        def dram(name, shape, dt=F32):
            return nc.dram_tensor(name, shape, dt)

        AT = sb("AT", [128, S * SB], U8)
        GH = sb("GH", [128, 2, 2, SB], U8)
        R = sb("R", [128, T * RW], F16)
        STG = sb("STG", [128, 4, 512])
        F1R = sb("F1R", [128, 2, SW])
        XIN = sb("XIN", [128, 3, 2, D])
        EV = sb("EV", [128, 2 * RW])
        T4 = sb("T4", [128, 4, D])
        WA = sb("WA", [128, 2, D])
        WB = sb("WB", [128, 2, D])
        ST16 = sb("ST16", [128, 2, RW], F16)
        ST32 = sb("ST32", [128, 2, D])
        WP = sb("WP", [128, D])
        WG = sb("WG", [128, D])
        IDF = sb("IDF", [128, D])
        IDB = sb("IDB", [128, D], BF16)
        TBL = sb("TBL", [128, S, 2, 8])
        CUR = sb("CUR", [128, 2, 8])
        RT = sb("RT", [128, S, 2, 4])
        RTC = sb("RTC", [128, 2, 4])
        DEN = sb("DEN", [128, 2, T])
        DEG = sb("DEG", [128, T])
        F1 = sb("F1", [128, T])
        F2N = sb("F2N", [128, 2, T])
        COL = sb("COL", [128, 48])
        SM = sb("SM", [128, 64])
        MV = sb("MV", [128, 2, 8])
        CO = sb("CO", [128, 6])
        FLG = sb("FLG", [128, 3])

        def col(i):
            return COL[:, i:i + 1]
        (MX0, MX3, AMY, AMX, AMG, SY, SX, SG, ISY, ISX, ISG, C0, C1, C2, C3, K2, BP, TG, KE1, KE2,
         NM0, NM3, BIAS0) = range(23)
        B6 = 24
        CSY, OMC2, E5, C1C0, AX1, AX2, ONE, MH, NC3, CG = 30, 31, 33, 40, 41, 42, 43, 44, 45, 46
        NW = 12

        GHf = GH[:].bitcast(FP8)
        GH16 = GH[:].bitcast(mybir.dt.uint16)
        GHI = GH[:].bitcast(I32)
        slots = AT[:].bitcast(F32).rearrange("p (k n) -> p k n", n=N)
        PX2, PY, PT, PU, PX, PH = (slots[:, k, :].rearrange("p (t d) -> p t d", d=D) for k in range(2, 8))
        P16 = {k: slots[:, k, :].bitcast(F16).rearrange("p (t c) -> p t c", c=256) for k in (2, 3, 6, 7)}
        A3 = slots[:, 1, 0:3 * D].rearrange("p (k d) -> p k d", d=D)
        LT = slots[:, 1, 512:512 + 24 * T].rearrange("p (k t) -> p k t", t=T)
        BNS = slots[:, 1, 1280:1280 + 6 * T].rearrange("p (t k) -> p t k", k=6)
        MVP = slots[:, 1, 1536:1536 + 2 * T].rearrange("p (t k) -> p t k", k=2)
        E16 = slots[:, 1, 2048:2048 + 6 * T].bitcast(F16).rearrange("p (q k t) -> p q k t", q=4, k=3)
        X16 = slots[:, 1, 3072:3072 + 8 * T].bitcast(F16).rearrange("p (t g e) -> p t g e", g=2, e=8)
        R3 = R[:].rearrange("p (t c) -> p t c", c=RW)
        R5 = R[:, 0:T * 512].rearrange("p (t c) -> p t c", c=512)
        WORK = (PT, PU)
        HI, LOW = ([R3[:, :, c:c + D], R3[:, :, RH + c:RH + c + D]] + [P16[k][:, :, c:c + D] for k in (6, 7, 2, 3)]
                   for c in (0, D))
        W8 = STG[:, 0:2, :].rearrange("p a (b d) -> p (a b) d", d=D)
        W8T = STG[:, 2:4, :].rearrange("p a (b d) -> p (a b) d", d=D)
        HT = STG[:, 0, 0:SW]
        H2T = STG[:, 1, 0:SW]
        NETS = GH[:, 0, 1, :].bitcast(F32).rearrange("p (l n) -> p l n", n=512)
        ROWS = GH[:, 1, 1, 0:4 * 3 * D].bitcast(F32).rearrange("p (k d) -> p k d", d=D)
        BG, BM, A1R = ROWS[:, 0, :], ROWS[:, 1, :], ROWS[:, 2, :]
        ONES = GH[:, 1, 1, 4 * 3 * D:4 * 4 * D].bitcast(F32)
        POS = GH[:, 1, 1, CB:3 * CB].rearrange("p (k n) -> p k n", n=CB)
        FT = T4[0:T, 0, :]
        F1T = T4[:, 0, 0:T]
        XT = EV[:, 0:6 * T].rearrange("p (k t) -> p k t", t=T)
        EVq = EV[:].rearrange("p (q c) -> p q c", c=RH)
        EV5 = EV[:, 0:1024].rearrange("p (q c) -> p q c", c=256)
        ST16q = ST16[:].rearrange("p i (g c) -> p (i g) c", c=RH)
        TBLt = TBL[:].rearrange("p s i w -> p (s i) w")
        RTt = RT[:].rearrange("p s i w -> p (s i) w")

        ps = [ctx.enter_context(nc.psum_tensor(f"ps{b}", [128, 512], F32)) for b in range(8)]

        f1_d = [dram(f"f1_{k}", [T, D]) for k in range(2)]
        h_d, feat_d, x1_d, xb_d, xc_d, ay_d = (dram(n, [128, T, D]) for n in ("h_s", "feat_s", "x1_s", "xb_s", "xc_s", "ay_s"))
        rb_d = dram("rb_s", [128, T, RW], F16)
        r1_d = dram("r1_s", [128, T, 512], F16)
        r2_d = dram("r2_s", [128, T, 512], F16)
        r3_d = dram("r3_s", [128, T, RW], F16)
        tile_rows = lambda t: t.rearrange("(t p) d -> p t d", p=128)

        wide = [slots[:, k, :] for k in range(8)] + [GH[:].rearrange("p a b n -> p (a b n)").bitcast(F32)[:, N * k:N * k + N] for k in range(2)] \
            + [R[:].bitcast(F32)[:, N * k:N * k + N] for k in range(2)]
        QX, QH, QB, QA, QW, QS, QY, QX2, QF, QM, Q0, QC = wide
        nodes = lambda q: q.rearrange("p (t d) -> p t d", d=D)
        NX, NH, NB, NW_, NS, NY, NX2, N0 = (nodes(q) for q in (QX, QH, QB, QW, QS, QY, QX2, Q0))
        GT = R[:].bitcast(F32)[:, 2 * N:2 * N + 6 * T].rearrange("p (k t) -> p k t", t=T)
        GMEAN, GVAR, GRSTD, GF1, GF2, GRS = range(6)
        TURN = EV[:, 0:1024].rearrange("p (b n) -> p b n", n=512)
        GROWS = STG[:, 0:2, :].rearrange("p a (b d) -> p (a b) d", d=D)
        GNET = [XIN[:, 0, :, :], XIN[:, 1, :, :], XIN[:, 2, :, :], ST32[:]]
        GA1, BAD = 38, 47
        FLAG = FLG[0:1, 0:1].bitcast(I32)
        one = lambda q, t: q[:, bass.ds(t, 1), :].rearrange("p o d -> p (o d)")

        sems = {n: sem(n) for n in SEMAPHORES.split()}
        sm = sems.__getitem__

        block = ctx.enter_context(nc.Block())
        BCAST = lambda ap1, n=D: ap1.unsqueeze(2).broadcast_to([128, ap1.shape[1], n])

        def ring(eng, body):
            for s in (0, 1):
                body(s, s, 0)
            with eng.Fori(1, S // 2 - 1) as k:
                body(k * 2, 0, k)
                body(k * 2 + 1, 1, k)
            for s in (S - 2, S - 1):
                body(s, s % 2, S // 2 - 1)

        first = lambda s: isinstance(s, int) and s == 0
        last = lambda s: isinstance(s, int) and s == S - 1

        @block.sync
        def _(sp):
            ld = lambda dst, src, s: sp.dma_start(dst, src).then_inc(sm(s), 16)
            ld(PX, tile_rows(x), "x_in")
            a0c = a0.rearrange("(k d) o -> k (d o)", k=2)
            ld(A3[:, 0, :], a0c[0, :].partition_broadcast(128), "vec_in")
            ld(A3[:, 1, :], a0c[1, :].partition_broadcast(128), "vec_in")
            ld(A3[:, 2, :], a2.rearrange("d o -> (d o)").partition_broadcast(128), "vec_in")
            ld(PY, tile_rows(y), "y_in")
            ld(PX2, tile_rows(x2), "x2_in")
            ld(WP[:], w_proj, "w_in")
            ld(WG[:], w_gcn, "w_in")
            ld(COL[:, C0:C0 + 5], temp.partition_broadcast(128), "w_in")
            ld(COL[:, KE1:KE1 + 1], eps1.partition_broadcast(128), "w_in")
            ld(COL[:, KE2:KE2 + 1], eps2.partition_broadcast(128), "w_in")
            ld(col(BP), b_proj.rearrange("(d o) -> d o", o=1), "w_in")
            for j, b in enumerate((b1, b2)):
                for l in range(3):
                    ld(COL[:, B6 + 3 * j + l:B6 + 3 * j + l + 1], b[l, :].rearrange("(d o) -> d o", o=1), "w_in")

            def load_strip_rows(s, between, start=0, stop=16):
                n = 0
                for cp in range(4):
                    for it in range(2):
                        for c in (2 * cp, 2 * cp + 1):
                            q = cp * 4 + it * 2 + c % 2
                            if not start <= q < stop:
                                continue
                            if not (isinstance(s, int) and s * 16 + q < 4):
                                sp.wait_ge(sm("rows_used"), s * 16 + (q - 3))
                            ld(STG[:, q % 4, :], adj[bass.ds(s * SW + it * 128, 128), c * 512:(c + 1) * 512],
                               f"rows_in{q % 4}")
                            if n in between:
                                between[n]()
                            n += 1

            load_strip_rows(0, {}, 0, 4)
            sp.wait_ge(sm("h_made"), 1)
            ld(h_d[:, :, :], PH, "h_x16_stored")
            sp.wait_ge(sm("f1t_made"), 1)
            ld(f1_d[0][:, :], FT, "f1_stored")
            sp.wait_ge(sm("f1_stored"), 16)
            f1row = lambda k: f1_d[k].rearrange("t p -> (t p)")

            def load_f1(k, s, par, g, compared=None):
                if compared:
                    sp.wait_ge(sm("v_mask"), compared)
                if g is not None:
                    sp.wait_ge(sm("masks_ready"), g)
                ld(F1R[:, par, :], f1row(k)[bass.ds(s * SW, SW)].partition_broadcast(128), f"f1_in{par}")

            def load_R(src, width, n, chunks, used=None):
                dst = R[:, 0:T * width].rearrange("p (t c) -> p t c", c=width)
                for c in chunks:
                    if c == 3:
                        sp.wait_ge(sm(used), 2 * S)
                    else:
                        sp.wait_ge(sm("R_free"), 3 * n + c + 1)
                    ld(dst[:, 8 * c:8 * c + 8, :], src[:, 8 * c:8 * c + 8, :], f"R_in{c}")

            load_f1(0, 0, 0, None)
            load_f1(0, 1, 1, None)
            load_strip_rows(0, {}, 4, 16)
            sp.wait_ge(sm("h_x16_stored"), 16)

            def l0a(s, par, k):
                def early():
                    if not (isinstance(s, int) and s >= S - 2):
                        load_f1(0, s + 2, par, 4 * (s + 1))

                def late():
                    if not first(s):
                        store_a(s - 1)
                        sp.wait_ge(sm("feat_ready"), s)
                    ld(XIN[:, 0, :, :], h_d[:, bass.ds(s * 2, 2), :], "xin_a")

                if last(s):
                    sp.wait_ge(sm("rb_stored"), 16 * (S - 2))
                    load_R(rb_d, RW, 0, range(3))
                    late()
                else:
                    load_strip_rows(s + 1, {7: early, 15: late})

            def store_a(s):
                sp.wait_ge(sm("feat_ready"), s + 1)
                ld(feat_d[:, bass.ds(s * 2, 2), :], ST32[:], "feat_stored")
                sp.wait_ge(sm("rb_ready"), s + 1)
                ld(rb_d[:, bass.ds(s * 2, 2), :], ST16[:], "rb_stored")

            ring(sp, l0a)
            store_a(S - 1)

            sp.wait_ge(sm("rb_stored"), 16 * S)
            load_R(rb_d, RW, 0, (3,), "prod_a")
            sp.wait_ge(sm("feat_stored"), 16 * S)

            xt = tile_rows(x)
            h0t = tile_rows(h0)

            def l0b(s, par, k):
                if not first(s):
                    sp.wait_ge(sm("xin_free_b"), s)
                ld(XIN[:, 0, :, :], xt[:, bass.ds(s * 2, 2), :], "xin_b")
                ld(XIN[:, 1, :, :], feat_d[:, bass.ds(s * 2, 2), :], "xin_b")
                ld(XIN[:, 2, :, :], h0t[:, bass.ds(s * 2, 2), :], "xin_b")
                if last(s):
                    sp.wait_ge(sm("r1_stored"), 16 * (S - 2))
                    sp.wait_ge(sm("r1y_stored"), 16)
                    load_R(r1_d, 512, 1, range(3))
                if not first(s):
                    store_b(s - 1)

            def store_b(s):
                sp.wait_ge(sm("x1_ready"), s + 1)
                ld(x1_d[:, bass.ds(s * 2, 2), :], ST32[:], "x1_stored")
                sp.wait_ge(sm("r1_ready"), s + 1)
                ld(r1_d[:, bass.ds(s * 2, 2), 0:256], ST16[:, :, 0:256], "r1_stored")

            ring(sp, l0b)
            store_b(S - 1)
            sp.wait_ge(sm("r1_stored"), 16 * S)
            load_R(r1_d, 512, 1, (3,), "prod_b")
            sp.wait_ge(sm("x1_stored"), 16 * S)

            for k, v in enumerate((b_gcn, bm, a1.rearrange("d o -> (d o)"))):
                ld(ROWS[:, k, :], v.partition_broadcast(128), "rows3_in")
            for j, w in enumerate((w1, w2)):
                for l in range(3):
                    ld(W8[:, 3 * j + l, :], w[l, :, :], "w8_in")
            for j in range(2):
                ld(W8[:, 6 + j, :], wm[:, j * D:(j + 1) * D], "w8_in")

            def l1(s, par, k):
                if not first(s):
                    sp.wait_ge(sm("xb_ready"), s)
                ld(XIN[:, 0, :, :], x1_d[:, bass.ds(s * 2, 2), :], "xin_1")
                if last(s):
                    sp.wait_ge(sm("r2_stored"), 16 * (S - 2))
                    sp.wait_ge(sm("r2x_stored"), 16)
                    load_R(r2_d, 512, 2, range(3))
                if not first(s):
                    store_1(s - 1)

            def store_1(s):
                sp.wait_ge(sm("xb_ready"), s + 1)
                ld(xb_d[:, bass.ds(s * 2, 2), :], ST32[:], "xb_stored")
                sp.wait_ge(sm("ay_ready"), s + 1)
                ld(ay_d[:, bass.ds(s * 2, 2), :], WB[:], "ay_stored")
                sp.wait_ge(sm("r2_ready"), s + 1)
                ld(r2_d[:, bass.ds(s * 2, 2), 0:256], ST16[:, :, 0:256], "r2_stored")

            ring(sp, l1)
            store_1(S - 1)
            sp.wait_ge(sm("r2_stored"), 16 * S)
            load_R(r2_d, 512, 2, (3,), "prod_1")
            sp.wait_ge(sm("xb_stored"), 16 * S)
            sp.wait_ge(sm("ay_stored"), 16 * S)

            def l2(s, par, k):
                if not first(s):
                    sp.wait_ge(sm("xin_free_2"), s)
                ld(XIN[:, 0, :, :], xb_d[:, bass.ds(s * 2, 2), :], "xin_2")
                if not (isinstance(s, int) and s < 2):
                    store_row(s - 2, par)
                if not first(s):
                    store_2(s - 1)

            def store_2(s):
                sp.wait_ge(sm("xc_ready"), s + 1)
                ld(xc_d[:, bass.ds(s * 2, 2), :], ST32[:], "xc_stored")

            def store_row(s, par):
                sp.wait_ge(sm("f1_row"), s + 1)
                ld(f1_d[1][bass.ds(s * 2, 2), :].rearrange("(o t) p -> o (t p)", o=1), F1R[0:1, par, :], "r3_f1_stored")

            ring(sp, l2)
            load_R(r3_d, RW, 3, range(4), "prod_2")
            store_row(S - 2, 0)

            sp.wait_ge(sm("r3_f1_stored"), 32 + 16 * (S - 1))
            load_f1(1, 0, 0, None, M2 - P2)
            store_2(S - 1)
            store_row(S - 1, 1)
            sp.wait_ge(sm("r3_f1_stored"), 32 + 16 * S)
            load_f1(1, 1, 1, None, M2 + P3)
            sp.wait_ge(sm("xc_stored"), 16 * S)

            def l3(s, par, k):
                if not first(s):
                    sp.wait_ge(sm("xin_free_3"), s)
                ld(XIN[:, 0, :, :], xc_d[:, bass.ds(s * 2, 2), :], "xin_3")
                ld(XIN[:, 1, :, :], ay_d[:, bass.ds(s * 2, 2), :], "xin_3")
                if not (isinstance(s, int) and s >= S - 2):
                    load_f1(1, s + 2, par, 8 * S + 4 * (s + 1))
                if not first(s):
                    store_3(s - 1)

            ot = tile_rows(out)

            def store_3(s):
                sp.wait_ge(sm("out_ready"), s + 1)
                ld(ot[:, bass.ds(s * 2, 2), :], ST32[:], "out_stored")

            ring(sp, l3)
            store_3(S - 1)
            sp.wait_ge(sm("out_stored"), 16 * S)

            def general():
                for dst, src in ((NX, x), (NY, y), (NX2, x2), (N0, h0)):
                    ld(dst, tile_rows(src), "x_in")
                for k, src in enumerate((a0c[0, :], a0c[1, :], a1.rearrange("d o -> (d o)"), a2.rearrange("d o -> (d o)"),
                                         b_gcn, bm)):
                    ld(GROWS[:, k, :], src.partition_broadcast(128), "vec_in")

                def f2_row(k):
                    sp.wait_ge(sm("f1t_made"), k + 1 + 1)
                    ld(f1_d[k][:, :], FT, "f1b_stored")
                    sp.wait_ge(sm("f1b_stored"), 16 * (k + 1))
                    ld(QF, f1row(k).partition_broadcast(128), "f1_in0")

                def rows(a):
                    with sp.Fori(0, T) as t:
                        sp.wait_ge(sm("g_weights"), t + (a * T + 1))
                        ld(QA, adj[bass.ds(t * D, D), :], "g_rows")

                f2_row(0)
                for a in range(4):
                    rows(a)
                f2_row(1)
                rows(4)
                sp.wait_ge(sm("g_x"), 1)
                ld(tile_rows(out), NX, "out_stored")
                sp.wait_ge(sm("out_stored"), 16 + 16 * S)

            sp.wait_ge(sm("flag_ready"), 1)
            flag = sp.value_load(FLAG)
            with sp.If(flag > 0):
                general()

        @block.gpsimd
        def _(pool):
            g = Steps(pool, sm("g_pro"))
            g.did(pool.memset(IDF[:], 0.0))
            g.did(pool.memset(IDB[:], 0.0))
            g.sync()
            for m in (IDF, IDB):
                g.did(pool.affine_select(out=m[:], in_=m[:], compare_op=ALU.not_equal, fill=1.0, base=0,
                                         pattern=[[-1, D]], channel_multiplier=1))
            for k in range(3):
                for q in range(2):
                    g.did(pool.memset(CO[:, 3 * q + k:3 * q + k + 1], 1.0 / VS / LO ** k))
            g.did(pool.memset(LT[:, 0, :], -0.5))
            g.did(pool.memset(COL[:, ONE:ONE + 1], 1.0))
            g.did(pool.memset(ST16[:], 0.0))
            g.did(pool.memset(COL[:, MH:MH + 1], -0.5))
            for w in (0, RH):
                g.did(pool.memset(R3[:, :, w + 262:w + 263], 1.0))
                g.did(pool.memset(R3[:, :, w + 263:w + 264], 0.0))
            g.did(pool.memset(X16[:, :, :, 6:7], 1.0))
            g.did(pool.memset(X16[:, :, :, 7:8], 0.0))
            g.sync()
            pool.nop().then_inc(sm("consts_made"), 1)
            pool.wait_ge(sm("var_made"), 1)
            pool.tensor_tensor(LT[:, 2, :], LT[:, 1, :], LT[:, 0, :], ALU.pow).then_inc(sm("rstd_made"), 1)
            pool.wait_ge(sm("maxima_made"), 1)
            pool.partition_all_reduce(COL[:, 0:5], SM[:, 0:5], 128, bass.bass_isa.ReduceOp.max).then_inc(sm("maxima_all"), 1)

            def rstd(phase):
                def body(s, par, k):
                    pool.wait_ge(sm("var_" + phase), s + 1)
                    pool.tensor_tensor(MV[:, :, 3], MV[:, :, 2], col(MH).broadcast_to([128, 2]),
                                       ALU.pow).then_inc(sm("rstd_" + phase), 1)
                with pool.Fori(0, S) as s:
                    body(s, 0, 0)

            rstd("b")
            rstd("1")
            rstd("2")

            pool.wait_ge(sm("bad_rows"), 1)
            pool.partition_all_reduce(col(BAD), SM[:, 2:3], 128, bass.bass_isa.ReduceOp.max).then_inc(sm("bad_any"), 1)

            pool.wait_ge(sm("flag_ready"), 1)
            flag = pool.value_load(FLAG)
            with pool.If(flag > 0):
                for n in range(4):
                    pool.wait_ge(sm("var_b"), n + 1 + S)
                    pool.tensor_tensor(GT[:, GRSTD, :], GT[:, GVAR, :], col(MH).broadcast_to([128, T]),
                                       ALU.pow).then_inc(sm("rstd_b"), 1)

        @block.vector
        def _(dve):
            v = Steps(dve, sm("v_pro"))
            ts, tt, stt, red = dve.tensor_scalar, dve.tensor_tensor, dve.scalar_tensor_tensor, dve.tensor_reduce
            lt = lambda k: LT[:, k, :]
            dve.wait_ge(sm("consts_made"), 1)
            dve.wait_ge(sm("x_in"), 16)
            for t in range(T):
                v.did(dve.bn_stats(BNS[:, t, :], PX[:, t, :]))
            v.sync()
            for t in range(T):
                v.did(dve.bn_aggr(MVP[:, t, :], BNS[:, t, :]))
            v.sync()
            ts(lt(1), MVP[:, :, 1], EPS, None, ALU.add).then_inc(sm("var_made"), 1)
            v.do(tt(PT, PX, BCAST(MVP[:, :, 0]), ALU.subtract))
            dve.wait_ge(sm("rstd_made"), 1)
            stt(PH, PT, 0.0, BCAST(lt(2)), ALU.max, ALU.mult).then_inc(sm("h_made"), 1)
            dve.wait_ge(sm("h_made"), 1)
            vec = lambda k: A3[:, k, :].unsqueeze(1).broadcast_to([128, T, D])
            dve.wait_ge(sm("vec_in"), 48)
            v.do(tt(PU, PH, vec(0), ALU.mult))
            red(F1[:], PU, AX.X, ALU.add).then_inc(sm("f1_done"), 1)
            dve.wait_ge(sm("f1_done"), 1)
            v.do(tt(PU, PH, vec(1), ALU.mult))
            v.do(red(lt(4), PU, AX.X, ALU.add))
            dve.wait_ge(sm("y_in"), 16)
            v.do(tt(PU, PY, vec(2), ALU.mult))
            v.do(red(lt(5), PU, AX.X, ALU.add))
            dve.wait_ge(sm("x2_in"), 16)
            dve.wait_ge(sm("w_in"), 16 * NW)
            v.did(red(SM[:, 0:1], lt(4), AX.X, ALU.max))
            v.did(red(SM[:, 1:2], lt(5), AX.X, ALU.max))
            v.did(red(SM[:, 2:3], PY, AX.XY, ALU.max, apply_absolute_value=True))
            v.did(red(SM[:, 3:4], PX2, AX.XY, ALU.max, apply_absolute_value=True))
            v.do(red(SM[:, 4:5], WG[:], AX.X, ALU.max, apply_absolute_value=True))
            v.do(ts(SM[:, 4:5], SM[:, 4:5], float(D), None, ALU.mult))
            dve.engine_nop().then_inc(sm("maxima_made"), 1)
            dve.wait_ge(sm("f1_ps"), 1)
            dve.tensor_copy(FT, ps[7][0:T, 0:D]).then_inc(sm("f1t_made"), 1)
            dve.wait_ge(sm("maxima_all"), 1)
            v.do(ts(SM[:, 8:11], COL[:, AMY:AMG + 1], 1e-30, None, ALU.max))
            v.do(ts(SM[:, 8:11].bitcast(I32), SM[:, 8:11].bitcast(I32), EXP_BITS, None, ALU.bitwise_and))
            v.did(ts(COL[:, ISY:ISY + 3], SM[:, 8:11], 1.0 / 8192, None, ALU.mult))
            v.do(dve.reciprocal(SM[:, 12:15], SM[:, 8:11]))
            v.did(ts(COL[:, SY:SY + 3], SM[:, 12:15], 8192.0, None, ALU.mult))
            v.did(ts(COL[:, NM0:NM0 + 2], COL[:, MX0:MX0 + 2], -1.0, None, ALU.mult))
            v.sync()
            v.do(ts(lt(6), F1[:], col(MX0), None, ALU.add))
            v.do(stt(lt(7), lt(6), LEAK, lt(6), ALU.mult, ALU.max))
            v.did(tt(lt(8), lt(6), lt(7), ALU.subtract))
            v.did(stt(lt(9), lt(6), LEAK, lt(7), ALU.mult, ALU.subtract))
            v.did(ts(lt(10), lt(4), col(MX0), None, ALU.subtract))
            v.did(ts(lt(11), lt(4), col(MX0), LEAK, ALU.subtract, ALU.mult))
            v.did(ts(lt(12), lt(5), col(MX3), None, ALU.subtract))
            v.did(ts(lt(13), lt(5), col(MX3), LEAK, ALU.subtract, ALU.mult))
            v.did(ts(F2N[:, 0, :], lt(4), -1.0, None, ALU.mult))
            v.did(ts(F2N[:, 1, :], lt(5), -1.0, None, ALU.mult))
            v.sync()
            dve.engine_nop().then_inc(sm("exps_wanted"), 1)
            dve.wait_ge(sm("exps_made"), 1)

            def factors(u, up):
                v.did(dve.tensor_copy(TBLt[:, :, 0], u))
                v.did(tt(TBLt[:, :, 1], u, u, ALU.mult))
                v.did(dve.tensor_copy(TBLt[:, :, 2], up))
                v.did(tt(TBLt[:, :, 3], up, up, ALU.mult))

            factors(lt(14), lt(15))
            for k, c in ((4, FS), (6, FS * LO)):
                v.did(ts(TBLt[:, :, k], lt(16), c, None, ALU.mult))
                v.did(ts(TBLt[:, :, k + 1], lt(17), c, None, ALU.mult))

            def extras(va, vb, dst):
                VV, RR = LT[:, 20:24, :], slots[:, 1, 3584:3584 + 4 * T].rearrange("p (k t) -> p k t", t=T)
                v.sync()
                v.did(ts(lt(20), va, VS, None, ALU.mult))
                v.did(ts(lt(22), vb, VS, None, ALU.mult))
                v.did(stt(lt(21), va, VS, va, ALU.mult, ALU.mult))
                v.do(stt(lt(23), vb, VS, vb, ALU.mult, ALU.mult))
                for part in range(3):
                    v.do(dve.tensor_copy(E16[:, :, part, :], VV))
                    if part < 2:
                        v.do(tt(RR, VV, E16[:, :, part, :], ALU.subtract))
                        v.do(ts(VV, RR, LO, None, ALU.mult))
                for q in range(4):
                    v.did(dve.tensor_copy(dst(q), E16[:, q, :, :].rearrange("p k t -> p t k")))
                v.sync()

            extras(lt(16), lt(17), lambda q: R3[:, :, RH * (q // 2) + 256 + 3 * (q % 2):RH * (q // 2) + 259 + 3 * (q % 2)])
            v.did(ts(lt(16), lt(16), HS, None, ALU.mult))
            v.did(ts(lt(17), lt(17), HS, None, ALU.mult))
            extras(lt(18), lt(19), lambda q: X16[:, :, q // 2, 3 * (q % 2):3 * (q % 2) + 3])
            dve.engine_nop().then_inc(sm("x16_made"), 1)
            v.did(ts(lt(18), lt(18), col(SY), None, ALU.mult))
            v.did(ts(lt(19), lt(19), col(SY), None, ALU.mult))
            c = lambda k: col(C0 + k)
            v.do(ts(COL[:, E5:E5 + 5], COL[:, E5:E5 + 5], 1.0, None, ALU.add))
            v.do(dve.reciprocal(COL[:, C0:C0 + 5], COL[:, E5:E5 + 5]))
            v.did(ts(SM[:, 16:20], COL[:, C0:C0 + 4], -1.0, 1.0, ALU.mult, ALU.add))
            v.sync()
            v.did(dve.tensor_copy(col(OMC2), SM[:, 18:19]))
            v.did(tt(col(K2), SM[:, 17:18], SM[:, 16:17], ALU.mult))
            v.did(tt(col(C1C0), SM[:, 17:18], c(0), ALU.mult))
            v.did(ts(col(NC3), c(3), -1.0, None, ALU.mult))
            v.did(tt(col(CG), col(TG), col(ISG), ALU.mult))
            v.did(ts(col(CSY), col(ISY), 0.5, None, ALU.mult))
            v.did(ts(col(AX1), col(KE1), 2.0, 1.0 / HS, ALU.add, ALU.mult))
            v.did(stt(col(AX2), col(KE2), 2.0, col(ISX), ALU.add, ALU.mult))
            v.sync()
            sources = ((PH, lt(16)), (PH, lt(17)), (PY, lt(18)), (PY, lt(19)), (PX2, col(SX)), (PY, col(SY)))

            def scaled(j):
                src, scale = sources[j]
                if j > 1:
                    dve.wait_ge(sm("job_done"), j - 1)
                if j < 4:
                    tt(WORK[j % 2], src, BCAST(scale), ALU.mult).then_inc(sm("scaled_made"), 1)
                else:
                    ts(WORK[j % 2], src, scale, None, ALU.mult).then_inc(sm("scaled_made"), 1)

            def remainder(j):
                dve.wait_ge(sm("hi_made"), j + 1)
                dve.wait_ge(sm("scaled_made"), j + 1)
                stt(WORK[j % 2], HI[j], -1.0, WORK[j % 2], ALU.mult, ALU.add).then_inc(sm("rest_made"), 1)

            scaled(0)
            scaled(1)
            remainder(0)
            remainder(1)

            def make_masks(s, par, k, chunks):
                for ch in chunks:
                    if ch == 0:
                        dve.wait_ge(sm(f"f1_in{par}"), (k + 1) * 16)
                        if not (isinstance(s, int) and s < 2):
                            dve.wait_ge(sm("prod_a"), 2 * (s - 1))
                    dve.wait_ge(sm("at_ready"), s * 8 + (2 * ch + 2))
                    for jb in range(8 * ch, 8 * ch + 8):
                        ins = ts(GH[:, par, 0, jb * SW:(jb + 1) * SW], F1R[:, par, :], F2N[:, 0, jb:jb + 1],
                                 float(FP8_ONE), ALU.is_gt, ALU.mult)
                        if ch > 0 and jb % 8 == 2:
                            code_edges(s, par, ch - 1)
                        if ch > 0 and jb % 8 == 5:
                            other_edges(s, par, ch - 1)
                    ins.then_inc(sm("v_mask"), 1)
                    mask_edges(s, par, ch)
                if CH - 1 in chunks:
                    code_edges(s, par, CH - 1)
                    other_edges(s, par, CH - 1)

            at_chunk = lambda s, ch: AT[:, bass.ds(s * SB + ch * CB, CB)].bitcast(I32)
            gh_chunk = lambda par, g, ch: GHI[:, par, g, ch * (CB // 4):(ch + 1) * (CB // 4)]

            def mask_edges(s, par, ch):
                g0 = gh_chunk(par, 0, ch)
                dve.wait_ge(sm("v_mask"), s * 8 + (2 * ch + 1))
                tt(g0, g0, at_chunk(s, ch), ALU.bitwise_and).then_inc(sm("v_mask"), 1)

            def code_edges(s, par, ch):
                at = at_chunk(s, ch)
                dve.wait_ge(sm("v_mask"), s * 8 + (2 * ch + 2))
                stt(at, gh_chunk(par, 0, ch), 2, at, ALU.logical_shift_left, ALU.bitwise_xor).then_inc(sm("coded_0"), 1)

            def other_edges(s, par, ch):
                dve.wait_ge(sm("coded_0"), s * 4 + (ch + 1))
                ts(gh_chunk(par, 1, ch), at_chunk(s, ch), every(TAKE_0[1][0]), None, ALU.bitwise_and).then_inc(sm("masks_ready"), 1)

            def take_masks(s, par, chunks, take, coded, used):
                dve.wait_ge(sm(coded[0]), coded[1])
                if used:
                    dve.wait_ge(sm(used[0]), used[1])
                for ch in chunks:
                    for g in range(2):
                        ins = ts(gh_chunk(par, g, ch), at_chunk(s, ch), every(take[g][0]), None, ALU.bitwise_and)
                    ins.then_inc(sm("masks_ready"), 1)

            def last_chunks(s, par, k):
                dve.wait_ge(sm(f"f1_in{par}"), (k + S // 2 + 1) * 16)
                done = M2 - P2 if first(s) else s * P3 + M2
                for ch in range(CODED, CH):
                    g0, at = gh_chunk(par, 0, ch), at_chunk(s, ch)
                    step = 3 * (ch - CODED)
                    for jb in range(8 * ch, 8 * ch + 8):
                        ins = ts(GH[:, par, 0, jb * SW:(jb + 1) * SW], F1R[:, par, :], F2N[:, 1, jb:jb + 1],
                                 float(TAKE_A[0]), ALU.is_gt, ALU.mult)
                    ins.then_inc(sm("v_mask"), 1)
                    dve.wait_ge(sm("v_mask"), done + (step + 1))
                    tt(g0, g0, at, ALU.bitwise_and).then_inc(sm("v_mask"), 1)
                    dve.wait_ge(sm("v_mask"), done + (step + 2))
                    stt(at, g0, 1, at, ALU.logical_shift_left, ALU.bitwise_xor).then_inc(sm("v_mask"), 1)
                    dve.wait_ge(sm("v_mask"), done + (step + 3))
                    for g in range(2):
                        ins = ts(gh_chunk(par, g, ch), at, every(TAKE_3[g][0]), None, ALU.bitwise_and)
                    ins.then_inc(sm("masks_ready"), 1)

            def masks(layer, s, par, k, chunks):
                early = isinstance(s, int) and s < 2
                if layer == 0:
                    make_masks(s, par, k, chunks)
                elif layer == 1:
                    take_masks(s, par, chunks, TAKE_0, ("coded_0", s * 4 + 4), ("prod_a", 2 * (S + s - 1)) if early else ("prod_b", 2 * (s - 1)))
                else:
                    take_masks(s, par, range(CODED), TAKE_3, ("v_mask", M0 + P2 if first(s) else M2 + P3), None if early else ("prod_3", 2 * (s - 1)))

            def softmax_sums(w, s, layer):
                w.do(dve.tensor_copy(CUR[:], TBL[:, bass.ds(s, 1), :, :].rearrange("p o i w -> p (o i) w")))
                w.do(tt(SM[:, 0:24].rearrange("p (q k) -> p q k", k=6), EVq[:, :, 256:262],
                        CO[:].unsqueeze(1).broadcast_to([128, 4, 6]), ALU.mult))
                w.do(red(SM[:, 24:32], SM[:, 0:24].rearrange("p (q k) -> p q k", k=3), AX.X, ALU.add))
                w.do(tt(SM[:, 32:40].rearrange("p (i w) -> p i w", i=2), SM[:, 24:32].rearrange("p (i w) -> p i w", i=2),
                        CUR[:, :, 0:4], ALU.mult))
                four = SM[:, 32:40].rearrange("p (i g w) -> p i g w", i=2, g=2)
                dq = SM[:, 40:44].rearrange("p (i w) -> p i w", i=2)
                w.do(tt(dq, four[:, :, 0, :], four[:, :, 1, :], ALU.add))
                w.did(dve.tensor_copy(DEN[:, layer, bass.ds(s * 2, 2)], dq[:, :, 0]))
                w.do(ts(SM[:, 44:46], dq[:, :, 0], DENOM_FLOOR, None, ALU.max))
                w.do(dve.reciprocal(SM[:, 44:46], SM[:, 44:46]))
                return dq, SM[:, 44:46]

            def combine(w, s, ev, name):
                stt(T4[:], ev[:, :, 128:256], 1.0 / LO, ev[:, :, 0:128], ALU.mult, ALU.add).then_inc(sm(name), 1)
                w.sync()
                dve.wait_ge(sm(name), s + 1)

            wa = Steps(dve, sm("v_a"))

            def filter_1(s):
                wa.begin(s)
                dve.wait_ge(sm("ev_a"), s * 2 + 2)
                dq, rd = softmax_sums(wa, s, 0)
                wa.do(tt(SM[:, 46:48], dq[:, :, 1], rd, ALU.mult))
                wa.do(stt(RTC[:, :, 2], SM[:, 46:48], 0.5, rd, ALU.mult, ALU.mult))
                wa.did(stt(RTC[:, :, 0:2], CUR[:, :, 0:4:2], 1.0 / HS, BCAST(rd, 2), ALU.mult, ALU.mult))
                wa.do(ts(RTC[:, :, 3], RTC[:, :, 2], -1.0, col(OMC2), ALU.mult, ALU.add))
                wa.did(dve.tensor_copy(RT[:, bass.ds(s, 1), :, :].rearrange("p o i w -> p (o i) w"), RTC[:]))
                combine(wa, s, EVq, "ev_free_a")
                dve.wait_ge(sm("xin_a"), s * 16 + 16)
                for it in range(2):
                    wa.did(ts(WA[:, it, :], T4[:, 2 * it + 1, :], RTC[:, it, 1:2], None, ALU.mult))
                wa.sync()
                for it in range(2):
                    wa.did(stt(WA[:, it, :], T4[:, 2 * it, :], RTC[:, it, 0:1], WA[:, it, :], ALU.mult, ALU.add))
                wa.sync()
                for it in range(2):
                    wa.did(stt(WA[:, it, :], XIN[:, 0, it, :], RTC[:, it, 3:4], WA[:, it, :], ALU.mult, ALU.add))
                wa.sync()
                wa.do(ts(WB[:], WA[:], TH, -TH, ALU.min, ALU.max))
                if not first(s):
                    dve.wait_ge(sm("feat_stored"), s * 16)
                tt(ST32[:], WA[:], WB[:], ALU.subtract).then_inc(sm("feat_ready"), 1)

            def filter_2(s):
                dve.wait_ge(sm("hi_a"), s + 1)
                stt(ST16q[:, :, 128:256], ST16q[:, :, 0:128], -LO, T4[:], ALU.mult, ALU.add).then_inc(sm("rb_ready"), 1)
                wa.end()

            masks(0, 0, 0, 0, range(CH))

            def l0a(s, par, k):
                if isinstance(s, int) and s == 1:
                    for step, j in ((scaled, 2), (remainder, 2), (scaled, 4), (remainder, 4)):
                        step(j)
                        step(j + 1)
                if first(s):
                    masks(0, 1, 1, 0, range(CH))
                    return
                filter_1(s - 1)
                nxt = (1, 0, 0, 0) if last(s) else (0, s + 1, 1 - par, k if par == 0 else k + 1)
                masks(*nxt, range(0, 1))
                filter_2(s - 1)
                masks(*nxt, range(1, CH))

            ring(dve, l0a)
            filter_1(S - 1)
            filter_2(S - 1)

            t0 = RTt[:, :, 2]
            v.did(ts(t0, t0, c(1), col(C1C0), ALU.mult, ALU.add))
            dve.wait_ge(sm("rb_ready"), S)
            v.sync()
            v.do(ts(F1T, t0, col(NC3), c(1), ALU.mult, ALU.add))
            for i in range(2):
                v.did(stt(RTt[:, :, i], RTt[:, :, i], HS / FS, F1T, ALU.mult, ALU.mult))
            v.sync()
            wb = Steps(dve, sm("v_b"))

            def copy_strip(phase, s, par):
                if not (isinstance(s, int) and s < 2):
                    dve.wait_ge(sm("prod_" + phase), 2 * (s - 1))
                if phase == "1":
                    at = AT[:, bass.ds(s * SB, SB)].bitcast(I32)
                    ts(GHI[:, par, 0, :], at, every(TAKE_A[0]), None, ALU.bitwise_and).then_inc(sm("copy_1"), 1)
                    dve.wait_ge(sm("copy_1"), s + 1)
                    ts(at, at, every(TAKE_A[0]), None, ALU.bitwise_and).then_inc(sm("cleaned"), 1)
                else:
                    at = AT[:, bass.ds(s * SB, SB)].bitcast(mybir.dt.uint16)
                    dve.tensor_copy(GH16[:, par, 0, :], at).then_inc(sm("copy_2"), 1)

            dve.wait_ge(sm("feat_stored"), 16 * S)

            def normalise(w, src, phase):
                for it in range(2):
                    w.did(dve.bn_stats(SM[:, 48 + 6 * it:54 + 6 * it], src[:, it, :]))
                w.sync()
                dve.memset(MV[:, :, 5:6], 0.0)
                for it in range(2):
                    w.did(dve.bn_aggr(MV[:, it, 0:2], SM[:, 48 + 6 * it:54 + 6 * it]))
                w.sync()
                ts(MV[:, :, 2], MV[:, :, 1], EPS, None, ALU.add).then_inc(sm("var_" + phase), 1)

            def normalise_2(s, phase):
                dve.wait_ge(sm("rstd_" + phase), s + 1)
                stt(MV[:, :, 4], MV[:, :, 0], -1.0, MV[:, :, 3], ALU.mult, ALU.mult).then_inc(sm("norm_" + phase), 1)

            def feed_1(s):
                wb.begin(s)
                wb.do(dve.tensor_copy(RTC[:], RT[:, bass.ds(s, 1), :, :].rearrange("p o i w -> p (o i) w")))
                dve.wait_ge(sm("ev_b"), s * 2 + 2)
                if not first(s):
                    dve.wait_ge(sm("r1_ready"), s)
                combine(wb, s, EVq, "ev_free_b")
                dve.wait_ge(sm("xin_b"), s * 48 + 48)
                wb.do(stt(WA[:], XIN[:, 2, :, :], col(K2), XIN[:, 0, :, :], ALU.mult, ALU.add))
                for it in range(2):
                    ins = stt(WA[:, it, :], XIN[:, 1, it, :], RTC[:, it, 2:3], WA[:, it, :], ALU.mult, ALU.add)
                ins.then_inc(sm("xin_free_b"), 1)
                dve.wait_ge(sm("xin_free_b"), s + 1)
                for it in range(2):
                    wb.did(stt(WA[:, it, :], T4[:, 2 * it, :], RTC[:, it, 0:1], WA[:, it, :], ALU.mult, ALU.add))
                wb.sync()
                if not first(s):
                    dve.wait_ge(sm("x1_stored"), s * 16)
                for it in range(2):
                    ins = stt(ST32[:, it, :], T4[:, 2 * it + 1, :], RTC[:, it, 1:2], WA[:, it, :], ALU.mult, ALU.add)
                ins.then_inc(sm("x1_ready"), 1)
                dve.wait_ge(sm("x1_ready"), s + 1)
                normalise(wb, ST32, "b")

            def feed_2(s):
                dve.wait_ge(sm("hi_b"), s + 1)
                stt(ST16[:, :, 128:256], ST16[:, :, 0:128], -LO, T4[:, 0:2, :], ALU.mult, ALU.add)\
                    .then_inc(sm("r1_ready"), 1)
                wb.end()

            def l0b(s, par, k):
                nxt = None if last(s) else (1, s + 1, 1 - par, k if par == 0 else k + 1)
                if first(s):
                    masks(*nxt, range(CH))
                    return
                feed_1(s - 1)
                if nxt:
                    masks(*nxt, range(0, 1))
                normalise_2(s - 1, "b")
                if nxt:
                    masks(*nxt, range(1, CH))
                feed_2(s - 1)

            ring(dve, l0b)
            feed_1(S - 1)
            dve.wait_ge(sm("prod_b"), 2 * S)
            copy_strip("1", 0, 0)
            normalise_2(S - 1, "b")
            feed_2(S - 1)

            w1s = Steps(dve, sm("v_1"))
            dve.wait_ge(sm("x1_stored"), 16 * S)
            dve.wait_ge(sm("rows3_in"), 48)
            two = lambda r: r.unsqueeze(1).broadcast_to([128, 2, D])

            def prune(s):
                w1s.begin(s)
                dve.wait_ge(sm("ev_1"), s * 2 + 2)
                if not first(s):
                    dve.wait_ge(sm("r2_ready"), s)
                combine(w1s, s, EV5, "ev_free_1")
                w1s.do(stt(WA[:], T4[:, 0:4:2, :], col(CG), two(BG), ALU.mult, ALU.add))
                dve.wait_ge(sm("xin_1"), s * 16 + 16)
                if not first(s):
                    dve.wait_ge(sm("xb_stored"), s * 16)
                stt(ST32[:], WA[:], 0.0, XIN[:, 0, :, :], ALU.max, ALU.add).then_inc(sm("xb_ready"), 1)
                dve.wait_ge(sm("xb_ready"), s + 1)
                if not first(s):
                    dve.wait_ge(sm("ay_stored"), s * 16)
                ts(WB[:], T4[:, 1:4:2, :], col(CSY), None, ALU.mult).then_inc(sm("ay_ready"), 1)
                normalise(w1s, ST32, "1")
                normalise_2(s, "1")
                dve.wait_ge(sm("hi_1"), s + 1)
                stt(ST16[:, :, 128:256], ST16[:, :, 0:128], -LO, T4[:, 2:4, :], ALU.mult, ALU.add)\
                    .then_inc(sm("r2_ready"), 1)
                w1s.end()

            def l1(s, par, k):
                if not last(s):
                    copy_strip("1", s + 1, 1 - par)
                if not first(s):
                    prune(s - 1)
                if isinstance(s, int) and s == 1:
                    for b in range(2):
                        dve.wait_ge(sm("w8_ps"), b + 1)
                        dve.tensor_copy(W8T[:, 4 * b:4 * b + 4, :], ps[6 + b][:].rearrange("p (b d) -> p b d", d=D))\
                            .then_inc(sm("w8t_ready"), 1)

            ring(dve, l1)
            prune(S - 1)

            dve.wait_ge(sm("prod_1"), 2 * S)
            dve.wait_ge(sm("cleaned"), S)
            v.do(dve.memset(ONES, 1.0))
            copy_strip("2", 0, 0)
            w2s = Steps(dve, sm("v_2"))
            dve.wait_ge(sm("xb_stored"), 16 * S)

            def attention_row(s, par):
                dve.wait_ge(sm("f1_row_ps"), s + 1)
                dve.wait_ge(sm("v_mask"), s * P2 + (M0 - P2))
                dve.wait_ge(sm("r3_f1_stored"), s * 16 + 32)
                dve.tensor_copy(F1R[:, par, :], ps[7][:, SW:2 * SW]).then_inc(sm("f1_row"), 1)
                dve.wait_ge(sm("f1_row"), s + 1)

            def code_3(s, par, chunks, others=0):
                for ch in chunks:
                    done = s * P2 + (M0 + 3 * ch + others)
                    dve.wait_ge(sm("v_mask"), s * P2 + (M0 + 3 * ch + others - 3))
                    pos, at = POS[:, ch % 2, :], at_chunk(s, ch)
                    for n in range(8):
                        jb = 8 * ch + n
                        ins = ts(pos[:, n * SW:(n + 1) * SW], F1R[:, par, :], F2N[:, 1, jb:jb + 1],
                                 float(TAKE_A[0]), ALU.is_gt, ALU.mult)
                    ins.then_inc(sm("v_mask"), 1)
                    dve.wait_ge(sm("v_mask"), done + 1)
                    tt(pos.bitcast(I32), pos.bitcast(I32), at, ALU.bitwise_and).then_inc(sm("v_mask"), 1)
                    dve.wait_ge(sm("v_mask"), done + 2)
                    stt(at, pos.bitcast(I32), 1, at, ALU.logical_shift_left, ALU.bitwise_xor).then_inc(sm("v_mask"), 1)

            def merge(s, between=lambda n: None):
                w2s.begin(s)
                dve.wait_ge(sm("ev_2"), s * 2 + 2)
                combine(w2s, s, EV5, "ev_free_2")
                between(0)
                dve.wait_ge(sm("net_ps0"), s + 1)
                dve.tensor_copy(NETS[:, 0, :], ps[4][:]).then_inc(sm("net_sb0"), 1)
                between(1)
                dve.wait_ge(sm("xin_2"), s * 16 + 16)
                if not first(s):
                    dve.wait_ge(sm("f1_row_ps"), s)
                tt(WA[:], XIN[:, 0, :, :], two(BM), ALU.add).then_inc(sm("xin_free_2"), 1)
                dve.wait_ge(sm("xin_free_2"), s + 1)
                if not first(s):
                    dve.wait_ge(sm("xc_stored"), s * 16)
                between(2)
                dve.wait_ge(sm("net_ps4"), s + 1)
                tt(ST32[:], WA[:], ps[7][:, 0:SW].rearrange("p (i d) -> p i d", d=D), ALU.add).then_inc(sm("xc_ready"), 1)
                dve.wait_ge(sm("xc_ready"), s + 1)
                normalise(w2s, ST32, "2")
                normalise_2(s, "2")
                dve.wait_ge(sm("hb_2"), s + 1)
                w2s.do(tt(WA[:], WB[:], two(A1R), ALU.mult))
                w2s.do(red(SM[:, 60:62], WA[:], AX.X, ALU.add))
                w2s.did(ts(F1[:, bass.ds(s * 2, 2)], SM[:, 60:62], 1.0, None, ALU.mult))
                for it in range(2):
                    ins = ts(WA[:, it, :], IDF[:], SM[:, 60 + it:61 + it], None, ALU.mult)
                ins.then_inc(sm("diag_made"), 1)
                w2s.end()

            def coding(s, par, n):
                if n == 0:
                    attention_row(s, par)
                else:
                    code_3(s, par, (n - 1,))

            def l2(s, par, k):
                if not last(s):
                    copy_strip("2", s + 1, 1 - par)
                if isinstance(s, int) and s < 2:
                    if s == 1:
                        merge(0)
                    return
                merge(s - 1, lambda n: coding(s - 2, par, n))

            ring(dve, l2)
            merge(S - 1, lambda n: coding(S - 2, 0, n))

            w2s.sync()
            xs = lambda k: XT[:, k, :]
            v.do(ts(xs(0), F1[:], col(MX3), None, ALU.add))
            v.do(stt(xs(1), xs(0), LEAK, xs(0), ALU.mult, ALU.max))
            v.did(tt(xs(2), xs(0), xs(1), ALU.subtract))
            v.did(stt(xs(3), xs(0), LEAK, xs(1), ALU.mult, ALU.subtract))
            v.sync()
            dve.engine_nop().then_inc(sm("u3_wanted"), 1)
            dve.wait_ge(sm("prod_2"), 2 * S)
            masks(2, 0, 0, 0, range(CH))
            dve.wait_ge(sm("u3_made"), 1)
            factors(xs(4), xs(5))
            v.sync()
            last_chunks(0, 0, 0)
            attention_row(S - 1, 1)
            code_3(S - 1, 1, range(CODED), P3)
            w3 = Steps(dve, sm("v_3"))
            dve.wait_ge(sm("xc_stored"), 16 * S)

            def attend(s):
                w3.begin(s)
                dve.wait_ge(sm("ev_3"), s * 2 + 2)
                dq, rd = softmax_sums(w3, s, 1)
                w3.do(tt(SM[:, 48:50], EVq[:, 0:4:2, 262], EVq[:, 1:4:2, 262], ALU.add))
                w3.did(dve.tensor_copy(DEG[:, bass.ds(s * 2, 2)], SM[:, 48:50]))
                w3.do(stt(SM[:, 50:52], SM[:, 48:50], col(CSY), rd, ALU.mult, ALU.mult))
                w3.do(tt(RTC[:, :, 0:2], CUR[:, :, 0:4:2], BCAST(SM[:, 50:52], 2), ALU.mult))
                combine(w3, s, EVq, "ev_free_3")
                dve.wait_ge(sm("xin_3"), s * 32 + 32)
                tt(WA[:], XIN[:, 0, :, :], XIN[:, 1, :, :], ALU.add).then_inc(sm("xin_free_3"), 1)
                dve.wait_ge(sm("xin_free_3"), s + 1)
                for it in range(2):
                    w3.did(stt(WA[:, it, :], T4[:, 2 * it, :], RTC[:, it, 0:1], WA[:, it, :], ALU.mult, ALU.add))
                w3.sync()
                if not first(s):
                    dve.wait_ge(sm("out_stored"), s * 16)
                for it in range(2):
                    ins = stt(ST32[:, it, :], T4[:, 2 * it + 1, :], RTC[:, it, 1:2], WA[:, it, :], ALU.mult, ALU.add)
                ins.then_inc(sm("out_ready"), 1)
                w3.end()

            def l3(s, par, k):
                nxt = None if last(s) else (2, s + 1, 1 - par, k if par == 0 else k + 1)
                if not first(s):
                    attend(s - 1)
                if nxt:
                    masks(*nxt, range(CH))
                    last_chunks(*nxt[1:])

            ring(dve, l3)
            attend(S - 1)

            f = Steps(dve, sm("v_g"))
            w3.sync()
            for layer in range(2):
                f.do(ts(SM[:, 0:T], DEN[:, layer, :], DENOM_MIN, None, ALU.is_ge))
                f.do(red(FLG[:, 1 + layer:2 + layer], SM[:, 0:T], AX.X, ALU.min))
            f.do(ts(SM[:, 0:T], DEG[:], float(TOPK), None, ALU.is_le))
            f.do(red(SM[:, T:T + 1], SM[:, 0:T], AX.X, ALU.min))
            f.do(tt(SM[:, T:T + 1], SM[:, T:T + 1], FLG[:, 1:2], ALU.min))
            f.do(tt(SM[:, T:T + 1], SM[:, T:T + 1], FLG[:, 2:3], ALU.min))
            ts(SM[:, 2:3], SM[:, T:T + 1], -1.0, 1.0, ALU.mult, ALU.add).then_inc(sm("bad_rows"), 1)
            dve.wait_ge(sm("bad_any"), 1)
            dve.tensor_copy(FLG[:, 0:1].bitcast(I32), col(BAD)).then_inc(sm("flag_ready"), 1)

            def general():
                q = f
                steps = (21, 21, 1, 31, 5, 17)
                loop = lambda n: Steps(dve, sm("v_tiles"), steps[n], T * sum(steps[:n]))
                gt = lambda k: GT[:, k, :]
                same = lambda dst, src: ts(dst, src, 1.0, None, ALU.mult)

                def layer_norm(n):
                    q.do(red(gt(GMEAN), NX, AX.X, ALU.add))
                    q.do(ts(gt(GMEAN), gt(GMEAN), 1.0 / D, None, ALU.mult))
                    q.do(tt(NS, NX, BCAST(gt(GMEAN)), ALU.subtract))
                    q.do(tt(NW_, NS, NS, ALU.mult))
                    q.do(red(gt(GVAR), NW_, AX.X, ALU.add))
                    ts(gt(GVAR), gt(GVAR), 1.0 / D, EPS, ALU.mult, ALU.add).then_inc(sm("var_b"), 1)
                    dve.wait_ge(sm("rstd_b"), n + 1 + S)
                    q.do(stt(NH, NS, 0.0, BCAST(gt(GRSTD)), ALU.max, ALU.mult))

                def scores(n, src1, k1, src2, k2):
                    row = lambda k: GROWS[:, k, :].unsqueeze(1).broadcast_to([128, T, D])
                    q.do(tt(NS, src1, row(k1), ALU.mult))
                    q.do(red(gt(GF1), NS, AX.X, ALU.add))
                    q.do(tt(NS, src2, row(k2), ALU.mult))
                    red(gt(GF2), NS, AX.X, ALU.add).then_inc(sm("f1_done"), 1)
                    dve.wait_ge(sm("f1_ps"), n + 1 + 1)
                    dve.tensor_copy(FT, ps[7][0:T, 0:D]).then_inc(sm("f1t_made"), 1)
                    dve.wait_ge(sm("f1_in0"), 16 * (n + 1) + 16 * S)

                def softmax_tile(w, t, a, e):
                    w.do(same(SM[:, 0:1], GT[:, GF1, bass.ds(t, 1)]))
                    dve.wait_ge(sm("g_rows"), (t + a * T + 1) * 16)
                    w.do(ts(QW, QF, SM[:, 0:1], None, ALU.add))
                    w.do(stt(QW, QW, LEAK, QW, ALU.mult, ALU.max))
                    w.do(ts(QM, QA, 0.0, None, ALU.is_gt))
                    w.do(tt(QW, QW, QM, ALU.mult))
                    w.do(ts(QM, QM, 1.0, MASK_FILL, ALU.subtract, ALU.mult))
                    w.do(tt(QW, QW, QM, ALU.add))
                    w.do(red(SM[:, 1:2], QW, AX.X, ALU.max))
                    ts(QW, QW, SM[:, 1:2], -200.0, ALU.subtract, ALU.max).then_inc(sm("exps_wanted"), 1)
                    dve.wait_ge(sm("exps_made"), t + (e * T + 1) + 1)
                    w.do(red(SM[:, 2:3], QS, AX.X, ALU.add))
                    w.do(dve.reciprocal(SM[:, 3:4], SM[:, 2:3]))
                    w.do(ts(QW, QS, SM[:, 3:4], None, ALU.mult))

                def aggregate(w, t, a):
                    w.sync()
                    dve.memset(FLG[:, 2:3], 0.0).then_inc(sm("g_weights"), 1)
                    for b in range(8):
                        dve.wait_ge(sm("g_turned"), (t + a * T) * 8 + (b + 1))
                        dve.wait_ge(sm("g_added"), (t + a * T) * 8 + (1 + max(b - 1, 0)))
                        dve.tensor_copy(TURN[:, b % 2, :], ps[b % 2][:]).then_inc(sm("g_copied"), 1)
                    dve.wait_ge(sm("g_added"), (t + a * T) * 8 + 9)

                for free in ("g_weights", "g_copied", "g_added"):
                    dve.engine_nop().then_inc(sm(free), 1)
                dve.wait_ge(sm("x_in"), 64 + 16)
                dve.wait_ge(sm("vec_in"), 96 + 48)
                layer_norm(0)
                scores(0, NH, 0, NH, 1)
                w0 = loop(0)
                with dve.Fori(0, T) as t:
                    w0.begin(t)
                    softmax_tile(w0, t, 0, 0)
                    w0.do(tt(QS, QW, QW, ALU.mult))
                    w0.do(red(SM[:, 4:5], QS, AX.X, ALU.add))
                    w0.do(ts(SM[:, 5:6], SM[:, 4:5], 0.5, None, ALU.mult))
                    w0.do(same(GT[:, GRS, bass.ds(t, 1)], SM[:, 5:6]))
                    w0.do(ts(SM[:, 6:7], SM[:, 5:6], -1.0, col(OMC2), ALU.mult, ALU.add))
                    w0.do(same(WA[:, 0, :], one(NH, t)))
                    aggregate(w0, t, 0)
                    w0.do(stt(WA[:, 1, :], WA[:, 0, :], SM[:, 6:7], ps[2][:, 0:D], ALU.mult, ALU.add))
                    w0.do(ts(WB[:, 0, :], WA[:, 1, :], TH, -TH, ALU.min, ALU.max))
                    w0.do(tt(WA[:, 0, :], WA[:, 1, :], WB[:, 0, :], ALU.subtract))
                    w0.do(same(one(NB, t), WA[:, 0, :]))
                    w0.end()
                w1_ = loop(1)
                with dve.Fori(0, T) as t:
                    w1_.begin(t)
                    softmax_tile(w1_, t, 1, 1)
                    w1_.do(same(SM[:, 4:5], GT[:, GRS, bass.ds(t, 1)]))
                    w1_.do(ts(SM[:, 5:6], SM[:, 4:5], c(1), col(C1C0), ALU.mult, ALU.add))
                    w1_.do(same(WA[:, 0, :], one(NB, t)))
                    w1_.do(same(WB[:, 0, :], one(N0, t)))
                    w1_.do(same(WB[:, 1, :], one(NX, t)))
                    w1_.do(stt(WB[:, 0, :], WB[:, 0, :], col(K2), WB[:, 1, :], ALU.mult, ALU.add))
                    aggregate(w1_, t, 1)
                    w1_.do(stt(WA[:, 0, :], ps[2][:, 0:D], col(NC3), WA[:, 0, :], ALU.mult, ALU.add))
                    w1_.do(stt(WB[:, 0, :], WA[:, 0, :], SM[:, 5:6], WB[:, 0, :], ALU.mult, ALU.add))
                    w1_.do(stt(WB[:, 0, :], ps[2][:, 0:D], c(1), WB[:, 0, :], ALU.mult, ALU.add))
                    w1_.do(same(one(NX, t), WB[:, 0, :]))
                    w1_.end()
                layer_norm(1)
                w2_ = loop(2)
                with dve.Fori(0, T) as t:
                    w2_.begin(t)
                    same(WB[:, 0, :], one(NH, t)).then_inc(sm("hb_b"), 1)
                    dve.wait_ge(sm("ht_ps"), t + 1 + S)
                    dve.tensor_copy(WA[:, 0, :], ps[4][:, 0:D]).then_inc(sm("ht_sb"), 1)
                    dve.wait_ge(sm("g_ps"), t + 1 + S)
                    w2_.do(same(one(NB, t), ps[6][:, 0:D]))
                    w2_.end()
                w3_ = loop(3)
                with dve.Fori(0, T) as t:
                    w3_.begin(t)
                    w3_.do(same(WB[:, 0, :], one(NX, t)))
                    dve.wait_ge(sm("g_rows"), (t + 2 * T + 1) * 16)
                    w3_.do(ts(QM, QA, 0.0, None, ALU.is_gt))
                    src = QM
                    for k in range(12):
                        dst, sh = (QS, QC)[k % 2], 2 ** k
                        w3_.did(dve.tensor_copy(dst[:, 0:sh], src[:, 0:sh]))
                        w3_.do(tt(dst[:, sh:N], src[:, sh:N], src[:, 0:N - sh], ALU.add))
                        src = dst
                    w3_.do(stt(QW, src, float(TOPK), QM, ALU.is_le, ALU.mult))
                    w3_.do(ts(QW, QW, col(TG), None, ALU.mult))
                    aggregate(w3_, t, 2)
                    w3_.do(tt(WA[:, 0, :], ps[2][:, 0:D], GROWS[:, 4, :], ALU.add))
                    w3_.do(stt(WB[:, 0, :], WA[:, 0, :], 0.0, WB[:, 0, :], ALU.max, ALU.add))
                    w3_.do(same(one(NX, t), WB[:, 0, :]))
                    w3_.end()
                layer_norm(2)
                q.do(ts(COL[:, GA1:GA1 + 2], COL[:, KE1:KE1 + 2], 2.0, None, ALU.add))
                w4_ = loop(4)
                with dve.Fori(0, T) as t:
                    w4_.begin(t)
                    w4_.do(same(WA[:, 0, :], one(NX, t)))
                    dve.wait_ge(sm("g_rows"), (t + 3 * T + 1) * 16)
                    w4_.do(dve.tensor_copy(QW, QA))
                    aggregate(w4_, t, 3)
                    for j in range(2):
                        ins = ts(WB[:, j, :], ps[2 + j][:, 0:D], col(GA1 + j), None, ALU.mult)
                    ins.then_inc(sm("g_ax"), 1)
                    dve.wait_ge(sm("net_ps0"), t + 1 + S)
                    dve.tensor_copy(GNET[0], ps[4][:, 0:SW].rearrange("p (i d) -> p i d", d=D)).then_inc(sm("net_sb0"), 1)
                    dve.wait_ge(sm("net_ps4"), t + 1 + S)
                    w4_.do(tt(WA[:, 1, :], ps[7][:, 0:D], GROWS[:, 5, :], ALU.add))
                    w4_.do(tt(WA[:, 0, :], WA[:, 0, :], WA[:, 1, :], ALU.add))
                    w4_.do(same(one(NX, t), WA[:, 0, :]))
                    w4_.end()
                layer_norm(3)
                scores(1, NH, 2, NY, 3)
                w5_ = loop(5)
                with dve.Fori(0, T) as t:
                    w5_.begin(t)
                    softmax_tile(w5_, t, 4, 2)
                    w5_.do(red(SM[:, 4:5], QA, AX.X, ALU.add))
                    w5_.do(ts(QW, QW, SM[:, 4:5], 0.5, ALU.mult, ALU.mult))
                    w5_.do(stt(QW, QA, 0.5, QW, ALU.mult, ALU.add))
                    w5_.do(same(WA[:, 0, :], one(NX, t)))
                    aggregate(w5_, t, 4)
                    w5_.do(tt(WA[:, 0, :], WA[:, 0, :], ps[2][:, 0:D], ALU.add))
                    w5_.do(same(one(NX, t), WA[:, 0, :]))
                    w5_.end()
                dve.engine_nop().then_inc(sm("g_x"), 1)

            dve.wait_ge(sm("flag_ready"), 1)
            flag = dve.value_load(FLAG)
            with dve.If(flag > 0):
                general()

        @block.scalar
        def _(act):
            A = act.activation
            ap = Steps(act, sm("a_pro"))
            act.wait_ge(sm("w_in"), 16 * NW)
            act.wait_ge(sm("consts_made"), 1)
            ap.did(A(COL[:, E5:E5 + 5], COL[:, C0:C0 + 5], ACT.Exp, scale=-1.0))
            ap.do(A(col(TG), col(ONE), ACT.Tanh))
            act.wait_ge(sm("exps_wanted"), 1)
            A(LT[:, 14:20, :], LT[:, 8:14, :], ACT.Exp).then_inc(sm("exps_made"), 1)

            def high(j):
                act.wait_ge(sm("scaled_made"), j + 1)
                if j == 3:
                    act.wait_ge(sm("h_x16_stored"), 16)
                A(HI[j], WORK[j % 2], ACT.Copy).then_inc(sm("hi_made"), 1)

            def low(j):
                act.wait_ge(sm("rest_made"), j + 1)
                A(LOW[j], WORK[j % 2], ACT.Copy, scale=LO).then_inc(sm("job_done"), 1)

            for step in (high, low):
                step(0)
                step(1)

            def keep_transposed(s, r):
                if isinstance(s, int) and s == 2 and r == 0:
                    act.wait_ge(sm("h_x16_stored"), 48)
                if not isinstance(s, int) and r == 0:
                    for name, n in (("r3_f1_stored", 32), ("r2x_stored", 16), ("r1y_stored", 16)):
                        act.wait_ge(sm(name), n)
                act.wait_ge(sm("rows_used"), s * 16 + (2 * r + 2))
                cp, it = r // 2, r % 2
                dst = AT[:, bass.ds(s * SB, SB)].rearrange("p (j i) -> p j i", i=SW)[:, 8 * cp:8 * cp + 8, it * D:(it + 1) * D]
                A(dst, ps[r % 2][:].bitcast(BF16).rearrange("p (j i) -> p j i", i=D), ACT.Copy, scale=float(FP8_ONE))\
                    .then_inc(sm("at_ready"), 1)

            def evacuate(phase, s, it, banks, width):
                scales = {"a": (1.0, TAKE_0[1][1]), "b": [k for _, k in TAKE_0], "1": TAKE_A[1:], "2": TAKE_A[1:],
                          "3": [k for _, k in TAKE_3]}[phase]
                act.wait_ge(sm("prod_" + phase), s * 2 + (it + 1))
                if it == 0 and not first(s):
                    act.wait_ge(sm("ev_free_" + phase), s)
                elif it == 0 and phase != "a":
                    act.wait_ge(sm("ev_free_" + {"b": "a", "1": "b", "2": "1", "3": "2"}[phase]), S)
                for n, b in enumerate(banks):
                    ins = A(EV[:, (it * len(banks) + n) * width:(it * len(banks) + n + 1) * width], ps[b][:, 0:width], ACT.Copy, scale=scales[n])
                ins.then_inc(sm("ev_" + phase), 1)

            for r in range(8):
                keep_transposed(0, r)
            st = lambda dst, src, name: act.dma_start(dst, src).then_inc(sm(name), 16)

            def splits():
                act.wait_ge(sm("x16_made"), 1)
                for g in range(2):
                    st(r3_d[:, :, g * RH + 256:(g + 1) * RH], X16[:, :, g, :], "h_x16_stored")
                for step, j in ((high, 2), (low, 2), (high, 4), (low, 4)):
                    step(j)
                    step(j + 1)
                    if (step, j) == (low, 2):
                        act.wait_ge(sm("job_done"), 4)
                        for g in range(2):
                            st(r3_d[:, :, g * RH:g * RH + 256], P16[6 + g], "r3_f1_stored")
                act.wait_ge(sm("job_done"), 6)
                st(r2_d[:, :, 256:512], P16[2], "r2x_stored")
                st(r1_d[:, :, 256:512], P16[3], "r1y_stored")

            def split_feat(s):
                act.wait_ge(sm("feat_ready"), s + 1)
                if not first(s):
                    act.wait_ge(sm("rb_stored"), s * 16)
                for it in range(2):
                    for g in range(2):
                        A(ST16[:, it, g * RH:g * RH + D], ST32[:, it, :], ACT.Copy, scale=CUR[:, it, 4 + g:5 + g])
                        ins = A(T4[:, 2 * it + g, :], ST32[:, it, :], ACT.Copy, scale=CUR[:, it, 6 + g:7 + g])
                ins.then_inc(sm("hi_a"), 1)

            def l0a(s, par, k):
                if isinstance(s, int) and s == 1:
                    splits()
                if not first(s):
                    evacuate("a", s - 1, 1, (4, 5), RH)
                if not last(s):
                    for r in range(4):
                        keep_transposed(s + 1, r)
                evacuate("a", s, 0, (2, 3), RH)
                if not last(s):
                    for r in range(4, 5):
                        keep_transposed(s + 1, r)
                if not first(s):
                    split_feat(s - 1)
                if not last(s):
                    for r in range(5, 8):
                        keep_transposed(s + 1, r)

            ring(act, l0a)
            evacuate("a", S - 1, 1, (4, 5), RH)
            split_feat(S - 1)

            ab = Steps(act, sm("a_b"))

            def project(s):
                ab.begin(s)
                act.wait_ge(sm("norm_b"), s + 1)
                for it in range(2):
                    ins = A(WB[:, it, :], ST32[:, it, :], ACT.Relu, bias=MV[:, it, 4:5], scale=MV[:, it, 3:4])
                ins.then_inc(sm("hb_b"), 1)
                act.wait_ge(sm("ht_ps"), s + 1)
                A(HT, ps[0][:, 0:SW], ACT.Copy).then_inc(sm("ht_sb"), 1)
                act.wait_ge(sm("pj_ps"), s + 1)
                A(H2T, ps[1][:, 0:SW], ACT.Tanh, bias=col(BP)).then_inc(sm("h2_sb"), 1)
                act.wait_ge(sm("g_ps"), s + 1)
                ab.do(A(WB[:], ps[6][:, 0:SW].rearrange("p (i d) -> p i d", d=D), ACT.Copy, scale=col(SG)))
                if not first(s):
                    act.wait_ge(sm("r1_stored"), s * 16)
                A(ST16[:, :, 0:D], WB[:], ACT.Copy)
                A(T4[:, 0:2, :], WB[:], ACT.Copy, scale=LO).then_inc(sm("hi_b"), 1)
                ab.end()

            act.wait_ge(sm("rb_stored"), 16 * S)

            def l0b(s, par, k):
                if not first(s):
                    evacuate("b", s - 1, 1, (4, 5), RH)
                    project(s - 1)
                evacuate("b", s, 0, (2, 3), RH)

            ring(act, l0b)
            evacuate("b", S - 1, 1, (4, 5), RH)
            project(S - 1)
            act.wait_ge(sm("r1_stored"), 16 * S)

            a1s = Steps(act, sm("a_1"))

            def split_1(s):
                a1s.begin(s)
                act.wait_ge(sm("norm_1"), s + 1)
                for it in range(2):
                    a1s.did(A(T4[:, it, :], ST32[:, it, :], ACT.Relu, bias=MV[:, it, 4:5], scale=MV[:, it, 3:4]))
                a1s.sync()
                if not first(s):
                    act.wait_ge(sm("r2_stored"), s * 16)
                A(ST16[:, :, 0:D], T4[:, 0:2, :], ACT.Copy, scale=HS)
                A(T4[:, 2:4, :], T4[:, 0:2, :], ACT.Copy, scale=HS * LO).then_inc(sm("hi_1"), 1)
                a1s.end()

            def l1(s, par, k):
                if not first(s):
                    evacuate("1", s - 1, 1, (2 * par + 1,), 512)
                    split_1(s - 1)
                evacuate("1", s, 0, (2 * (1 - par),), 512)

            ring(act, l1)
            evacuate("1", S - 1, 1, (1,), 512)
            split_1(S - 1)

            act.wait_ge(sm("ay_stored"), 16 * S)

            def nets(s):
                for l in range(3):
                    act.wait_ge(sm(f"net_ps{l + 1}"), s + 1)
                    for j in range(2):
                        ins = A(NETS[:, l + 1, j * SW:(j + 1) * SW], ps[5 + l % 2][:, j * SW:(j + 1) * SW], ACT.Relu,
                          bias=col(B6 + 3 * j + l), scale=(col(AX1 + j) if l == 0 else 1.0))
                    ins.then_inc(sm(f"net_sb{l + 1}"), 1)
                act.wait_ge(sm("norm_2"), s + 1)
                for it in range(2):
                    ins = A(WB[:, it, :], ST32[:, it, :], ACT.Relu, bias=MV[:, it, 4:5], scale=MV[:, it, 3:4])
                ins.then_inc(sm("hb_2"), 1)

            def l2(s, par, k):
                if not first(s):
                    evacuate("2", s - 1, 1, (2 * par + 1,), 512)
                    nets(s - 1)
                evacuate("2", s, 0, (2 * (1 - par),), 512)

            ring(act, l2)
            evacuate("2", S - 1, 1, (1,), 512)
            nets(S - 1)

            act.wait_ge(sm("u3_wanted"), 1)
            A(XT[:, 4:6, :], XT[:, 2:4, :], ACT.Exp).then_inc(sm("u3_made"), 1)

            def l3(s, par, k):
                if not first(s):
                    evacuate("3", s - 1, 1, (4, 5), RH)
                evacuate("3", s, 0, (2, 3), RH)

            ring(act, l3)
            evacuate("3", S - 1, 1, (4, 5), RH)

            def general():
                def exps(e):
                    with act.Fori(0, T) as t:
                        act.wait_ge(sm("exps_wanted"), t + (e * T + 1) + 1)
                        A(QS, QW, ACT.Exp).then_inc(sm("exps_made"), 1)

                exps(0)
                exps(1)
                with act.Fori(0, T) as t:
                    act.wait_ge(sm("pj_ps"), t + 1 + S)
                    A(T4[:, 1, :], ps[5][:, 0:D], ACT.Tanh, bias=col(BP)).then_inc(sm("h2_sb"), 1)
                with act.Fori(0, T) as t:
                    for l in range(3):
                        act.wait_ge(sm(f"net_ps{l + 1}"), t + 1 + S)
                        for j in range(2):
                            ins = A(GNET[l + 1][:, j, :], ps[5 + l % 2][:, j * D:(j + 1) * D], ACT.Relu, bias=col(B6 + 3 * j + l))
                        ins.then_inc(sm(f"net_sb{l + 1}"), 1)
                exps(2)

            act.wait_ge(sm("flag_ready"), 1)
            flag = act.value_load(FLAG)
            with act.If(flag > 0):
                general()

        @block.tensor
        def _(pe):
            def transpose_pair(s, r):
                cp, it = r // 2, r % 2
                if not (isinstance(s, int) and s == 0 and r < 2):
                    pe.wait_ge(sm("at_ready"), s * 8 + (r - 1))
                for cc in range(2):
                    q = cp * 4 + it * 2 + cc
                    pe.wait_ge(sm(f"rows_in{q % 4}"), s * 64 + 16 * (q // 4 + 1))
                    rows = STG[:, q % 4, :].bitcast(BF16).rearrange("p (c two) -> p c two", two=2)
                    for b in range(4):
                        o = (cc * 4 + b) * D
                        ins = pe.transpose(ps[r % 2][:].bitcast(BF16)[:, o:o + D], rows[:, b * D:(b + 1) * D, 1], IDB[:])
                    ins.then_inc(sm("rows_used"), 1)

            def gate(s, bank, fresh):
                if not isinstance(s, int):
                    pe.matmul(ps[bank][:, 511:512], IDB[:], IDB[:, 0:1], start=fresh, stop=True, skip_group_check=True)

            def units(phase, s):
                return [(u % 2, u // 2) if last(s) or (first(s) and phase != "a") else (u // 8, u % 8) for u in range(16)]

            def two_halves(phase, q0, s, par, r_ready, hooks):
                for u, (it, c8) in enumerate(units(phase, s)):
                    if u in hooks:
                        hooks[u]()
                    if c8 == 0 and not first(s):
                        pe.wait_ge(sm("ev_" + phase), s * 2 + (it - 1))
                    if it == 0 and c8 % 2 == 0:
                        pe.wait_ge(sm("masks_ready"), (s + q0) * 4 + (c8 // 2 + 1))
                        if first(s):
                            r_ready(c8 // 2)
                    if c8 == 0 or (it == 0 and c8 % 2 == 0):
                        gate(s, 2 + 2 * it, c8 == 0)
                    for jb in range(4 * c8, 4 * c8 + 4):
                        for g in range(2):
                            b = 2 + 2 * it + g
                            o = jb * SW + it * D
                            ins = pe.matmul(ps[b][:, 0:RH], GHf[:, par, g, o:o + D], R3[:, jb, g * RH:(g + 1) * RH],
                                            start=jb == 0, stop=jb == T - 1, skip_group_check=True)
                    if c8 == 7:
                        ins.then_inc(sm("prod_" + phase), 1)
                    elif last(s) and it == 1 and c8 % 2 == 1:
                        ins.then_inc(sm("R_free"), 1)

            pe.wait_ge(sm("consts_made"), 1)
            for r in range(2):
                transpose_pair(0, r)
            pe.wait_ge(sm("f1_done"), 1)
            pe.transpose(ps[7][0:T, 0:D], F1[:], IDF[:]).then_inc(sm("f1_ps"), 1)
            for r in range(2, 8):
                transpose_pair(0, r)

            def l0a(s, par, k):
                hooks = {} if last(s) else {2 * r: (lambda r=r: transpose_pair(s + 1, r)) for r in range(8)}
                two_halves("a", 0, s, par, lambda c: pe.wait_ge(sm("job_done"), 2), hooks)

            ring(pe, l0a)

            def norm_transposed(s):
                pe.wait_ge(sm("hb_b"), s + 1)
                for it in range(2):
                    ins = pe.transpose(ps[0][:, it * D:(it + 1) * D], WB[:, it, :], IDF[:])
                ins.then_inc(sm("ht_ps"), 1)

            def proj(s):
                pe.wait_ge(sm("ht_sb"), s + 1)
                pe.matmul(ps[1][:, 0:SW], WP[:], HT, start=True, stop=True).then_inc(sm("pj_ps"), 1)

            def gcn(s):
                pe.wait_ge(sm("h2_sb"), s + 1)
                for it in range(2):
                    ins = pe.matmul(ps[6][:, it * D:(it + 1) * D], H2T[:, it * D:(it + 1) * D], WG[:], start=True, stop=True)
                ins.then_inc(sm("g_ps"), 1)

            def l0b(s, par, k):
                hooks = {} if first(s) else {8: lambda: norm_transposed(s - 1), 10: lambda: proj(s - 1), 13: lambda: gcn(s - 1)}
                if first(s):
                    pe.wait_ge(sm("ev_a"), 2 * S)
                two_halves("b", S, s, par, lambda c: pe.wait_ge(sm(f"R_in{c}"), 16), hooks)

            ring(pe, l0b)
            def one_half(phase, s, par, hooks):
                pe.wait_ge(sm("copy_" + phase), s + 1)
                for u, (it, c8) in enumerate(units(phase, s)):
                    if u in hooks:
                        hooks[u]()
                    if c8 == 0 and not (isinstance(s, int) and s < 2):
                        pe.wait_ge(sm("ev_" + phase), s * 2 + (it - 3))
                    if first(s) and it == 0 and c8 % 2 == 0:
                        pe.wait_ge(sm(f"R_in{c8 // 2}"), {"1": 32, "2": 48}[phase])
                    if c8 == 0:
                        gate(s, 2 * (1 - par) + it, True)
                    for jb in range(4 * c8, 4 * c8 + 4):
                        o = jb * SW + it * D
                        ins = pe.matmul(ps[2 * (1 - par) + it][:], GHf[:, par, 0, o:o + D], R5[:, jb, :],
                                        start=jb == 0, stop=jb == T - 1)
                    if c8 == 7:
                        ins.then_inc(sm("prod_" + phase), 1)
                    elif last(s) and it == 1 and c8 % 2 == 1:
                        ins.then_inc(sm("R_free"), 1)

            def weights_transposed():
                pe.wait_ge(sm("w8_in"), 16 * 8)
                for b in range(2):
                    for j in range(4):
                        ins = pe.transpose(ps[6 + b][:, j * D:(j + 1) * D], W8[:, 4 * b + j, :], IDF[:])
                    ins.then_inc(sm("w8_ps"), 1)

            def l1(s, par, k):
                hooks = {}
                if first(s):
                    pe.wait_ge(sm("ev_b"), 2 * S)
                    hooks = {1: lambda: norm_transposed(S - 1), 2: lambda: proj(S - 1), 4: lambda: gcn(S - 1)}
                elif isinstance(s, int) and s == 1:
                    pe.wait_ge(sm("hi_b"), S)
                    hooks = {8: weights_transposed}
                one_half("1", s, par, hooks)

            ring(pe, l1)

            pe.wait_ge(sm("w8t_ready"), 2)

            def net_in(s):
                pe.wait_ge(sm("ev_free_2"), s + 1)
                for j in range(2):
                    for it in range(2):
                        o = (2 * j + it) * D
                        ins = pe.transpose(ps[4][:, o:o + D], T4[:, 2 * it + j, :], IDF[:])
                ins.then_inc(sm("net_ps0"), 1)

            def net_layer(s, l):
                pe.wait_ge(sm(f"net_sb{l}"), s + 1)
                for j in range(2):
                    ins = pe.matmul(ps[5 + l % 2][:, j * SW:(j + 1) * SW], W8T[:, 3 * j + l, :],
                                    NETS[:, l, j * SW:(j + 1) * SW], start=True, stop=True)
                ins.then_inc(sm(f"net_ps{l + 1}"), 1)

            def net_out(s):
                pe.wait_ge(sm("net_sb3"), s + 1)
                if not first(s):
                    pe.wait_ge(sm("xc_ready"), s)
                    pe.wait_ge(sm("f1_row"), s)
                for it in range(2):
                    for j in range(2):
                        o = j * SW + it * D
                        ins = pe.matmul(ps[7][:, it * D:(it + 1) * D], NETS[:, 3, o:o + D], W8T[:, 6 + j, :],
                                        start=j == 0, stop=j == 1)
                ins.then_inc(sm("net_ps4"), 1)

            def f1_row(s):
                pe.wait_ge(sm("diag_made"), s + 1)
                if not first(s):
                    pe.wait_ge(sm("f1_row"), s)
                pe.matmul(ps[7][:, SW:2 * SW], ONES, WA[:].rearrange("p i d -> p (i d)"), start=True, stop=True)\
                    .then_inc(sm("f1_row_ps"), 1)

            def l2(s, par, k):
                hooks = {} if first(s) else {6: lambda: net_in(s - 1), 8: lambda: net_layer(s - 1, 0),
                                             10: lambda: net_layer(s - 1, 1), 12: lambda: net_layer(s - 1, 2),
                                             14: lambda: net_out(s - 1)}
                if not (isinstance(s, int) and s < 2):
                    hooks[5] = lambda: f1_row(s - 2)
                else:
                    pe.wait_ge(sm("ev_1"), 2 * (S - 1 + s))
                one_half("2", s, par, hooks)

            ring(pe, l2)
            f1_row(S - 2)
            net_in(S - 1)
            for l in range(3):
                net_layer(S - 1, l)
            net_out(S - 1)
            f1_row(S - 1)

            ring(pe, lambda s, par, k: two_halves("3", 2 * S, s, par, lambda c: pe.wait_ge(sm(f"R_in{c}"), 64), {}))

            def general():
                def f2_row(n):
                    pe.wait_ge(sm("f1_done"), n + 1 + 1)
                    pe.transpose(ps[7][0:T, 0:D], GT[:, GF2, :], IDF[:]).then_inc(sm("f1_ps"), 1)

                def product(t, a, right):
                    pe.wait_ge(sm("g_weights"), t + (a * T + 2))
                    for b in range(8):
                        pe.wait_ge(sm("g_copied"), (t + a * T) * 8 + (1 + max(b - 1, 0)))
                        for j in range(4):
                            o = (4 * b + j) * D
                            ins = pe.transpose(ps[b % 2][:, j * D:(j + 1) * D], QW[:, o:o + D], IDF[:])
                        ins.then_inc(sm("g_turned"), 1)
                        pe.wait_ge(sm("g_copied"), (t + a * T) * 8 + (b + 2))
                        for j in range(4):
                            for n, r in enumerate(right):
                                ins = pe.matmul(ps[2 + n][:, 0:D], TURN[:, b % 2, j * D:(j + 1) * D], r[:, 4 * b + j, :],
                                                start=b == 0 and j == 0, stop=b == 7 and j == 3)
                        ins.then_inc(sm("g_added"), 1)

                f2_row(0)
                with pe.Fori(0, T) as t:
                    product(t, 0, [NH])
                with pe.Fori(0, T) as t:
                    product(t, 1, [NB])
                with pe.Fori(0, T) as t:
                    pe.wait_ge(sm("hb_b"), t + 1 + S)
                    pe.transpose(ps[4][:, 0:D], WB[:, 0, :], IDF[:]).then_inc(sm("ht_ps"), 1)
                    pe.wait_ge(sm("ht_sb"), t + 1 + S)
                    pe.matmul(ps[5][:, 0:D], WP[:], WA[:, 0, :], start=True, stop=True).then_inc(sm("pj_ps"), 1)
                    pe.wait_ge(sm("h2_sb"), t + 1 + S)
                    pe.matmul(ps[6][:, 0:D], T4[:, 1, :], WG[:], start=True, stop=True).then_inc(sm("g_ps"), 1)
                with pe.Fori(0, T) as t:
                    product(t, 2, [NB])
                with pe.Fori(0, T) as t:
                    product(t, 3, [NH, NX2])
                    pe.wait_ge(sm("g_ax"), t + 1)
                    for j in range(2):
                        ins = pe.transpose(ps[4][:, j * D:(j + 1) * D], WB[:, j, :], IDF[:])
                    ins.then_inc(sm("net_ps0"), 1)
                    for l in range(3):
                        pe.wait_ge(sm(f"net_sb{l}"), t + 1 + S)
                        for j in range(2):
                            ins = pe.matmul(ps[5 + l % 2][:, j * D:(j + 1) * D], W8T[:, 3 * j + l, :], GNET[l][:, j, :],
                                            start=True, stop=True)
                        ins.then_inc(sm(f"net_ps{l + 1}"), 1)
                    pe.wait_ge(sm("net_sb3"), t + 1 + S)
                    for j in range(2):
                        ins = pe.matmul(ps[7][:, 0:D], GNET[3][:, j, :], W8T[:, 6 + j, :], start=j == 0, stop=j == 1)
                    ins.then_inc(sm("net_ps4"), 1)
                f2_row(1)
                with pe.Fori(0, T) as t:
                    product(t, 4, [NY])

            pe.wait_ge(sm("flag_ready"), 1)
            flag = pe.value_load(FLAG)
            with pe.If(flag > 0):
                general()


_INS = ["x", "adj", "L0_gnn_h0", "L0_gnn_a", "L0_gnn_temp", "L1_gnn_W_proj", "L1_gnn_b_proj", "L1_gnn_W_gcn",
        "L1_gnn_b_gcn", "L2_gnn_x2", "L2_gnn_eps1", "L2_gnn_eps2", "L2_gnn_W1", "L2_gnn_b1", "L2_gnn_W2", "L2_gnn_b2",
        "L2_gnn_Wm", "L2_gnn_bm", "L3_gnn_input2", "L3_gnn_a1", "L3_gnn_a2"]


def kernel(**inputs):
    import numpy as _np
    import concourse.bacc as _bacc
    from concourse import mybir as _mybir
    from concourse.bass_utils import run_bass_kernel_spmd as _run

    nc = _bacc.Bacc("TRN2", target_bir_lowering=False, num_devices=1, dynamic_dma_scratch_size=1024)
    arrays, args = {}, []
    for name in _INS:
        a = _np.ascontiguousarray(inputs[name])
        arrays[f"in_{name}_dram"] = a
        args.append(nc.dram_tensor(f"in_{name}_dram", a.shape, _mybir.dt.from_np(a.dtype), kind="ExternalInput").ap())
    out = nc.dram_tensor("out_0_dram", (N, D), _mybir.dt.float32, kind="ExternalOutput").ap()
    build(nc, *args, out)
    r = _run(nc, [arrays], core_ids=[0])
    return r.results[0]["out_0_dram"]
```
